# Optimizing a Trainium2 kernel written in Bass

```python
import numpy as np
import jax
import jax.numpy as jnp

def _softmax(x, axis=-1):
    return jax.nn.softmax(x, axis=axis)

def _gelu(x):
    return jax.nn.gelu(x, approximate=True)

def _silu(x):
    return jax.nn.silu(x)

def _sigmoid(x):
    return jax.nn.sigmoid(x)

def _layernorm(x, axis=-1, eps=1e-05):
    m = jnp.mean(x, axis=axis, keepdims=True)
    v = jnp.var(x, axis=axis, keepdims=True)
    return (x - m) / jnp.sqrt(v + eps)

def _scatter_add(tgt, idx, src, axis=0):
    return tgt.at[idx].add(src)

def _segment_sum(src, seg, n):
    return jax.ops.segment_sum(src, seg, n)
kernel_name = 'mk_recurrent_d1_jaxref_r4_f09298'

def setup_inputs(seed: int=0):
    np.random.seed(seed)
    _w = jnp.asarray

    def _L0_attn_setup():
        import jax, jax.numpy as jnp
        import numpy as np
        import math
        D_MODEL = 256
        NUM_HEADS = 16
        HEAD_DIM = D_MODEL // NUM_HEADS
        LN_EPS = 1e-05

        def _layer_norm(x, g, b):
            mu = jnp.mean(x, axis=-1, keepdims=True)
            var = jnp.mean(jnp.square(x - mu), axis=-1, keepdims=True)
            return (x - mu) * jax.lax.rsqrt(var + LN_EPS) * g + b

        def _rope_tables(seq_len, dim, dtype):
            inv_freq = 1.0 / 10000.0 ** (jnp.arange(0, dim, 2, dtype=jnp.float32) / dim)
            t = jnp.arange(seq_len, dtype=jnp.float32)
            freqs = t[:, None] * inv_freq[None, :]
            emb = jnp.concatenate([freqs, freqs], axis=-1)
            return (jnp.cos(emb).astype(dtype), jnp.sin(emb).astype(dtype))

        def _rotate_half(x):
            x1, x2 = jnp.split(x, 2, axis=-1)
            return jnp.concatenate([-x2, x1], axis=-1)
        key = jax.random.key(seed)
        ks = jax.random.split(key, 8)
        B, S, D = (2, 512, D_MODEL)
        s_in = 1.0 / math.sqrt(D)
        return {'x': jax.random.normal(ks[0], (B, S, D), jnp.float32), 'ln1_g': jnp.ones((D,), jnp.float32), 'ln1_b': jnp.zeros((D,), jnp.float32), 'Wqkv': jax.random.normal(ks[1], (D, 3 * D), jnp.float32) * s_in, 'bqkv': jnp.zeros((3 * D,), jnp.float32), 'Wo': jax.random.normal(ks[2], (D, D), jnp.float32) * s_in, 'bo': jnp.zeros((D,), jnp.float32), 'ln2_g': jnp.ones((D,), jnp.float32), 'ln2_b': jnp.zeros((D,), jnp.float32), 'W1': jax.random.normal(ks[3], (D, 4 * D), jnp.float32) * s_in, 'b1': jnp.zeros((4 * D,), jnp.float32), 'W2': jax.random.normal(ks[4], (4 * D, D), jnp.float32) / math.sqrt(4 * D), 'b2': jnp.zeros((D,), jnp.float32)}
    _L0_attn_in = _L0_attn_setup()

    def _L0_ffn_setup():
        import jax, jax.numpy as jnp
        import numpy as np
        B, T, H, F, E, TOPK = (4, 256, 256, 1024, 8, 2)

        def _moe_forward(x, rw, rb, w1, b1, w2, b2, sw1, sb1, sw2, sb2):
            Bb, Tt, Hh = x.shape
            N = Bb * Tt
            Ee = rw.shape[0]
            cap = max(1, int(N / Ee * 1.0))
            xf = x.reshape(N, Hh)
            logits = xf @ rw.T + rb
            g_soft = jax.nn.softmax(logits, axis=-1)
            _, idx = jax.lax.top_k(g_soft, TOPK)
            primary, second = (idx[:, 0], idx[:, 1])
            ohp = jax.nn.one_hot(primary, Ee, dtype=jnp.int32)
            posp = jnp.cumsum(ohp, axis=0) - ohp
            pos_tok = jnp.take_along_axis(posp, primary[:, None], 1)[:, 0]
            keep_primary = pos_tok < cap
            used = jnp.minimum(ohp.sum(axis=0), cap)
            overflow = ~keep_primary
            ohs = jax.nn.one_hot(second, Ee, dtype=jnp.int32) * overflow[:, None].astype(jnp.int32)
            poss = jnp.cumsum(ohs, axis=0) - ohs
            pos2 = jnp.take_along_axis(poss, second[:, None], 1)[:, 0]
            take2 = overflow & (used[second] + pos2 < cap)
            assign = jnp.where(keep_primary, primary, jnp.where(take2, second, -1))
            overflow = overflow & ~take2
            h = jax.nn.gelu(jnp.einsum('nh,ehf->enf', xf, w1) + b1[:, None, :], approximate=False)
            stack = jnp.einsum('enf,efh->enh', h, w2) + b2[:, None, :]
            one_hot_a = jax.nn.one_hot(assign, Ee, dtype=stack.dtype)
            y = jnp.einsum('enh,ne->nh', stack, one_hot_a)
            y_fb = jax.nn.gelu(xf @ sw1 + sb1, approximate=False) @ sw2 + sb2
            y = jnp.where(overflow[:, None], y_fb, y)
            return y.reshape(Bb, Tt, Hh)
        key = jax.random.key(seed)
        ks = jax.random.split(key, 12)
        s = 0.02
        return {'x': jax.random.normal(ks[0], (B, T, H), dtype=jnp.float32), 'rw': jax.random.normal(ks[1], (E, H), dtype=jnp.float32) * s, 'rb': jnp.zeros((E,), dtype=jnp.float32), 'w1': jax.random.normal(ks[2], (E, H, F), dtype=jnp.float32) * s, 'b1': jnp.zeros((E, F), dtype=jnp.float32), 'w2': jax.random.normal(ks[3], (E, F, H), dtype=jnp.float32) * s, 'b2': jnp.zeros((E, H), dtype=jnp.float32), 'sw1': jax.random.normal(ks[4], (H, F), dtype=jnp.float32) * s, 'sb1': jnp.zeros((F,), dtype=jnp.float32), 'sw2': jax.random.normal(ks[5], (F, H), dtype=jnp.float32) * s, 'sb2': jnp.zeros((H,), dtype=jnp.float32)}
    _L0_ffn_in = _L0_ffn_setup()
    _d = {'L0_attn_x': _L0_attn_in['x'], 'L0_attn_ln1_g': _L0_attn_in['ln1_g'], 'L0_attn_ln1_b': _L0_attn_in['ln1_b'], 'L0_attn_Wqkv': _L0_attn_in['Wqkv'], 'L0_attn_bqkv': _L0_attn_in['bqkv'], 'L0_attn_Wo': _L0_attn_in['Wo'], 'L0_attn_bo': _L0_attn_in['bo'], 'L0_attn_ln2_g': _L0_attn_in['ln2_g'], 'L0_attn_ln2_b': _L0_attn_in['ln2_b'], 'L0_attn_W1': _L0_attn_in['W1'], 'L0_attn_b1': _L0_attn_in['b1'], 'L0_attn_W2': _L0_attn_in['W2'], 'L0_attn_b2': _L0_attn_in['b2'], 'L0_ffn_rw': _L0_ffn_in['rw'], 'L0_ffn_rb': _L0_ffn_in['rb'], 'L0_ffn_w1': _L0_ffn_in['w1'], 'L0_ffn_b1': _L0_ffn_in['b1'], 'L0_ffn_w2': _L0_ffn_in['w2'], 'L0_ffn_b2': _L0_ffn_in['b2'], 'L0_ffn_sw1': _L0_ffn_in['sw1'], 'L0_ffn_sb1': _L0_ffn_in['sb1'], 'L0_ffn_sw2': _L0_ffn_in['sw2'], 'L0_ffn_sb2': _L0_ffn_in['sb2']}
    _x0 = _d['L0_attn_x']
    _d['L0_attn_x'] = jax.random.normal(jax.random.fold_in(jax.random.key(seed), 1), (1, 4096, 256), dtype=_x0.dtype)
    del _x0
    return _d

def reference(L0_attn_x, L0_attn_ln1_g, L0_attn_ln1_b, L0_attn_Wqkv, L0_attn_bqkv, L0_attn_Wo, L0_attn_bo, L0_attn_ln2_g, L0_attn_ln2_b, L0_attn_W1, L0_attn_b1, L0_attn_W2, L0_attn_b2, L0_ffn_rw, L0_ffn_rb, L0_ffn_w1, L0_ffn_b1, L0_ffn_w2, L0_ffn_b2, L0_ffn_sw1, L0_ffn_sb1, L0_ffn_sw2, L0_ffn_sb2):

    def _L0_attn_ref(x, ln1_g, ln1_b, Wqkv, bqkv, Wo, bo, ln2_g, ln2_b, W1, b1, W2, b2):
        import jax, jax.numpy as jnp
        import numpy as np
        import math
        D_MODEL = 256
        NUM_HEADS = 16
        HEAD_DIM = D_MODEL // NUM_HEADS
        LN_EPS = 1e-05

        def _layer_norm(x, g, b):
            mu = jnp.mean(x, axis=-1, keepdims=True)
            var = jnp.mean(jnp.square(x - mu), axis=-1, keepdims=True)
            return (x - mu) * jax.lax.rsqrt(var + LN_EPS) * g + b

        def _rope_tables(seq_len, dim, dtype):
            inv_freq = 1.0 / 10000.0 ** (jnp.arange(0, dim, 2, dtype=jnp.float32) / dim)
            t = jnp.arange(seq_len, dtype=jnp.float32)
            freqs = t[:, None] * inv_freq[None, :]
            emb = jnp.concatenate([freqs, freqs], axis=-1)
            return (jnp.cos(emb).astype(dtype), jnp.sin(emb).astype(dtype))

        def _rotate_half(x):
            x1, x2 = jnp.split(x, 2, axis=-1)
            return jnp.concatenate([-x2, x1], axis=-1)
        B, S, D = x.shape
        H, hd = (NUM_HEADS, HEAD_DIM)
        normed = _layer_norm(x, ln1_g, ln1_b)
        qkv = (normed @ Wqkv + bqkv).reshape(B, S, 3, H, hd)
        qkv = jnp.transpose(qkv, (2, 0, 3, 1, 4))
        q, k, v = (qkv[0], qkv[1], qkv[2])
        cos, sin = _rope_tables(S, hd, q.dtype)
        cos = cos[None, None, :, :]
        sin = sin[None, None, :, :]
        q = q * cos + _rotate_half(q) * sin
        k = k * cos + _rotate_half(k) * sin
        scores = jnp.einsum('bhqd,bhkd->bhqk', q, k) / math.sqrt(hd)
        causal = jnp.triu(jnp.ones((S, S), dtype=bool), k=1)
        scores = jnp.where(causal[None, None], -jnp.inf, scores)
        attn = jax.nn.softmax(scores, axis=-1)
        attn_out = jnp.einsum('bhqk,bhkd->bhqd', attn, v)
        attn_out = jnp.transpose(attn_out, (0, 2, 1, 3)).reshape(B, S, D)
        attn_out = attn_out @ Wo + bo
        x = x + attn_out
        h = _layer_norm(x, ln2_g, ln2_b)
        h = jax.nn.gelu(h @ W1 + b1, approximate=False) @ W2 + b2
        return x + h

    def _L0_ffn_ref(x, rw, rb, w1, b1, w2, b2, sw1, sb1, sw2, sb2):
        import jax, jax.numpy as jnp
        import numpy as np
        B, T, H, F, E, TOPK = (4, 256, 256, 1024, 8, 2)

        def _moe_forward(x, rw, rb, w1, b1, w2, b2, sw1, sb1, sw2, sb2):
            Bb, Tt, Hh = x.shape
            N = Bb * Tt
            Ee = rw.shape[0]
            cap = max(1, int(N / Ee * 1.0))
            xf = x.reshape(N, Hh)
            logits = xf @ rw.T + rb
            g_soft = jax.nn.softmax(logits, axis=-1)
            _, idx = jax.lax.top_k(g_soft, TOPK)
            primary, second = (idx[:, 0], idx[:, 1])
            ohp = jax.nn.one_hot(primary, Ee, dtype=jnp.int32)
            posp = jnp.cumsum(ohp, axis=0) - ohp
            pos_tok = jnp.take_along_axis(posp, primary[:, None], 1)[:, 0]
            keep_primary = pos_tok < cap
            used = jnp.minimum(ohp.sum(axis=0), cap)
            overflow = ~keep_primary
            ohs = jax.nn.one_hot(second, Ee, dtype=jnp.int32) * overflow[:, None].astype(jnp.int32)
            poss = jnp.cumsum(ohs, axis=0) - ohs
            pos2 = jnp.take_along_axis(poss, second[:, None], 1)[:, 0]
            take2 = overflow & (used[second] + pos2 < cap)
            assign = jnp.where(keep_primary, primary, jnp.where(take2, second, -1))
            overflow = overflow & ~take2
            h = jax.nn.gelu(jnp.einsum('nh,ehf->enf', xf, w1) + b1[:, None, :], approximate=False)
            stack = jnp.einsum('enf,efh->enh', h, w2) + b2[:, None, :]
            one_hot_a = jax.nn.one_hot(assign, Ee, dtype=stack.dtype)
            y = jnp.einsum('enh,ne->nh', stack, one_hot_a)
            y_fb = jax.nn.gelu(xf @ sw1 + sb1, approximate=False) @ sw2 + sb2
            y = jnp.where(overflow[:, None], y_fb, y)
            return y.reshape(Bb, Tt, Hh)
        return _moe_forward(x, rw, rb, w1, b1, w2, b2, sw1, sb1, sw2, sb2)
    x = L0_attn_x
    xn = _layernorm(x, axis=-1)
    s = _L0_attn_ref(xn, L0_attn_ln1_g, L0_attn_ln1_b, L0_attn_Wqkv, L0_attn_bqkv, L0_attn_Wo, L0_attn_bo, L0_attn_ln2_g, L0_attn_ln2_b, L0_attn_W1, L0_attn_b1, L0_attn_W2, L0_attn_b2)
    g = _silu(_L0_ffn_ref(xn, L0_ffn_rw, L0_ffn_rb, L0_ffn_w1, L0_ffn_b1, L0_ffn_w2, L0_ffn_b2, L0_ffn_sw1, L0_ffn_sb1, L0_ffn_sw2, L0_ffn_sb2))
    x = x + s * g
    return x

_drawn_inputs = setup_inputs


def setup_inputs(seed=0):
    import zlib

    import numpy as np

    out = dict(_drawn_inputs(seed))
    spreads = {'L0_attn_ln1_g': (1.0, 0.6),
     'L0_attn_ln1_b': (0.0, 0.8),
     'L0_attn_bqkv': (0.0, 0.8),
     'L0_attn_bo': (0.0, 2.0),
     'L0_attn_ln2_g': (1.0, 0.6),
     'L0_attn_ln2_b': (0.0, 2.0),
     'L0_attn_b1': (0.0, 2.0),
     'L0_attn_b2': (0.0, 2.0),
     'L0_ffn_rb': (0.0, 0.1),
     'L0_ffn_b1': (0.0, 0.37),
     'L0_ffn_b2': (0.0, 0.1),
     'L0_ffn_sb1': (0.0, 0.8),
     'L0_ffn_sb2': (0.0, 0.389)}
    factors = {'L0_attn_Wqkv': 5.083, 'L0_attn_Wo': 4.065, 'L0_ffn_sw1': 2.705}
    for name, (base, spread) in spreads.items():
        noise = np.random.default_rng([zlib.crc32(name.encode()), seed]).standard_normal(out[name].shape)
        drawn = base * np.exp(spread * noise) if base else spread * noise
        out[name] = jnp.asarray(drawn.astype(out[name].dtype))
    for name, factor in factors.items():
        out[name] = (out[name] * factor).astype(out[name].dtype)
    return out
```

```python
import numpy as np
import concourse.bass as bass
from concourse import mybir
from contextlib import ExitStack

F32, BF16, I32 = mybir.dt.float32, mybir.dt.bfloat16, mybir.dt.int32
ACT, ALU, AX = mybir.ActivationFunctionType, mybir.AluOpType, mybir.AxisListType

P = 128
N, D = 4096, 256
H, HD = 16, 16
F, E = 1024, 8
NT = N // P
CH = 512
NC = N // CH
TPC = CH // P
EPS = 1e-5
def project_tokens(nc, io, scratch, keep):
    x, wqkv, rwT = io["x"], io["wqkv"], io["rwT"]
    with ExitStack() as ctx:
        sb = lambda name, shape, dt=F32: ctx.enter_context(nc.sbuf_tensor("proj_" + name, shape, dt))
        sem = lambda name: ctx.enter_context(nc.semaphore("proj_" + name))
        X = sb("X", [P, NT, D])
        XN = keep["XN"]
        XNs = sb("XNs", [P, TPC, D])
        XNN = sb("XNN", [P, TPC, D])
        XT = sb("XT", [P, 2, CH])
        NX = sb("NX", [P, 2, CH])
        W = sb("W", [P, 2, 3 * D])
        RW = sb("RW", [P, 2, E])
        BQ = sb("BQ", [P, 3 * D])
        RB = sb("RB", [P, E])
        G1 = sb("G1", [P, 2, 2])
        COS = sb("COS", [P, NT, HD])
        SIN = sb("SIN", [P, NT, HD])
        QB = sb("QB", [P, 2, 2 * D])
        QC = sb("QC", [P, 2, 2 * D])
        QS = sb("QS", [P, 2, 2 * D])
        QR = sb("QR", [P, TPC, 2 * D])
        VA = sb("VA", [P, 2, H, 2 * HD])
        PT = sb("PT", [P, 2, 3, CH], BF16)
        RS = sb("RS", [P, 2, CH])
        ST = sb("ST", [P, NT, 6])
        MV = sb("MV", [P, NT, 2])
        SD = sb("SD", [P, NT])
        R1 = sb("R1", [P, NT])
        MV2 = sb("MV2", [P, NT, 2])
        SD2 = sb("SD2", [P, NT])
        R2 = sb("R2", [P, NT])
        B2 = sb("B2", [P, NT])
        ident = keep["ident"]
        LG = keep["LG"]
        ps = ctx.enter_context(nc.psum_tensor("psA", [P, 8, CH], F32))
        TB, QKB, VB, QTB = 0, 2, 4, 6
        w_in, stats, std, rstd = sem("w_in"), sem("stats"), sem("std"), sem("rstd")
        xn_ready, stats2, std2, rstd2 = sem("xn_ready"), sem("stats2"), sem("std2"), sem("rstd2")
        chunk_in, xposed, t_free, xt_ready = sem("chunk_in"), sem("xposed"), sem("t_free"), sem("xt_ready")
        qk_ps, qk_biased, v_ps, v_biased = sem("qk_ps"), sem("qk_biased"), sem("v_ps"), sem("v_biased")
        cosed, sined, rotated = sem("cosed"), sem("sined"), sem("rotated")
        qt_ps, part1, rest1, part2, part3 = sem("qt_ps"), sem("part1"), sem("rest1"), sem("part2"), sem("part3")
        va_ok, xt_out = sem("va_ok"), sem("xt_out")
        v_out, p_out = [sem("v_out0"), sem("v_out1")], [sem("p_out0"), sem("p_out1")]
        consts, first_part = sem("consts"), sem("first_part")
        x_in = [sem(f"x_in{c}") for c in range(NC)]
        xv = x.rearrange("o (t p) d -> p (o t) d", p=P)
        with nc.Block() as block:
            @block.sync
            def _(sp):
                for c in range(NC):
                    sp.dma_start(X[:, TPC * c:TPC * (c + 1), :], xv[:, TPC * c:TPC * (c + 1), :]).then_inc(x_in[c], 16)
                for dst, src in ((W[:, :, :], wqkv.rearrange("(k p) n -> p k n", p=P)),
                                 (RW[:, :, :], rwT.rearrange("(k p) n -> p k n", p=P)),
                                 (COS[:, :, :], io["cos"].rearrange("(t p) d -> p t d", p=P)),
                                 (SIN[:, :, :], io["sin"].rearrange("(t p) d -> p t d", p=P)),
                                 (BQ[:, :], io["bqkv"].rearrange("(a n) -> a n", a=1).broadcast_to([P, 3 * D])),
                                 (RB[:, :], io["rb"].rearrange("(a n) -> a n", a=1).broadcast_to([P, E])),
                                 (G1[:, 0, :], io["ln1_g"].rearrange("(k p) -> p k", p=P)),
                                 (G1[:, 1, :], io["ln1_b"].rearrange("(k p) -> p k", p=P))):
                    sp.dma_start(dst, src, allow_slow_non_contiguous=True).then_inc(w_in, 16)
                with sp.Fori(0, NC) as c:
                    col = sp.snap(c * CH)
                    sp.wait_ge(xt_ready, 4 * c + 2)
                    sp.dma_start(scratch["xnT"].rearrange("(k p) n -> p k n", p=P)[:, :, bass.ds(col, CH)],
                                 XT[:, :, :]).then_inc(xt_out, 16)
                    for j in range(TPC):
                        sp.wait_ge(v_biased, TPC * c + j + 1)
                        sp.dma_start(scratch["v"].rearrange("(t p) n -> p t n", p=P)[:, bass.ds(TPC * c + j, 1), :],
                                     VA[:, j % 2, :, :].rearrange("p h d -> p (h d)").rearrange("p (a n) -> p a n", a=1)).then_inc(v_out[j % 2], 16)
                    for u in range(4):
                        sp.wait_ge(part3, 4 * (c + 1) + u + 1)
                        if u == 0:
                            sp.sem_inc(first_part, 1)
                        sp.dma_start(scratch["qkp"].rearrange("s (u p) n -> u p s n", u=4)[u, :, :, bass.ds(col, CH)],
                                     PT[:, u % 2, :, :]).then_inc(p_out[u % 2], 16)
                sp.wait_ge(xt_out, 16 * (NC + 1))
                for half in range(2):
                    sp.wait_ge(v_out[half], 16 * (NT // 2 + 1))
                    sp.wait_ge(p_out[half], 16 * (2 * NC + 1))

            @block.gpsimd
            def _(pool):
                nc.gpsimd.memset(ident[:, :], 0.0).then_inc(consts, 1)
                nc.gpsimd.memset(VA[:, :, :, :], 0.0).then_inc(consts, 1)
                pool.wait_ge(consts, 2)
                nc.gpsimd.affine_select(out=ident[:, :], in_=ident[:, :], compare_op=ALU.not_equal, fill=1.0,
                                        base=0, pattern=[[-1, P]], channel_multiplier=1).then_inc(va_ok, 1)
                nc.gpsimd.memset(VA[:, :, :, HD:HD + 1], 1.0).then_inc(va_ok, 1)
                pool.wait_ge(w_in, 16 * 8)
                with pool.Fori(0, NC) as c:
                    for j in range(TPC):
                        pool.wait_ge(qk_biased, TPC * c + j + 1)
                        pool.wait_ge(rotated, TPC * c + j + 1)
                        nc.gpsimd.tensor_tensor(
                            QC[:, j % 2, :].rearrange("p (h d) -> p h d", d=HD),
                            QB[:, j % 2, :].rearrange("p (h d) -> p h d", d=HD),
                            COS[:, bass.ds(TPC * c + j, 1), :].broadcast_to([P, 2 * H, HD]), ALU.mult).then_inc(cosed, 1)

            @block.vector
            def _(dve):
                dve.sem_inc(rotated, 2)
                dve.sem_inc(rest1, 2)
                dve.sem_inc(qt_ps, 4)
                dve.sem_inc(part3, 4)
                dve.sem_inc(v_out[0], 16)
                dve.sem_inc(v_out[1], 16)
                for c in range(NC):
                    dve.wait_ge(x_in[c], 16)
                    for t in range(TPC * c, TPC * (c + 1)):
                        nc.vector.bn_stats(ST[:, t, :], X[:, t, :]).then_inc(stats, 1)
                for t in range(NT):
                    dve.wait_ge(stats, t + 1)
                    nc.vector.bn_aggr(MV[:, t, :], ST[:, t, :]).then_inc(std, 1)
                dve.wait_ge(std, NT)
                nc.vector.tensor_scalar(SD[:, :], MV[:, :, 1], EPS, None, ALU.add).then_inc(std, 1)
                dve.wait_ge(rstd, 1)
                nc.vector.reciprocal(R1[:, :], SD[:, :]).then_inc(rstd, 1)
                dve.wait_ge(rstd, 2)
                for t in range(NT):
                    nc.vector.tensor_scalar(XN[:, t, :], X[:, t, :], MV[:, t, 0:1], R1[:, t:t + 1],
                                            ALU.subtract, ALU.mult).then_inc(xn_ready, 1)
                for t in range(NT):
                    dve.wait_ge(xn_ready, t + 1)
                    nc.vector.bn_stats(ST[:, t, :], XN[:, t, :]).then_inc(stats2, 1)
                for t in range(NT):
                    dve.wait_ge(stats2, t + 1)
                    nc.vector.bn_aggr(MV2[:, t, :], ST[:, t, :]).then_inc(std2, 1)
                dve.wait_ge(std2, NT)
                nc.vector.tensor_scalar(SD2[:, :], MV2[:, :, 1], EPS, None, ALU.add).then_inc(std2, 1)
                dve.wait_ge(rstd2, 1)
                nc.vector.reciprocal(R2[:, :], SD2[:, :]).then_inc(rstd2, 1)
                dve.wait_ge(rstd2, 2)
                nc.vector.scalar_tensor_tensor(B2[:, :], MV2[:, :, 0], -1.0, R2[:, :], ALU.mult, ALU.mult).then_inc(rstd2, 1)
                dve.wait_ge(w_in, 16 * 8)
                dve.wait_ge(va_ok, 2)

                def rotate(c, j):
                    dve.wait_ge(cosed, TPC * c + j + 1)
                    dve.wait_ge(sined, 2 * (TPC * c + j + 1))
                    nc.vector.tensor_tensor(QR[:, j, :], QC[:, j % 2, :], QS[:, j % 2, :], ALU.add).then_inc(rotated, 1)

                with dve.Fori(0, NC) as c:
                    for j in range(TPC):
                        dve.wait_ge(qk_ps, TPC * c + j + 1)
                        dve.wait_ge(rotated, TPC * c + j + 1)
                        nc.vector.tensor_tensor(QB[:, j % 2, :], ps[:, QKB + j % 2, :], BQ[:, 0:2 * D], ALU.add).then_inc(qk_biased, 1)
                        dve.wait_ge(v_ps, TPC * (c + 1) + j + 1)
                        dve.wait_ge(v_out[j % 2], 16 * (2 * c + j // 2 + 1))
                        nc.vector.tensor_tensor(VA[:, j % 2, :, 0:HD],
                                                ps[:, VB + j % 2, 0:D].rearrange("p (h d) -> p h d", d=HD),
                                                BQ[:, 2 * D:3 * D].rearrange("p (h d) -> p h d", d=HD), ALU.add).then_inc(v_biased, 1)
                        nc.vector.tensor_tensor(LG[:, bass.ds(TPC * c + j, 1), :].rearrange("p a e -> p (a e)"),
                                                ps[:, VB + j % 2, D:D + E], RB[:, :], ALU.add).then_inc(keep["routed"], 1)
                        dve.wait_ge(qk_biased, TPC * c + j + 1)
                        qb = QB[:, j % 2, :].rearrange("p (h d) -> p h d", d=HD)
                        qs = QS[:, j % 2, :].rearrange("p (h d) -> p h d", d=HD)
                        for lo, hi in ((0, HD // 2), (HD // 2, 0)):
                            nc.vector.tensor_tensor(qs[:, :, lo:lo + HD // 2], qb[:, :, hi:hi + HD // 2],
                                                    SIN[:, bass.ds(TPC * c + j, 1), lo:lo + HD // 2].broadcast_to([P, 2 * H, HD // 2]),
                                                    ALU.mult).then_inc(sined, 1)
                        if j == 0:
                            dve.wait_ge(qt_ps, 4 * (c + 1))
                        if j > 0:
                            rotate(c, j - 1)
                    rotate(c, TPC - 1)
                    for u in range(5):
                        if u < 4:
                            dve.wait_ge(part1, 4 * c + u + 1)
                            if u < 2:
                                dve.wait_ge(part3, 4 * (c + 1))
                            else:
                                dve.wait_ge(part3, 4 * (c + 1) + u - 1)
                            nc.vector.tensor_tensor(RS[:, u % 2, :], ps[:, QTB + u % 2, :], PT[:, u % 2, 0, :], ALU.subtract).then_inc(rest1, 1)
                        if u > 0:
                            dve.wait_ge(part2, 4 * c + u)
                            nc.vector.tensor_tensor(PT[:, (u - 1) % 2, 2, :], RS[:, (u - 1) % 2, :], PT[:, (u - 1) % 2, 1, :],
                                                    ALU.subtract).then_inc(part3, 1)

            @block.scalar
            def _(act):
                act.sem_inc(t_free, 2)
                act.sem_inc(xposed, 4)
                act.sem_inc(v_ps, TPC)
                act.sem_inc(xt_out, 16)
                act.sem_inc(p_out[0], 16)
                act.sem_inc(p_out[1], 16)
                act.wait_ge(std, NT + 1)
                nc.scalar.activation(SD[:, :], SD[:, :], ACT.Sqrt).then_inc(rstd, 1)
                act.wait_ge(std2, NT + 1)
                nc.scalar.activation(SD2[:, :], SD2[:, :], ACT.Sqrt).then_inc(rstd2, 1)
                act.wait_ge(rstd2, 3)
                act.wait_ge(w_in, 16 * 8)
                with act.Fori(0, NC) as c:
                    act.wait_ge(xposed, 4 * (c + 1))
                    nc.scalar.activation(XNs[:, :, :], XN[:, bass.ds(TPC * c, TPC), :], ACT.Copy).then_inc(chunk_in, 1)
                    for j in range(TPC):
                        nc.scalar.activation(XNN[:, j, :], XN[:, bass.ds(TPC * c + j, 1), :].rearrange("p a n -> p (a n)"),
                                             ACT.Identity, scale=R2[:, bass.ds(TPC * c + j, 1)],
                                             bias=B2[:, bass.ds(TPC * c + j, 1)]).then_inc(chunk_in, 1)
                    for k in range(2):
                        act.wait_ge(xposed, 4 * (c + 1) + k + 1)
                        act.wait_ge(v_ps, TPC * (c + 1))
                        act.wait_ge(xt_out, 16 * (c + 1))
                        nc.scalar.activation(XT[:, k, :], ps[:, TB + k, :], ACT.Copy).then_inc(xt_ready, 1)
                        act.wait_ge(xt_ready, 4 * c + k + 1)
                        act.sem_inc(t_free, 1)
                    for k in range(2):
                        act.wait_ge(xposed, 4 * (c + 1) + k + 3)
                        nc.scalar.activation(NX[:, k, :], ps[:, TB + k, :], ACT.Identity, scale=G1[:, 0, k:k + 1],
                                             bias=G1[:, 1, k:k + 1]).then_inc(xt_ready, 1)
                        act.wait_ge(xt_ready, 4 * c + k + 3)
                        act.sem_inc(t_free, 1)
                    for u in range(5):
                        if u < 4:
                            act.wait_ge(qt_ps, 4 * (c + 1) + u + 1)
                            act.wait_ge(p_out[u % 2], 16 * (2 * c + u // 2 + 1))
                            nc.scalar.activation(PT[:, u % 2, 0, :], ps[:, QTB + u % 2, :], ACT.Copy).then_inc(part1, 1)
                        if u > 0:
                            act.wait_ge(rest1, 4 * c + u + 2)
                            nc.scalar.activation(PT[:, (u - 1) % 2, 1, :], RS[:, (u - 1) % 2, :], ACT.Copy).then_inc(part2, 1)

            @block.tensor
            def _(pe):
                pe.sem_inc(keep["routed"], TPC)
                pe.wait_ge(va_ok, 1)
                pe.wait_ge(w_in, 16 * 8)
                with pe.Fori(0, NC) as c:
                    for v, (src, need) in enumerate(((XNs, 1), (XNN, 5))):
                        pe.wait_ge(chunk_in, 5 * c + need)
                        for k in range(2):
                            pe.wait_ge(t_free, 4 * c + 2 * v + k + 1)
                            for j in range(TPC):
                                mm = nc.tensor.transpose(ps[:, TB + k, j * P:(j + 1) * P], src[:, j, k * P:(k + 1) * P], ident[:, :])
                            mm.then_inc(xposed, 1)
                    pe.wait_ge(xt_ready, 4 * c + 4)
                    for j in range(TPC):
                        tok = slice(j * P, (j + 1) * P)
                        pe.wait_ge(rotated, TPC * c + j + 1)
                        for k in range(2):
                            mm = nc.tensor.matmul(ps[:, QKB + j % 2, :], NX[:, k, tok], W[:, k, 0:2 * D], start=(k == 0), stop=(k == 1))
                        mm.then_inc(qk_ps, 1)
                        if j < 2:
                            pe.wait_ge(keep["routed"], TPC * (c + 1))
                        else:
                            pe.wait_ge(keep["routed"], TPC * (c + 1) + j - 1)
                        for k in range(2):
                            nc.tensor.matmul(ps[:, VB + j % 2, 0:D], NX[:, k, tok], W[:, k, 2 * D:3 * D], start=(k == 0), stop=(k == 1))
                        for k in range(2):
                            mm = nc.tensor.matmul(ps[:, VB + j % 2, D:D + E], XT[:, k, tok], RW[:, k, :], start=(k == 0), stop=(k == 1))
                        mm.then_inc(v_ps, 1)
                    for u in range(4):
                        pe.wait_ge(rest1, 4 * c + u + 1)
                        for j in range(TPC):
                            if u == 0:
                                pe.wait_ge(rotated, TPC * c + j + 3)
                            mm = nc.tensor.transpose(ps[:, QTB + u % 2, j * P:(j + 1) * P], QR[:, j, u * P:(u + 1) * P], ident[:, :])
                        mm.then_inc(qt_ps, 1)
HG = 4
NG = H // HG
PAIRS = ((0, 0), (0, 1), (1, 0), (1, 1), (0, 2), (2, 0))
MROW = HD * len(PAIRS)
KROWS = MROW + 2 * HG
BIG = -1e30


def attend(nc, scratch):
    qk = scratch["qkp"].rearrange("s (w g h d) n -> s w g d h n", w=2, g=NG, h=HG)
    vv = scratch["v"].rearrange("(t p) (g n) -> g p t n", p=P, g=NG)
    units = [[(kb, max(0, kb - TPC * c)) for kb in range(TPC * (c + 1))] for c in range(NC)]
    jobs = [[(j, h, kc) for kc in range(c + 1) for j in range(TPC) for h in range(HG)] for c in range(NC)]
    S_PER = sum(2 * len(u) + 1 for u in units)
    J_PER = sum(len(j) for j in jobs)
    U_PER = sum(len(u) for u in units)
    s_base = [1 + sum(2 * len(u) + 1 for u in units[:c]) for c in range(NC)]
    u_base = [sum(len(u) for u in units[:c]) for c in range(NC)]
    j_base = [sum(len(j) for j in jobs[:c]) for c in range(NC)]
    RING = 3
    MLAG = 2

    with ExitStack() as ctx:
        sb = lambda name, shape, dt=F32: ctx.enter_context(nc.sbuf_tensor("attn_" + name, shape, dt))
        sem = lambda name: ctx.enter_context(nc.semaphore("attn_" + name))
        KS = sb("KS", [P, HG, N], BF16)
        QS = sb("QS", [P, 4, HG, CH], BF16)
        V = sb("V", [P, NT, HG * 2 * HD])
        PB = sb("PB", [P, RING, HG, CH])
        MX = sb("MX", [P, TPC * HG, NC])
        NM = sb("NM", [P, TPC * HG])
        MH = sb("MH", [P, TPC, 2, HG], BF16)
        OU = sb("OU", [P, 2, CH])
        idb = sb("idb", [P, P], BF16)
        mask_qk = sb("mask_qk", [P, P], BF16)
        mask_kq = sb("mask_kq", [P, P], BF16)
        ps = ctx.enter_context(nc.psum_tensor("psB", [P, 8, CH], F32))
        PV, MB = 4, 5
        q_in = [sem(f"q_in{s}") for s in range(4)]
        k_in = [sem(f"k_in{c}") for c in range(NC)]
        v_in = [sem(f"v_in{c}") for c in range(NC)]
        consts, masks, kones = sem("consts"), sem("masks"), sem("kones")
        scored, expd, pv_done, ou_ready = sem("scored"), sem("expd"), sem("pv_done"), sem("ou_ready")
        maxed, reduced, negmax, mparts = sem("maxed"), sem("reduced"), sem("negmax"), sem("mparts")
        ou_out = [sem("ou_out0"), sem("ou_out1")]

        def nxt(g, c):
            return ((g + 1) % NG, g + 1, 0) if c == NC - 1 else (g, g, c + 1)

        with nc.Block() as block:
            @block.sync
            def _(sp):
                def load_q(group, c):
                    for i, (a, _) in enumerate(PAIRS):
                        sp.dma_start(QS[HD * i:HD * (i + 1), c % 4, :, :],
                                     qk[a, 0, bass.ds(group, 1), :, :, c * CH:(c + 1) * CH].rearrange("g d h n -> (g d) h n")).then_inc(q_in[c % 4], 16)

                def load_k(group, c):
                    for i, (_, b) in enumerate(PAIRS):
                        sp.dma_start(KS[HD * i:HD * (i + 1), :, c * CH:(c + 1) * CH],
                                     qk[b, 1, bass.ds(group, 1), :, :, c * CH:(c + 1) * CH].rearrange("g d h n -> (g d) h n")).then_inc(k_in[c], 16)

                def load_v(group, c):
                    sp.dma_start(V[:, TPC * c:TPC * (c + 1), :],
                                 vv[bass.ds(group, 1), :, TPC * c:TPC * (c + 1), :].rearrange("g p t n -> (g p) t n")).then_inc(v_in[c], 16)

                for c in range(NC):
                    if c < 2:
                        load_q(0, c)
                    load_k(0, c)
                    load_v(0, c)
                with sp.Fori(0, NG) as g:
                    after = sp.snap((g + 1) % NG)
                    for c in range(NC):
                        sp.wait_ge(scored, g * S_PER + s_base[c])
                        load_q(g if c < NC - 2 else after, (c + 2) % NC)
                        if c > 0:
                            sp.wait_ge(ou_ready, g * NC + c + 1)
                            sp.dma_start(scratch["ao"][bass.ds(g, 1), :, (c - 1) * CH:c * CH].rearrange("g r n -> (g r) n"), OU[:, (c - 1) % 2, :]).then_inc(ou_out[(c - 1) % 2], 16)
                    for kc in range(NC):
                        sp.wait_ge(scored, g * S_PER + s_base[NC - 1] + 2 * TPC * (kc + 1) + (1 if kc == NC - 1 else 0))
                        load_k(after, kc)
                        sp.wait_ge(pv_done, RING + g * U_PER + u_base[NC - 1] + TPC * (kc + 1))
                        load_v(after, kc)
                    sp.wait_ge(ou_ready, g * NC + NC + 1)
                    sp.dma_start(scratch["ao"][bass.ds(g, 1), :, (NC - 1) * CH:].rearrange("g r n -> (g r) n"), OU[:, (NC - 1) % 2, :]).then_inc(ou_out[(NC - 1) % 2], 16)
                for half in range(2):
                    sp.wait_ge(ou_out[half], 16 * (NG * NC // 2 + 1))
                for s in range(4):
                    sp.wait_ge(q_in[s], 96 * (2 * NG + (1 if s < 2 else 0)))
                for kc in range(NC):
                    sp.wait_ge(k_in[kc], 96 * (NG + 1))
                    sp.wait_ge(v_in[kc], 16 * (NG + 1))

            @block.gpsimd
            def _(pool):
                nc.gpsimd.memset(idb[:, :], 0.0).then_inc(consts, 1)
                nc.gpsimd.memset(mask_qk[:, :], 0.0).then_inc(consts, 1)
                nc.gpsimd.memset(mask_kq[:, :], 0.0).then_inc(consts, 1)
                pool.wait_ge(consts, 3)
                nc.gpsimd.affine_select(out=idb[:, :], in_=idb[:, :], compare_op=ALU.not_equal, fill=1.0, base=0,
                                        pattern=[[-1, P]], channel_multiplier=1).then_inc(masks, 1)
                nc.gpsimd.affine_select(out=mask_qk[:, :], in_=mask_qk[:, :], compare_op=ALU.is_ge, fill=BIG, base=0,
                                        pattern=[[-1, P]], channel_multiplier=1).then_inc(masks, 1)
                nc.gpsimd.affine_select(out=mask_kq[:, :], in_=mask_kq[:, :], compare_op=ALU.is_ge, fill=BIG, base=0,
                                        pattern=[[1, P]], channel_multiplier=-1).then_inc(masks, 1)
                pool.wait_ge(masks, 3)
                for q in range(4):
                    part = KS[MROW:KROWS, :, q * N // 4:(q + 1) * N // 4]
                    nc.gpsimd.memset(part, 0.0).then_inc(consts, 1)
                    for first in range(2):
                        pool.wait_ge(consts, 4 + 3 * q + first)
                        nc.gpsimd.affine_select(out=part, in_=part, compare_op=ALU.not_equal, fill=1.0, base=-HG * first,
                                                pattern=[[-1, HG], [0, N // 4]], channel_multiplier=1).then_inc(consts, 1)
                pool.wait_ge(consts, 3 + 12)
                pool.sem_inc(kones, 1)

            @block.tensor
            def _(pe):
                def max_job(cg, c, m, job):
                    j, h, kc = job
                    w = CH if kc < c else P * (j + 1)
                    if h == 0 and j == 0:
                        pe.wait_ge(k_in[kc], 96 * (cg + 1))
                    n, off = m
                    if n is not None:
                        pe.wait_ge(reduced, n)
                    bank = MB + off % 3
                    mm = nc.tensor.matmul(ps[:, bank, 0:w], QS[0:MROW, c % 4, h, j * P:(j + 1) * P],
                                          KS[0:MROW, h, kc * CH:kc * CH + w], start=True, stop=(kc < c))
                    if kc == c:
                        mm = nc.tensor.matmul(ps[:, bank, w - P:w], idb[:, :], mask_qk[:, :], start=False, stop=True)
                    mm.then_inc(maxed, 1)

                def max_rows(s, need):
                    pe.wait_ge(mparts, need)
                    if s[0] is not None:
                        pe.wait_ge(expd, s[0])
                    for j in range(TPC):
                        mm = nc.tensor.matmul(ps[MROW:KROWS, 2 * (s[1] % 2), j * P:(j + 1) * P],
                                              MH[:, j, :, :].rearrange("p s h -> p (s h)"), idb[:, :], start=True, stop=True)
                    mm.then_inc(scored, 1)

                def scores(g, c, k, pair):
                    kb, r = units[c][k]
                    s = s_base[c] + 2 * k + pair + (1 if k > len(units[c]) - 1 - MLAG else 0)
                    if s > 1:
                        pe.wait_ge(expd, g * S_PER + s - 1)
                    for i in range(2):
                        h = 2 * pair + i
                        bank = 2 * (s % 2) + i
                        mm = nc.tensor.matmul(ps[:, bank, r * P:CH], KS[0:KROWS, h, kb * P:(kb + 1) * P], QS[0:KROWS, c % 4, h, r * P:CH],
                                              start=True, stop=(kb < TPC * c))
                        if kb >= TPC * c:
                            mm = nc.tensor.matmul(ps[:, bank, r * P:(r + 1) * P], idb[:, :], mask_kq[:, :], start=False, stop=True)
                    mm.then_inc(scored, 1)

                def weigh(g, c, k):
                    kb, r = units[c][k]
                    s = s_base[c] + 2 * k + 1 + (1 if k > len(units[c]) - 1 - MLAG else 0)
                    pe.wait_ge(expd, g * S_PER + s + 1)
                    if k % TPC == 0:
                        pe.wait_ge(v_in[k // TPC], 16 * (g + 1))
                    if k == 0:
                        pe.wait_ge(ou_ready, g * NC + c + 1)
                    u = u_base[c] + k
                    for h in range(HG):
                        mm = nc.tensor.matmul(ps[32 * h:32 * (h + 1), PV, r * P:CH], V[:, kb, 32 * h:32 * (h + 1)],
                                              PB[:, u % RING, h, r * P:CH], start=(k == 0), stop=(k == len(units[c]) - 1))
                    mm.then_inc(pv_done, 1)

                pe.sem_inc(ou_ready, 1)
                pe.sem_inc(pv_done, RING)
                pe.wait_ge(masks, 3)
                pe.wait_ge(q_in[0], 96)
                for i, job in enumerate(jobs[0]):
                    max_job(0, 0, (i - 2 if i > 2 else None, i), job)
                max_rows((None, 0), 1)
                pe.wait_ge(kones, 1)
                with pe.Fori(0, NG) as g:
                    for c in range(NC):
                        _, cg, c2 = nxt(g, c)
                        todo = list(jobs[c2])
                        nj = J_PER if c == NC - 1 else 0
                        count, at = len(units[c]), 0
                        if c == 0:
                            pe.wait_ge(expd, g * S_PER + 1)
                        for k in range(count + 1):
                            if k < count:
                                scores(g, c, k, 0)
                                scores(g, c, k, 1)
                            if k == 0:
                                pe.wait_ge(q_in[c2 % 4], 96 * (2 * cg + c2 // 4 + 1))
                            first = 8 if c == NC - 1 else 0
                            last = count - 1 - MLAG
                            share = 0 if k < first else min(len(todo), -(-len(jobs[c2]) * (k + 1 - first) // max(1, last + 1 - first))) if k <= last else len(todo)
                            while at < share:
                                off = j_base[c2] + nj + at
                                max_job(cg, c2, (g * J_PER + off - 2, off), todo[at])
                                at += 1
                            if k == last:
                                max_rows((g * S_PER + s_base[c] + 2 * (k + 1) - 1, s_base[c] + 2 * (k + 1)), g * NC + c + 2)
                            if k > 0:
                                weigh(g, c, k - 1)

            @block.scalar
            def _(act):
                def rows(c, s):
                    act.wait_ge(scored, s[0] + 1)
                    nc.scalar.activation(QS[MROW:KROWS, c % 4, :, :], ps[MROW:KROWS, 2 * (s[1] % 2):2 * (s[1] % 2) + 1, :].broadcast_to([2 * HG, HG, CH]),
                                         ACT.Copy).then_inc(expd, 1)

                act.sem_inc(ou_out[0], 16)
                act.sem_inc(ou_out[1], 16)
                act.wait_ge(q_in[0], 96)
                rows(0, (0, 0))
                with act.Fori(0, NG) as g:
                    for c in range(NC):
                        count = len(units[c])
                        for k in range(count):
                            kb, r = units[c][k]
                            u = u_base[c] + k
                            for pair in range(2):
                                s = s_base[c] + 2 * k + pair + (1 if k > count - 1 - MLAG else 0)
                                act.wait_ge(scored, g * S_PER + s + 1)
                                if pair == 0:
                                    act.wait_ge(pv_done, g * U_PER + u + 1)
                                nc.scalar.activation(PB[:, u % RING, 2 * pair:2 * pair + 2, r * P:CH],
                                                     ps[:, 2 * (s % 2):2 * (s % 2) + 2, r * P:CH], ACT.Exp, scale=HD ** -0.5).then_inc(expd, 1)
                            if k == count - 1 - MLAG:
                                rows((c + 1) % NC, (g * S_PER + s_base[c] + 2 * (k + 1), s_base[c] + 2 * (k + 1)))
                        act.wait_ge(pv_done, RING + g * U_PER + u_base[c] + count)
                        act.wait_ge(ou_out[c % 2], 16 * (g * (NC // 2) + c // 2 + 1))
                        nc.scalar.activation(OU[:, c % 2, :], ps[:, PV, :], ACT.Copy).then_inc(ou_ready, 1)

            @block.vector
            def _(dve):
                def reduce_job(m, job, c):
                    j, h, kc = job
                    w = CH if kc < c else P * (j + 1)
                    dve.wait_ge(maxed, m[0] + 1)
                    nc.vector.tensor_reduce(MX[:, HG * j + h, kc:kc + 1], ps[:, MB + m[1] % 3, 0:w], AX.X, ALU.max).then_inc(reduced, 1)

                def finish(c, jobs_done, need):
                    dve.wait_ge(reduced, jobs_done)
                    if not isinstance(need, int):
                        dve.wait_ge(mparts, need)
                    nc.vector.tensor_reduce(NM[:, :], MX[:, :, 0:c + 1], AX.X, ALU.max, negate=True).then_inc(negmax, 1)
                    dve.wait_ge(negmax, 2 * need + 1)
                    nm = NM[:, :].rearrange("p (j h) -> p j h", h=HG)
                    nc.vector.tensor_copy(MH[:, :, 0, :], nm).then_inc(negmax, 1)
                    dve.wait_ge(negmax, 2 * need + 2)
                    nc.vector.tensor_tensor(MH[:, :, 1, :], nm, MH[:, :, 0, :], ALU.subtract).then_inc(mparts, 1)

                for i, job in enumerate(jobs[0]):
                    reduce_job((i, i), job, 0)
                finish(0, len(jobs[0]), 0)
                with dve.Fori(0, NG) as g:
                    for c in range(NC):
                        c2 = (c + 1) % NC
                        nj = J_PER if c == NC - 1 else 0
                        dve.wait_ge(negmax, 2 * (g * NC + c + 1))
                        for at, job in enumerate(jobs[c2]):
                            off = j_base[c2] + nj + at
                            reduce_job((g * J_PER + off, off), job, c2)
                        dve.wait_ge(scored, g * S_PER + s_base[c])
                        finish(c2, g * J_PER + j_base[c2] + nj + len(jobs[c2]), g * NC + c + 1)
def route(nc, scratch, keep):
    CAP = N // E
    with ExitStack() as ctx:
        sb = lambda name, shape, dt=F32: ctx.enter_context(nc.sbuf_tensor("route_" + name, shape, dt))
        sem = lambda name: ctx.enter_context(nc.semaphore("route_" + name))
        LG, FB, KEPT, SLOT, TAKE, XN = keep["LG"], keep["FB"], keep["KEPT"], keep["SLOT"], keep["TAKE"], keep["XN"]
        W8 = sb("W8", [P, E])
        ONE = sb("ONE", [P, NT])
        TOK = sb("TOK", [P, NT])
        TOKI = sb("TOKI", [P, NT], I32)
        tri = sb("tri", [P, P], BF16)
        ones = sb("ones", [P, P], BF16)
        ZR = sb("ZR", [P, D])
        OH = [sb(f"OH{i}", [P, NT, E]) for i in range(2)]
        OHB = sb("OHB", [P, 2, NT, E], BF16)
        A = sb("A", [P, NT, E])
        B = sb("B", [P, NT, E])
        INC = sb("INC", [P, NT, E])
        POS = sb("POS", [P, NT, E])
        M = sb("M", [P, NT])
        R = [sb(f"R{i}", [P, NT]) for i in range(2)]
        PT1 = sb("PT1", [P, NT])
        PT2 = sb("PT2", [P, NT])
        USED = sb("USED", [P, E])
        OVF = sb("OVF", [P, NT])
        T2 = sb("T2", [P, NT])
        S1 = sb("S1", [P, NT])
        S2 = sb("S2", [P, NT])
        ps = ctx.enter_context(nc.psum_tensor("psR", [P, 4, CH], F32))
        consts, cum, link, ohb, slots = sem("r_consts"), sem("r_cum"), sem("r_link"), sem("r_ohb"), sem("r_slots")
        zeroed, sent = sem("r_zeroed"), sem("r_sent")
        over_t = lambda ap: ap.rearrange("p (a e) -> p a e", a=1).broadcast_to([P, NT, E])
        over_e = lambda ap: ap.rearrange("p (t a) -> p t a", a=1).broadcast_to([P, NT, E])
        with nc.Block() as block:
            @block.sync
            def _(sp):
                sp.wait_ge(consts, 3)
                for t in range(E * CAP // P):
                    sp.dma_start(scratch["xs"][t * P:(t + 1) * P, :], ZR[:, :]).then_inc(zeroed, 16)

            @block.gpsimd
            def _(pool):
                nc.gpsimd.memset(tri[:, :], 1.0).then_inc(consts, 1)
                nc.gpsimd.memset(ones[:, :], 1.0).then_inc(consts, 1)
                nc.gpsimd.memset(ZR[:, :], 0.0).then_inc(consts, 1)
                pool.wait_ge(consts, 3)
                nc.gpsimd.affine_select(out=tri[:, :], in_=tri[:, :], compare_op=ALU.is_gt, fill=0.0, base=0,
                                        pattern=[[1, P]], channel_multiplier=-1).then_inc(consts, 1)
                nc.gpsimd.iota(TOKI[:, :], pattern=[[P, NT]], base=0, channel_multiplier=1).then_inc(consts, 1)
                pool.wait_ge(slots, 1)
                pool.wait_ge(zeroed, 16 * E * CAP // P)
                for t in range(NT):
                    nc.gpsimd.indirect_dma_start(out=scratch["xs"], out_offset=bass.IndirectOffsetOnAxis(ap=SLOT[:, t:t + 1], axis=0),
                                                 in_=XN[:, t, :], in_offset=None).then_inc(sent, 16)
                pool.wait_ge(sent, 16 * NT)

            @block.tensor
            def _(pe):
                for i in range(2):
                    pe.wait_ge(ohb, i + 1)
                    pe.wait_ge(consts, 5)
                    rhs = OHB[:, i, :, :].rearrange("p t e -> p (t e)")
                    nc.tensor.matmul(ps[:, 2 * i, 0:NT * E], tri[:, :], rhs, start=True, stop=True).then_inc(cum, 1)
                    nc.tensor.matmul(ps[:, 2 * i + 1, 0:NT * E], ones[:, :], rhs, start=True, stop=True).then_inc(cum, 1)

            @block.vector
            def _(dve):
                v = nc.vector
                made = [0]

                def link_up(ins):
                    made[0] += 1
                    ins.then_inc(link, 1)
                    dve.wait_ge(link, made[0])

                def first_of(logits, i):
                    link_up(v.tensor_reduce(M[:, :], logits[:, :, :], AX.X, ALU.max))
                    link_up(v.tensor_tensor(A[:, :, :], logits[:, :, :], over_e(M[:, :]), ALU.is_equal))
                    link_up(v.tensor_tensor(A[:, :, :], A[:, :, :], over_t(W8[:, :]), ALU.mult))
                    link_up(v.tensor_reduce(R[i][:, :], A[:, :, :], AX.X, ALU.max))
                    link_up(v.tensor_tensor(OH[i][:, :, :], A[:, :, :], over_e(R[i][:, :]), ALU.is_equal))

                def places(i, out):
                    psv = lambda b: ps[:, b, 0:NT * E].rearrange("p (t e) -> p t e", e=E)
                    dve.wait_ge(cum, 2 * (i + 1))
                    link_up(v.tensor_copy(B[:, :, :], psv(2 * i + 1)))
                    for e in range(E):
                        link_up(v.tensor_tensor_scan(INC[:, :, e], ONE[:, :], B[:, :, e], 0.0, ALU.mult, ALU.add))
                    link_up(v.tensor_tensor(B[:, :, :], INC[:, :, :], B[:, :, :], ALU.subtract))
                    link_up(v.tensor_tensor(POS[:, :, :], psv(2 * i), B[:, :, :], ALU.add))

                for e in range(E):
                    link_up(v.memset(W8[:, e:e + 1], float(E - e)))
                link_up(v.memset(ONE[:, :], 1.0))
                first_of(LG, 0)
                v.tensor_copy(OHB[:, 0, :, :], OH[0][:, :, :]).then_inc(ohb, 1)
                link_up(v.scalar_tensor_tensor(B[:, :, :], OH[0][:, :, :], BIG, LG[:, :, :], ALU.mult, ALU.add))
                first_of(B, 1)
                places(0, POS)
                link_up(v.tensor_tensor(A[:, :, :], OH[0][:, :, :], POS[:, :, :], ALU.mult))
                link_up(v.tensor_reduce(PT1[:, :], A[:, :, :], AX.X, ALU.add))
                link_up(v.tensor_scalar(KEPT[:, :], PT1[:, :], float(CAP), None, ALU.is_lt))
                link_up(v.tensor_scalar(USED[:, :], INC[:, NT - 1, :], float(CAP), None, ALU.min))
                link_up(v.tensor_scalar(OVF[:, :], KEPT[:, :], -1.0, 1.0, ALU.mult, ALU.add))
                v.tensor_tensor(OHB[:, 1, :, :], OH[1][:, :, :], over_e(OVF[:, :]), ALU.mult).then_inc(ohb, 1)
                places(1, POS)
                link_up(v.tensor_tensor(A[:, :, :], POS[:, :, :], over_t(USED[:, :]), ALU.add))
                link_up(v.tensor_tensor(A[:, :, :], A[:, :, :], OH[1][:, :, :], ALU.mult))
                link_up(v.tensor_reduce(PT2[:, :], A[:, :, :], AX.X, ALU.add))
                link_up(v.tensor_scalar(T2[:, :], PT2[:, :], float(CAP), None, ALU.is_lt))
                link_up(v.tensor_tensor(T2[:, :], T2[:, :], OVF[:, :], ALU.mult))
                link_up(v.tensor_tensor(FB[:, :], OVF[:, :], T2[:, :], ALU.subtract))
                for r, pos, gate, out in ((R[0], PT1, KEPT, S1), (R[1], PT2, T2, S2)):
                    link_up(v.tensor_scalar(out[:, :], r[:, :], -float(CAP), float(N), ALU.mult, ALU.add))
                    link_up(v.tensor_tensor(out[:, :], out[:, :], pos[:, :], ALU.add))
                    link_up(v.tensor_tensor(out[:, :], out[:, :], gate[:, :], ALU.mult))
                dve.wait_ge(consts, 5)
                link_up(v.tensor_copy(TOK[:, :], TOKI[:, :]))
                link_up(v.tensor_scalar(TOK[:, :], TOK[:, :], float(N), None, ALU.add))
                link_up(v.tensor_tensor(TOK[:, :], TOK[:, :], FB[:, :], ALU.mult))
                link_up(v.tensor_tensor(S1[:, :], S1[:, :], S2[:, :], ALU.add))
                link_up(v.tensor_tensor(S1[:, :], S1[:, :], TOK[:, :], ALU.add))
                link_up(v.tensor_copy(SLOT[:, :], S1[:, :]))
                link_up(v.tensor_scalar(S1[:, :], S1[:, :], float(N - 1), None, ALU.min))
                link_up(v.tensor_copy(TAKE[:, :], S1[:, :]))
                link_up(v.tensor_scalar(KEPT[:, :], FB[:, :], -1.0, 1.0, ALU.mult, ALU.add))
                dve.sem_inc(slots, 1)


def networks(nc, io, scratch, keep, kind):
    experts, shared, dense = kind == "experts", kind == "shared", kind == "dense"
    FBK = F // P
    KX = D // P
    with ExitStack() as ctx:
        sb = lambda name, shape, dt=F32: ctx.enter_context(nc.sbuf_tensor(f"{name}_{kind}", shape, dt))
        sem = lambda name: ctx.enter_context(nc.semaphore(f"{kind}_{name}"))
        XI = sb("XI", [P, TPC, D])
        XT = sb("XT", [P, KX, CH])
        W1 = sb("W1", [P, KX, F])
        W2 = sb("W2", [P, FBK, D])
        B1 = sb("B1", [P, E if experts else 1, FBK])
        B2 = sb("B2", [P, E if experts else 1, D])
        HT = sb("HT", [P, FBK, CH])
        Y = sb("Y", [P, TPC, D])
        YG = sb("YG", [P, TPC, D])
        G2 = sb("G2", [P, 2, KX])
        RD = sb("RD", [P, NT])
        ident = keep["ident"]
        ps = ctx.enter_context(nc.psum_tensor(f"ps_{kind}", [P, 8, CH], F32))
        TB, HB, YB = 0, 2, 6
        b_in, w1_in, w2_in, xi_ready, xposed, xt_ready = sem("b_in"), sem("w1_in"), sem("w2_in"), sem("xi"), sem("xposed"), sem("xt")
        h_ps, h_act, y_ps, y_taken, y_sum, y_done, y_out = sem("h_ps"), sem("h_act"), sem("y_ps"), sem("y_taken"), sem("y_sum"), sem("y_done"), sem("y_out")
        yg_in, root, gated = sem("yg_in"), sem("root"), sem("gated")
        nb = 4 if dense else 2
        with nc.Block() as block:
            @block.sync
            def _(sp):
                if experts:
                    sp.dma_start(B1[:, :, :], io["w_b1"].rearrange("e (f p) -> p e f", p=P), allow_slow_non_contiguous=True).then_inc(b_in, 16)
                    sp.dma_start(B2[:, :, :].rearrange("p e d -> p (e d)"), io["w_b2"].rearrange("e d -> (e d)").rearrange("(a n) -> a n", a=1).broadcast_to([P, E * D])).then_inc(b_in, 16)
                else:
                    sp.dma_start(B1[:, 0, :], io["w_b1"].rearrange("(f p) -> p f", p=P), allow_slow_non_contiguous=True).then_inc(b_in, 16)
                    sp.dma_start(B2[:, 0, :], io["w_b2"].rearrange("(a n) -> a n", a=1).broadcast_to([P, D])).then_inc(b_in, 16)
                    sp.dma_start(W1[:, :, :], io["w_1"].rearrange("(k p) f -> p k f", p=P)).then_inc(w1_in, 16)
                    sp.dma_start(W2[:, :, :], io["w_2"].rearrange("(f p) d -> p f d", p=P)).then_inc(w2_in, 16)
                if dense:
                    sp.dma_start(G2[:, 0, :], io["ln2_g"].rearrange("(k p) -> p k", p=P), allow_slow_non_contiguous=True).then_inc(b_in, 16)
                    sp.dma_start(G2[:, 1, :], io["ln2_b"].rearrange("(k p) -> p k", p=P), allow_slow_non_contiguous=True).then_inc(b_in, 16)

                def load_x(i):
                    if experts:
                        sp.dma_start(XI[:, :, :], scratch["xs"][bass.ds(i * CH, CH), :].rearrange("(j p) d -> p j d", p=P)).then_inc(xi_ready, 16)
                    if shared:
                        sp.dma_start(XT[:, :, :], scratch["xnT"][:, bass.ds(i * CH, CH)].rearrange("(k p) n -> p k n", p=P)).then_inc(xt_ready, 16)

                sp.sem_inc(y_ps, TPC)
                sp.sem_inc(y_done, TPC)
                load_x(0)
                if experts:
                    sp.dma_start(W1[:, :, :], io["w_1"][0, :, :].rearrange("(k p) f -> p k f", p=P)).then_inc(w1_in, 16)
                with sp.Fori(0, NC) as i:
                    after = sp.snap((i + 1) % NC)
                    if experts:
                        sp.wait_ge(xposed, KX * (i + 1))
                        load_x(after)
                        sp.wait_ge(y_ps, TPC * (i + 1))
                        sp.dma_start(W2[:, :, :], io["w_2"][bass.ds(i, 1), :, :].rearrange("e (f p) d -> p (e f) d", p=P)).then_inc(w2_in, 16)
                        sp.wait_ge(h_ps, FBK * (i + 1))
                        sp.dma_start(W1[:, :, :], io["w_1"][bass.ds(after, 1), :, :].rearrange("e (k p) f -> p (e k) f", p=P)).then_inc(w1_in, 16)
                    if shared:
                        sp.wait_ge(h_ps, FBK * (i + 1))
                        load_x(after)
                    if dense:
                        sp.wait_ge(y_done, TPC * (i + 1))
                        sp.dma_start(YG[:, :, :], io["x"].rearrange("o (t p) d -> p (o t) d", p=P)[:, bass.ds(i * TPC, TPC), :]).then_inc(yg_in, 16)
                    if experts or dense:
                        sp.wait_ge(y_done, TPC * (i + 2))
                    if experts:
                        sp.dma_start(scratch["ys"][bass.ds(i * CH, CH), :].rearrange("(j p) d -> p j d", p=P), Y[:, :, :]).then_inc(y_out, 16)
                    if dense:
                        sp.dma_start(io["out"].rearrange("o (t p) d -> p (o t) d", p=P)[:, bass.ds(i * TPC, TPC), :], Y[:, :, :]).then_inc(y_out, 16)
                if experts or dense:
                    sp.wait_ge(y_out, 16 * (NC + 1))
                if experts:
                    sp.wait_ge(xi_ready, 16 * (NC + 1))
                    sp.wait_ge(w1_in, 16 * (NC + 1))
                if shared:
                    sp.wait_ge(xt_ready, 16 * (NC + 1))

            if shared:
                @block.gpsimd
                def _(pool):
                    for t in range(NT):
                        if t % TPC == 0 and t:
                            pool.wait_ge(y_done, TPC + t)
                        nc.gpsimd.indirect_dma_start(out=YG[:, t % TPC, :], out_offset=None, in_=scratch["ys"],
                                                     in_offset=bass.IndirectOffsetOnAxis(ap=keep["TAKE"][:, t:t + 1], axis=0)).then_inc(yg_in, 16)

            @block.tensor
            def _(pe):
                def transposes():
                    for k in range(KX):
                        for j in range(TPC):
                            mm = nc.tensor.transpose(ps[:, TB + k, j * P:(j + 1) * P], XI[:, j, k * P:(k + 1) * P], ident[:, :])
                        mm.then_inc(xposed, 1)

                if experts or dense:
                    pe.wait_ge(xi_ready, 16 if experts else TPC)
                    transposes()
                with pe.Fori(0, NC) as i:
                    pe.wait_ge(xt_ready, 16 * (i + 1) if shared else KX * (i + 1))
                    pe.wait_ge(w1_in, 16 * (i + 1) if experts else 16)
                    for f in range(FBK):
                        pe.wait_ge(h_act, FBK * i + f + 1)
                        for k in range(KX):
                            mm = nc.tensor.matmul(ps[:, HB + f % 4, :], W1[:, k, f * P:(f + 1) * P], XT[:, k, :], start=(k == 0), stop=(k == KX - 1))
                        mm.then_inc(h_ps, 1)
                    if experts or dense:
                        pe.wait_ge(xi_ready, 16 * (i + 2) if experts else TPC * (i + 2))
                        transposes()
                    pe.wait_ge(w2_in, 16 * (i + 1) if experts else 16)
                    pe.wait_ge(h_act, FBK * (i + 1) + 4)
                    for j in range(TPC):
                        pe.wait_ge(y_taken, TPC * i + j + 1)
                        for f in range(FBK):
                            mm = nc.tensor.matmul(ps[:, YB + j % 2, 0:D], HT[:, f, j * P:(j + 1) * P], W2[:, f, :], start=(f == 0), stop=(f == FBK - 1))
                        mm.then_inc(y_ps, 1)

            @block.scalar
            def _(act):
                act.sem_inc(h_act, 4)

                def evacuate(need):
                    for k in range(KX):
                        act.wait_ge(xposed, need + k + 1)
                        if dense:
                            nc.scalar.activation(XT[:, k, :], ps[:, TB + k, :], ACT.Identity, scale=G2[:, 0, k:k + 1], bias=G2[:, 1, k:k + 1]).then_inc(xt_ready, 1)
                        else:
                            nc.scalar.activation(XT[:, k, :], ps[:, TB + k, :], ACT.Copy).then_inc(xt_ready, 1)

                if dense:
                    act.wait_ge(root, 1)
                    nc.scalar.activation(RD[:, :], RD[:, :], ACT.Sqrt).then_inc(root, 1)
                act.wait_ge(b_in, 16 * nb)
                if experts or dense:
                    evacuate(0)
                with act.Fori(0, NC) as i:
                    for f in range(FBK):
                        act.wait_ge(h_ps, FBK * i + f + 1)
                        bias = B1[:, bass.ds(i, 1), f:f + 1].rearrange("p a f -> p (a f)") if experts else B1[:, 0, f:f + 1]
                        nc.scalar.activation(HT[:, f, :], ps[:, HB + f % 4, :], ACT.Gelu, bias=bias).then_inc(h_act, 1)
                    if experts or dense:
                        evacuate(KX * (i + 1))
                    if shared:
                        act.wait_ge(y_done, TPC * (i + 2))
                        nc.scalar.activation(keep["G"][:, bass.ds(TPC * i, TPC), :], Y[:, :, :], ACT.Silu).then_inc(gated, 1)

            @block.vector
            def _(dve):
                dve.sem_inc(y_taken, 2)
                dve.sem_inc(gated if shared else y_out, 1 if shared else 16)
                MV, X1, G = keep["MV"], keep["X1"], keep["G"]
                tile = lambda buf, i, j: buf[:, bass.ds(TPC * i + j, 1), :].rearrange("p a d -> p (a d)")

                def center(i):
                    for j in range(TPC):
                        nc.vector.tensor_scalar(XI[:, j, :], tile(X1, i, j), tile(MV, i, j)[:, 0:1], RD[:, bass.ds(TPC * i + j, 1)],
                                                ALU.subtract, ALU.mult).then_inc(xi_ready, 1)
                if dense:
                    nc.vector.tensor_scalar(RD[:, :], MV[:, :, 1], EPS, None, ALU.add).then_inc(root, 1)
                    dve.wait_ge(root, 2)
                    nc.vector.reciprocal(RD[:, :], RD[:, :]).then_inc(root, 1)
                    dve.wait_ge(root, 3)
                    center(0)
                dve.wait_ge(b_in, 16 * nb)
                with dve.Fori(0, NC) as i:
                    if dense:
                        dve.wait_ge(xposed, KX * (i + 1))
                        center((i + 1) % NC)
                    for j in range(TPC):
                        dve.wait_ge(y_ps, TPC * (i + 1) + j + 1)
                        if j == 0:
                            if experts or dense:
                                dve.wait_ge(y_out, 16 * (i + 1))
                            else:
                                dve.wait_ge(gated, i + 1)
                        bias = B2[:, bass.ds(i, 1), :].rearrange("p a d -> p (a d)") if experts else B2[:, 0, :]
                        if experts:
                            nc.vector.tensor_tensor(Y[:, j, :], ps[:, YB + j % 2, 0:D], bias, ALU.add).then_inc(y_done, 1)
                            dve.wait_ge(y_done, TPC * (i + 1) + j + 1)
                            dve.sem_inc(y_taken, 1)
                            continue
                        nc.vector.tensor_tensor(Y[:, j, :], ps[:, YB + j % 2, 0:D], bias, ALU.add).then_inc(y_taken, 1)
                        dve.wait_ge(y_taken, TPC * i + j + 3)
                        if shared:
                            t = TPC * i + j
                            if j == 0:
                                dve.wait_ge(yg_in, 16 * TPC * (i + 1))
                            nc.vector.tensor_scalar(YG[:, j, :], YG[:, j, :], keep["KEPT"][:, bass.ds(t, 1)], None, ALU.mult).then_inc(y_sum, 1)
                            dve.wait_ge(y_sum, TPC * i + j + 1)
                            nc.vector.scalar_tensor_tensor(Y[:, j, :], Y[:, j, :], keep["FB"][:, bass.ds(t, 1)], YG[:, j, :], ALU.mult, ALU.add).then_inc(y_done, 1)
                        if dense:
                            nc.vector.tensor_tensor(Y[:, j, :], Y[:, j, :], tile(X1, i, j), ALU.add).then_inc(y_sum, 1)
                            dve.wait_ge(y_sum, 2 * (TPC * i + j) + 1)
                            nc.vector.tensor_tensor(Y[:, j, :], Y[:, j, :], tile(G, i, j), ALU.mult).then_inc(y_sum, 1)
                            dve.wait_ge(y_sum, 2 * (TPC * i + j) + 2)
                            if j == 0:
                                dve.wait_ge(yg_in, 16 * (i + 1))
                            nc.vector.tensor_tensor(Y[:, j, :], Y[:, j, :], YG[:, j, :], ALU.add).then_inc(y_done, 1)


def project_attention(nc, io, scratch, keep):
    with ExitStack() as ctx:
        sb = lambda name, shape, dt=F32: ctx.enter_context(nc.sbuf_tensor("wo_" + name, shape, dt))
        sem = lambda name: ctx.enter_context(nc.semaphore("wo_" + name))
        AO = sb("AO", [P, 2, CH])
        DN = sb("DN", [P, 2, CH])
        RC = sb("RC", [P, 2, CH])
        AT = sb("AT", [P, 2, CH])
        WO = sb("WO", [P, 2, D])
        BO = sb("BO", [P, D])
        ST2 = sb("ST2", [P, NT, 6])
        X1, XN, MV = keep["X1"], keep["XN"], keep["MV"]
        ps = ctx.enter_context(nc.psum_tensor("psO", [P, 4, CH], F32))
        w_in, a_in, inv, at_ready, o_ps, o_sum, x1_ready, st_ready, mv_ready = (sem("o_w_in"), sem("o_a_in"), sem("o_inv"), sem("o_at"), sem("o_ps"),
                                                                                sem("o_sum"), sem("o_x1"), sem("o_st"), sem("o_mv"))
        ao = scratch["ao"].rearrange("(k g) (h r) n -> k g h r n", k=2, h=HG)
        with nc.Block() as block:
            @block.sync
            def _(sp):
                sp.dma_start(WO[:, :, :], io["wo"].rearrange("(k p) n -> p k n", p=P)).then_inc(w_in, 16)
                sp.dma_start(BO[:, :], io["bo"].rearrange("(a n) -> a n", a=1).broadcast_to([P, D])).then_inc(w_in, 16)
                sp.sem_inc(at_ready, 2)
                with sp.Fori(0, NC) as c:
                    sp.wait_ge(at_ready, 2 * (c + 1))
                    for k in range(2):
                        for g in range(2):
                            for h in range(HG):
                                rows = slice(g * 64 + h * HD, g * 64 + (h + 1) * HD)
                                cols = bass.ds(c * CH, CH)
                                sp.dma_start(AO[rows, k, :], ao[k, g, h, 0:HD, cols]).then_inc(a_in, 16)
                                sp.dma_start(DN[rows, k, :], ao[k, g, h, HD:HD + 1, cols].broadcast_to([HD, CH])).then_inc(a_in, 16)

            @block.tensor
            def _(pe):
                pe.wait_ge(w_in, 32)
                with pe.Fori(0, NC) as c:
                    pe.wait_ge(at_ready, 2 * (c + 2))
                    for j in range(TPC):
                        pe.wait_ge(o_sum, TPC * c + j + 1)
                        for k in range(2):
                            mm = nc.tensor.matmul(ps[:, j, 0:D], AT[:, k, j * P:(j + 1) * P], WO[:, k, :], start=(k == 0), stop=(k == 1))
                        mm.then_inc(o_ps, 1)

            @block.vector
            def _(dve):
                dve.sem_inc(o_sum, 4)
                dve.sem_inc(o_ps, TPC)
                dve.wait_ge(w_in, 32)
                tile = lambda buf, c, j: buf[:, bass.ds(TPC * c + j, 1), :].rearrange("p a d -> p (a d)")
                with dve.Fori(0, NC) as c:
                    dve.wait_ge(a_in, 16 * 32 * (c + 1))
                    for k in range(2):
                        nc.vector.reciprocal(RC[:, k, :], DN[:, k, :]).then_inc(inv, 1)
                    dve.wait_ge(o_ps, TPC * (c + 1))
                    for k in range(2):
                        dve.wait_ge(inv, 2 * c + k + 1)
                        nc.vector.tensor_tensor(AT[:, k, :], AO[:, k, :], RC[:, k, :], ALU.mult).then_inc(at_ready, 1)
                    for j in range(TPC):
                        dve.wait_ge(o_ps, TPC * (c + 1) + j + 1)
                        nc.vector.tensor_tensor(tile(X1, c, j), ps[:, j, 0:D], tile(XN, c, j), ALU.add).then_inc(o_sum, 1)
                        dve.wait_ge(o_sum, TPC * c + j + 5)
                        nc.vector.tensor_tensor(tile(X1, c, j), tile(X1, c, j), BO[:, :], ALU.add).then_inc(x1_ready, 1)
                        dve.wait_ge(x1_ready, TPC * c + j + 1)
                        nc.vector.bn_stats(tile(ST2, c, j), tile(X1, c, j)).then_inc(st_ready, 1)
                dve.wait_ge(st_ready, NT)
                for t in range(NT):
                    nc.vector.bn_aggr(MV[:, t, :], ST2[:, t, :]).then_inc(mv_ready, 1)


def build(nc, io):
    scratch = {
        "xnT": nc.dram_tensor("xnT", [D, N], F32, kind="Internal").ap(),
        "v": nc.dram_tensor("v_rows", [N, 2 * D], F32, kind="Internal").ap(),
        "qkp": nc.dram_tensor("qk_parts", [3, 2 * D, N], BF16, kind="Internal").ap(),
        "ao": nc.dram_tensor("attention_sums", [NG, P, N], F32, kind="Internal").ap(),
        "xs": nc.dram_tensor("rows_by_place", [2 * N, D], F32, kind="Internal").ap(),
        "ys": nc.dram_tensor("experts_rows", [N, D], F32, kind="Internal").ap(),
    }
    with ExitStack() as ctx:
        sb = lambda name, shape, dt=F32: ctx.enter_context(nc.sbuf_tensor(name, shape, dt))
        keep = {
            "ident": sb("ident", [P, P]), "XN": sb("XN", [P, NT, D]), "LG": sb("LG", [P, NT, E]),
            "FB": sb("FB", [P, NT]), "KEPT": sb("KEPT", [P, NT]), "SLOT": sb("SLOT", [P, NT], I32), "TAKE": sb("TAKE", [P, NT], I32),
            "MV": sb("MVX", [P, NT, 2]), "routed": ctx.enter_context(nc.semaphore("routed")),
        }
        project_tokens(nc, io, scratch, keep)
        route(nc, scratch, keep)
        attend(nc, scratch)
        keep["G"], keep["X1"] = sb("G", [P, NT, D]), sb("X1", [P, NT, D])
        networks(nc, dict(w_1=io["w1"], w_b1=io["b1"], w_2=io["w2"], w_b2=io["b2"]), scratch, keep, "experts")
        networks(nc, dict(w_1=io["sw1"], w_b1=io["sb1"], w_2=io["sw2"], w_b2=io["sb2"]), scratch, keep, "shared")
        project_attention(nc, io, scratch, keep)
        networks(nc, dict(w_1=io["W1"], w_b1=io["bb1"], w_2=io["W2"], w_b2=io["bb2"], ln2_g=io["ln2_g"], ln2_b=io["ln2_b"],
                          x=io["x"], out=io["out"]), scratch, keep, "dense")


_INS = {"x": "L0_attn_x", "ln1_g": "L0_attn_ln1_g", "ln1_b": "L0_attn_ln1_b", "wqkv": "L0_attn_Wqkv", "bqkv": "L0_attn_bqkv",
        "wo": "L0_attn_Wo", "bo": "L0_attn_bo", "ln2_g": "L0_attn_ln2_g", "ln2_b": "L0_attn_ln2_b", "W1": "L0_attn_W1",
        "bb1": "L0_attn_b1", "W2": "L0_attn_W2", "bb2": "L0_attn_b2", "rb": "L0_ffn_rb", "w1": "L0_ffn_w1", "b1": "L0_ffn_b1",
        "w2": "L0_ffn_w2", "b2": "L0_ffn_b2", "sw1": "L0_ffn_sw1", "sb1": "L0_ffn_sb1", "sw2": "L0_ffn_sw2", "sb2": "L0_ffn_sb2"}


def rotary_tables():
    inv = np.float32(1) / (10000.0 ** (np.arange(0, HD, 2) / HD)).astype(np.float32)
    angle = np.arange(N, dtype=np.float32)[:, None] * inv[None]
    c, s = np.cos(angle), np.sin(angle)
    return np.concatenate([c, c], 1).astype(np.float32), np.concatenate([-s, s], 1).astype(np.float32)


def kernel(**inputs):
    import concourse.bacc as bacc
    from concourse.bass_utils import run_bass_kernel_spmd

    nc = bacc.Bacc("TRN2", target_bir_lowering=False, num_devices=1)
    arrays = {short: np.ascontiguousarray(inputs[name]) for short, name in _INS.items()}
    arrays["rwT"] = np.ascontiguousarray(np.asarray(inputs["L0_ffn_rw"]).T)
    arrays["cos"], arrays["sin"] = rotary_tables()
    feed, io = {}, {}
    for short, a in arrays.items():
        feed[f"in_{short}"] = a
        io[short] = nc.dram_tensor(f"in_{short}", a.shape, mybir.dt.from_np(a.dtype), kind="ExternalInput").ap()
    io["out"] = nc.dram_tensor("out", (1, N, D), F32, kind="ExternalOutput").ap()
    build(nc, io)
    r = run_bass_kernel_spmd(nc, [feed], core_ids=[0])
    return r.results[0]["out"]
```

```python
import numpy as np
import concourse.bass as bass
from concourse import mybir
from contextlib import ExitStack

F32, BF16, I32 = mybir.dt.float32, mybir.dt.bfloat16, mybir.dt.int32
F32R = mybir.dt.float32r
ACT, ALU, AX = mybir.ActivationFunctionType, mybir.AluOpType, mybir.AxisListType

P = 128
N, D = 4096, 256
H, HD = 16, 16
F, E = 1024, 8
NT = N // P
CH = 512
NC = N // CH
TPC = CH // P
EPS = 1e-5
def root_steps(nc, dve, made, out, var, root, t):
    sem, n = made
    steps = (lambda: nc.vector.reciprocal(out, root),
             lambda: nc.vector.tensor_tensor(t, out, out, ALU.mult),
             lambda: nc.vector.tensor_tensor(t, t, var, ALU.mult),
             lambda: nc.vector.tensor_scalar(t, t, -0.5, 1.5, ALU.mult, ALU.add),
             lambda: nc.vector.tensor_tensor(out, out, t, ALU.mult))
    for step in steps:
        step().then_inc(sem, 1)
        n += 1
        dve.wait_ge(sem, n)
    return n


def project_tokens(nc, io, scratch, keep):
    x, wqkv, rwT = io["x"], io["wqkv"], io["rwT"]
    with ExitStack() as ctx:
        sb = lambda name, shape, dt=F32: ctx.enter_context(nc.sbuf_tensor("proj_" + name, shape, dt))
        sem = lambda name: ctx.enter_context(nc.semaphore("proj_" + name))
        X = sb("X", [P, NT, D])
        XN = keep["XN"]
        XNs = sb("XNs", [P, TPC, D])
        XNN = sb("XNN", [P, TPC, D])
        XT = sb("XT", [P, 2, CH])
        NX = sb("NX", [P, 2, CH])
        W = sb("W", [P, 2, 3 * D])
        RW = sb("RW", [P, 2, E])
        BQ = sb("BQ", [P, 3 * D])
        RB = sb("RB", [P, E])
        G1 = sb("G1", [P, 2, 2])
        COS = sb("COS", [P, NT, HD])
        SIN = sb("SIN", [P, NT, HD])
        QB = sb("QB", [P, 2, 2 * D])
        QC = sb("QC", [P, 2, 2 * D])
        QS = sb("QS", [P, 2, 2 * D])
        QR = sb("QR", [P, TPC, 2 * D])
        VA = sb("VA", [P, 2, H, 2 * HD])
        S1 = sb("S1", [P, 2, F])
        S2 = sb("S2", [P, F // P, D])
        SB1 = sb("SB1", [P, F // P])
        SB2 = sb("SB2", [P, D])
        HT = sb("HT", [P, F // P, CH])
        YS = sb("YS", [P, TPC, D])
        PT = sb("PT", [P, 4, 3, CH], BF16)
        RS = sb("RS", [P, 2, CH])
        ST = sb("ST", [P, NT, 6])
        MV = sb("MV", [P, NT, 2])
        SD = sb("SD", [P, NT])
        VE = sb("VE", [P, NT])
        TN = sb("TN", [P, NT])
        R1 = sb("R1", [P, NT])
        MV2 = sb("MV2", [P, NT, 2])
        SD2 = sb("SD2", [P, NT])
        R2 = sb("R2", [P, NT])
        B2 = sb("B2", [P, NT])
        ident = keep["ident"]
        LG = keep["LG"]
        ps = ctx.enter_context(nc.psum_tensor("psA", [P, 8, CH], F32))
        TB, QKB, VB, QTB = 0, 2, 4, 6
        FBK = F // P
        w_in, stats, std, rstd = sem("w_in"), sem("stats"), sem("std"), sem("rstd")
        xn_ready, stats2, std2, rstd2 = sem("xn_ready"), sem("stats2"), sem("std2"), sem("rstd2")
        chunk_in, xposed, xt_ready = sem("chunk_in"), sem("xposed"), sem("xt_ready")
        h_ps, h_act, y_ps, y_taken, y_out = sem("h_ps"), sem("h_act"), sem("y_ps"), sem("y_taken"), sem("y_out")
        qk_ps, qk_biased, v_ps, v_biased = sem("qk_ps"), sem("qk_biased"), sem("v_ps"), sem("v_biased")
        cosed, sined, rotated = sem("cosed"), sem("sined"), sem("rotated")
        qt_ps, part1, rest1, part2, part3 = sem("qt_ps"), sem("part1"), sem("rest1"), sem("part2"), sem("part3")
        va_ok = sem("va_ok")
        v_out, p_out = [sem("v_out0"), sem("v_out1")], [sem(f"p_out{u}") for u in range(4)]
        consts, first_part = sem("consts"), sem("first_part")
        x_in = [sem(f"x_in{c}") for c in range(NC)]
        xv = x.rearrange("o (t p) d -> p (o t) d", p=P)
        with nc.Block() as block:
            @block.sync
            def _(sp):
                for c in range(NC):
                    sp.dma_start(X[:, TPC * c:TPC * (c + 1), :], xv[:, TPC * c:TPC * (c + 1), :]).then_inc(x_in[c], 16)
                for dst, src in ((W[:, :, :], wqkv.rearrange("(k p) n -> p k n", p=P)),
                                 (RW[:, :, :], rwT.rearrange("(k p) n -> p k n", p=P)),
                                 (COS[:, :, :], io["cos"].rearrange("(t p) d -> p t d", p=P)),
                                 (SIN[:, :, :], io["sin"].rearrange("(t p) d -> p t d", p=P)),
                                 (BQ[:, :], io["bqkv"].rearrange("(a n) -> a n", a=1).broadcast_to([P, 3 * D])),
                                 (RB[:, :], io["rb"].rearrange("(a n) -> a n", a=1).broadcast_to([P, E])),
                                 (G1[:, 0, :], io["ln1_g"].rearrange("(k p) -> p k", p=P)),
                                 (G1[:, 1, :], io["ln1_b"].rearrange("(k p) -> p k", p=P)),
                                 (S1[:, :, :], io["sw1"].rearrange("(k p) f -> p k f", p=P)),
                                 (S2[:, :, :], io["sw2"].rearrange("(f p) d -> p f d", p=P)),
                                 (SB1[:, :], io["sb1"].rearrange("(f p) -> p f", p=P)),
                                 (SB2[:, :], io["sb2"].rearrange("(a n) -> a n", a=1).broadcast_to([P, D]))):
                    sp.dma_start(dst, src, allow_slow_non_contiguous=True).then_inc(w_in, 16)
                with sp.Fori(0, NC) as c:
                    col = sp.snap(c * CH)
                    for j in range(TPC):
                        sp.wait_ge(v_biased, TPC * c + j + 1)
                        sp.dma_start(scratch["v"].rearrange("(t p) n -> p t n", p=P)[:, bass.ds(TPC * c + j, 1), :],
                                     VA[:, j % 2, :, :].rearrange("p h d -> p (h d)").rearrange("p (a n) -> p a n", a=1)).then_inc(v_out[j % 2], 16)
                    sp.wait_ge(y_taken, 4 * (c + 2))
                    sp.dma_start(scratch["ysh"].rearrange("(t p) d -> p t d", p=P)[:, bass.ds(TPC * c, TPC), :], YS[:, :, :]).then_inc(y_out, 16)
                    for u in range(4):
                        sp.wait_ge(part3, 4 * (c + 1) + u + 1)
                        if u == 0:
                            sp.sem_inc(first_part, 1)
                        sp.dma_start(scratch["qkp"].rearrange("s (u p) n -> u p s n", u=4)[u, :, :, bass.ds(col, CH)],
                                     PT[:, u, :, :]).then_inc(p_out[u], 16)
                sp.wait_ge(y_out, 16 * (NC + 1))
                for half in range(2):
                    sp.wait_ge(v_out[half], 16 * (NT // 2 + 1))
                for u in range(4):
                    sp.wait_ge(p_out[u], 16 * (NC + 1))

            @block.gpsimd
            def _(pool):
                nc.gpsimd.memset(ident[:, :], 0.0).then_inc(consts, 1)
                nc.gpsimd.memset(VA[:, :, :, :], 0.0).then_inc(consts, 1)
                pool.wait_ge(consts, 2)
                nc.gpsimd.affine_select(out=ident[:, :], in_=ident[:, :], compare_op=ALU.not_equal, fill=1.0,
                                        base=0, pattern=[[-1, P]], channel_multiplier=1).then_inc(va_ok, 1)
                nc.gpsimd.memset(VA[:, :, :, HD:HD + 1], 1.0).then_inc(va_ok, 1)
                pool.wait_ge(w_in, 16 * 12)
                with pool.Fori(0, NC) as c:
                    for j in range(TPC):
                        pool.wait_ge(qk_biased, TPC * c + j + 1)
                        pool.wait_ge(rotated, TPC * c + j + 1)
                        nc.gpsimd.tensor_tensor(
                            QC[:, j % 2, :].rearrange("p (h d) -> p h d", d=HD),
                            QB[:, j % 2, :].rearrange("p (h d) -> p h d", d=HD),
                            COS[:, bass.ds(TPC * c + j, 1), :].broadcast_to([P, 2 * H, HD]), ALU.mult).then_inc(cosed, 1)

            @block.vector
            def _(dve):
                dve.sem_inc(rotated, 2)
                dve.sem_inc(rest1, 2)
                dve.sem_inc(qt_ps, 4)
                dve.sem_inc(part3, 4)
                dve.sem_inc(y_taken, 4)
                dve.sem_inc(y_out, 16)
                dve.sem_inc(v_out[0], 16)
                dve.sem_inc(v_out[1], 16)
                for c in range(NC):
                    dve.wait_ge(x_in[c], 16)
                    for t in range(TPC * c, TPC * (c + 1)):
                        nc.vector.bn_stats(ST[:, t, :], X[:, t, :]).then_inc(stats, 1)
                for t in range(NT):
                    dve.wait_ge(stats, t + 1)
                    nc.vector.bn_aggr(MV[:, t, :], ST[:, t, :]).then_inc(std, 1)
                dve.wait_ge(std, NT)
                nc.vector.tensor_scalar(VE[:, :], MV[:, :, 1], EPS, None, ALU.add).then_inc(std, 1)
                dve.wait_ge(rstd, 1)
                root_steps(nc, dve, (rstd, 1), R1[:, :], VE[:, :], SD[:, :], TN[:, :])
                for t in range(NT):
                    nc.vector.tensor_scalar(XN[:, t, :], X[:, t, :], MV[:, t, 0:1], R1[:, t:t + 1],
                                            ALU.subtract, ALU.mult).then_inc(xn_ready, 1)
                for t in range(NT):
                    dve.wait_ge(xn_ready, t + 1)
                    nc.vector.bn_stats(ST[:, t, :], XN[:, t, :]).then_inc(stats2, 1)
                for t in range(NT):
                    dve.wait_ge(stats2, t + 1)
                    nc.vector.bn_aggr(MV2[:, t, :], ST[:, t, :]).then_inc(std2, 1)
                dve.wait_ge(std2, NT)
                nc.vector.tensor_scalar(VE[:, :], MV2[:, :, 1], EPS, None, ALU.add).then_inc(std2, 1)
                dve.wait_ge(rstd2, 1)
                root_steps(nc, dve, (rstd2, 1), R2[:, :], VE[:, :], SD2[:, :], TN[:, :])
                nc.vector.scalar_tensor_tensor(B2[:, :], MV2[:, :, 0], -1.0, R2[:, :], ALU.mult, ALU.mult).then_inc(rstd2, 1)
                dve.wait_ge(w_in, 16 * 12)
                dve.wait_ge(va_ok, 2)

                def rotate(c, j):
                    dve.wait_ge(cosed, TPC * c + j + 1)
                    dve.wait_ge(sined, 2 * (TPC * c + j + 1))
                    nc.vector.tensor_tensor(QR[:, j, :], QC[:, j % 2, :], QS[:, j % 2, :], ALU.add).then_inc(rotated, 1)

                with dve.Fori(0, NC) as c:
                    for j in range(TPC):
                        dve.wait_ge(qk_ps, TPC * c + j + 1)
                        dve.wait_ge(rotated, TPC * c + j + 1)
                        nc.vector.tensor_tensor(QB[:, j % 2, :], ps[:, QKB + j % 2, :], BQ[:, 0:2 * D], ALU.add).then_inc(qk_biased, 1)
                        dve.wait_ge(v_ps, TPC * c + j + 1)
                        dve.wait_ge(v_out[j % 2], 16 * (2 * c + j // 2 + 1))
                        nc.vector.tensor_tensor(VA[:, j % 2, :, 0:HD],
                                                ps[:, VB + j % 2, 0:D].rearrange("p (h d) -> p h d", d=HD),
                                                BQ[:, 2 * D:3 * D].rearrange("p (h d) -> p h d", d=HD), ALU.add).then_inc(v_biased, 1)
                        nc.vector.tensor_tensor(LG[:, bass.ds(TPC * c + j, 1), :].rearrange("p a e -> p (a e)"),
                                                ps[:, VB + j % 2, D:D + E], RB[:, :], ALU.add).then_inc(keep["routed"], 1)
                        dve.wait_ge(qk_biased, TPC * c + j + 1)
                        qb = QB[:, j % 2, :].rearrange("p (h d) -> p h d", d=HD)
                        qs = QS[:, j % 2, :].rearrange("p (h d) -> p h d", d=HD)
                        for lo, hi in ((0, HD // 2), (HD // 2, 0)):
                            nc.vector.tensor_tensor(qs[:, :, lo:lo + HD // 2], qb[:, :, hi:hi + HD // 2],
                                                    SIN[:, bass.ds(TPC * c + j, 1), lo:lo + HD // 2].broadcast_to([P, 2 * H, HD // 2]),
                                                    ALU.mult).then_inc(sined, 1)
                        if j == 0:
                            dve.wait_ge(qt_ps, 4 * (c + 1))
                        if j > 0:
                            rotate(c, j - 1)
                    rotate(c, TPC - 1)
                    for j in range(TPC):
                        dve.wait_ge(y_ps, TPC * c + j + 1)
                        if j == 0:
                            dve.wait_ge(y_out, 16 * (c + 1))
                        nc.vector.tensor_tensor(YS[:, j, :], ps[:, VB + j % 2, 0:D], SB2[:, :], ALU.add).then_inc(y_taken, 1)
                    for u in range(5):
                        if u < 4:
                            dve.wait_ge(part1, 4 * c + u + 1)
                            if u < 2:
                                dve.wait_ge(part3, 4 * (c + 1))
                            else:
                                dve.wait_ge(part3, 4 * (c + 1) + u - 1)
                            nc.vector.tensor_tensor(RS[:, u % 2, :], ps[:, QTB + u % 2, :], PT[:, u, 0, :], ALU.subtract).then_inc(rest1, 1)
                        if u > 0:
                            dve.wait_ge(part2, 4 * c + u)
                            nc.vector.tensor_tensor(PT[:, u - 1, 2, :], RS[:, (u - 1) % 2, :], PT[:, u - 1, 1, :],
                                                    ALU.subtract).then_inc(part3, 1)

            @block.scalar
            def _(act):
                for u in range(4):
                    act.sem_inc(p_out[u], 16)
                act.wait_ge(std, NT + 1)
                nc.scalar.activation(SD[:, :], VE[:, :], ACT.Sqrt).then_inc(rstd, 1)
                act.wait_ge(std2, NT + 1)
                nc.scalar.activation(SD2[:, :], VE[:, :], ACT.Sqrt).then_inc(rstd2, 1)
                act.wait_ge(rstd2, 7)
                act.wait_ge(w_in, 16 * 12)

                def stage(t):
                    nc.scalar.activation(XNs[:, :, :], XN[:, bass.ds(t, TPC), :], ACT.Copy).then_inc(chunk_in, 1)
                    for j in range(TPC):
                        nc.scalar.activation(XNN[:, j, :], XN[:, bass.ds(t + j, 1), :].rearrange("p a n -> p (a n)"),
                                             ACT.Identity, scale=R2[:, bass.ds(t + j, 1)], bias=B2[:, bass.ds(t + j, 1)]).then_inc(chunk_in, 1)

                def take(c):
                    for k in range(2):
                        act.wait_ge(xposed, 4 * c + k + 1)
                        nc.scalar.activation(XT[:, k, :], ps[:, TB + k, :], ACT.Copy).then_inc(xt_ready, 1)
                    for k in range(2):
                        act.wait_ge(xposed, 4 * c + k + 3)
                        nc.scalar.activation(NX[:, k, :], ps[:, TB + k, :], ACT.Identity, scale=G1[:, 0, k:k + 1],
                                             bias=G1[:, 1, k:k + 1]).then_inc(xt_ready, 1)

                stage(0)
                take(0)
                with act.Fori(0, NC) as c:
                    stage((c + 1) % NC * TPC)
                    for f in range(FBK):
                        act.wait_ge(h_ps, FBK * c + f + 1)
                        nc.scalar.activation(HT[:, f, :], ps[:, TB + f % 2, :], ACT.Gelu, bias=SB1[:, f:f + 1]).then_inc(h_act, 1)
                    take(c + 1)
                    for u in range(5):
                        if u < 4:
                            act.wait_ge(qt_ps, 4 * (c + 1) + u + 1)
                            act.wait_ge(p_out[u], 16 * (c + 1))
                            nc.scalar.activation(PT[:, u, 0, :], ps[:, QTB + u % 2, :], ACT.Copy).then_inc(part1, 1)
                        if u > 0:
                            act.wait_ge(rest1, 4 * c + u + 2)
                            nc.scalar.activation(PT[:, u - 1, 1, :], RS[:, (u - 1) % 2, :], ACT.Copy).then_inc(part2, 1)

            @block.tensor
            def _(pe):
                def transposes(c):
                    for v, (src, need) in enumerate(((XNs, 1), (XNN, 5))):
                        pe.wait_ge(chunk_in, 5 * c + need)
                        for k in range(2):
                            if v == 1:
                                pe.wait_ge(xt_ready, 4 * c + k + 1)
                            for j in range(TPC):
                                mm = nc.tensor.transpose(ps[:, TB + k, j * P:(j + 1) * P], src[:, j, k * P:(k + 1) * P], ident[:, :])
                            mm.then_inc(xposed, 1)

                pe.sem_inc(keep["routed"], TPC)
                pe.wait_ge(va_ok, 1)
                pe.wait_ge(w_in, 16 * 12)
                transposes(0)
                with pe.Fori(0, NC) as c:
                    pe.wait_ge(xt_ready, 4 * c + 4)
                    for j in range(TPC):
                        tok = slice(j * P, (j + 1) * P)
                        pe.wait_ge(rotated, TPC * c + j + 1)
                        for k in range(2):
                            mm = nc.tensor.matmul(ps[:, QKB + j % 2, :], NX[:, k, tok], W[:, k, 0:2 * D], start=(k == 0), stop=(k == 1))
                        mm.then_inc(qk_ps, 1)
                        if j == 0:
                            pe.wait_ge(y_taken, TPC * (c + 1))
                        if j >= 2:
                            pe.wait_ge(keep["routed"], TPC * (c + 1) + j - 1)
                        for k in range(2):
                            nc.tensor.matmul(ps[:, VB + j % 2, 0:D], NX[:, k, tok], W[:, k, 2 * D:3 * D], start=(k == 0), stop=(k == 1))
                        for k in range(2):
                            mm = nc.tensor.matmul(ps[:, VB + j % 2, D:D + E], XT[:, k, tok], RW[:, k, :], start=(k == 0), stop=(k == 1))
                        mm.then_inc(v_ps, 1)
                    for f in range(FBK):
                        if f >= 2:
                            pe.wait_ge(h_act, FBK * c + f - 1)
                        for k in range(2):
                            mm = nc.tensor.matmul(ps[:, TB + f % 2, :], S1[:, k, f * P:(f + 1) * P], XT[:, k, :], start=(k == 0), stop=(k == 1))
                        mm.then_inc(h_ps, 1)
                    pe.wait_ge(h_act, FBK * (c + 1))
                    transposes(c + 1)
                    for j in range(TPC):
                        if j == 0:
                            pe.wait_ge(keep["routed"], TPC * (c + 2))
                        if j >= 2:
                            pe.wait_ge(y_taken, TPC * (c + 1) + j - 1)
                        for f in range(FBK):
                            mm = nc.tensor.matmul(ps[:, VB + j % 2, 0:D], HT[:, f, j * P:(j + 1) * P], S2[:, f, :], start=(f == 0), stop=(f == FBK - 1))
                        mm.then_inc(y_ps, 1)
                    for u in range(4):
                        pe.wait_ge(rest1, 4 * c + u + 1)
                        for j in range(TPC):
                            if u == 0:
                                pe.wait_ge(rotated, TPC * c + j + 3)
                            mm = nc.tensor.transpose(ps[:, QTB + u % 2, j * P:(j + 1) * P], QR[:, j, u * P:(u + 1) * P], ident[:, :])
                        mm.then_inc(qt_ps, 1)
HG = 4
NG = H // HG
PAIRS = ((0, 0), (0, 1), (1, 0), (1, 1), (0, 2), (2, 0))
MROW = HD * len(PAIRS)
KROWS = MROW + 2 * HG
BIG = -1e30


def attend(nc, scratch):
    qk = scratch["qkp"].rearrange("s (w g h d) n -> s w g d h n", w=2, g=NG, h=HG)
    vv = scratch["v"].rearrange("(t p) (g n) -> g p t n", p=P, g=NG)
    ao = scratch["ao"].rearrange("(g h d) n -> g h d n", g=NG, h=HG)
    den = scratch["den"].rearrange("(g h) n -> g h n", g=NG)
    steps = [(0, c) for c in range(NC)] + [(1, c) for c in reversed(range(NC))]
    LS = len(steps)
    units = [[(kb, max(0, kb - TPC * c)) for kb in range(TPC * (c + 1))] for _, c in steps]
    jobs = [[(j, h, kc) for kc in range(c + 1) for j in range(TPC) for h in range(HG)] for _, c in steps]
    S_PER = sum(2 * len(u) + 1 for u in units)
    J_PER = sum(len(j) for j in jobs)
    U_PER = sum(len(u) for u in units)
    s_base = [1 + sum(2 * len(u) + 1 for u in units[:i]) for i in range(LS + 1)]
    u_base = [sum(len(u) for u in units[:i]) for i in range(LS + 1)]
    j_base = [sum(len(j) for j in jobs[:i]) for i in range(LS + 1)]
    RING = 3
    rows_at = lambda i: len(units[i]) - 2
    s_of = lambda i, k, pair: s_base[i] + 2 * k + pair + (1 if k > rows_at(i) else 0)
    s_rows = lambda i: s_base[i] + 2 * (rows_at(i) + 1)

    with ExitStack() as ctx:
        sb = lambda name, shape, dt=F32: ctx.enter_context(nc.sbuf_tensor("attn_" + name, shape, dt))
        sem = lambda name: ctx.enter_context(nc.semaphore("attn_" + name))
        KS = [sb(f"KS{w}", [P, HG, N], BF16) for w in range(2)]
        V = [sb(f"V{w}", [P, NT, HG * 2 * HD]) for w in range(2)]
        QS = sb("QS", [P, 4, HG, CH], BF16)
        PB = sb("PB", [P, RING, HG, CH])
        MX = sb("MX", [P, TPC * HG, NC])
        NM = sb("NM", [P, TPC * HG])
        MH = sb("MH", [P, TPC, 2, HG], BF16)
        OU = sb("OU", [P, 2, CH])
        idb = sb("idb", [P, P], BF16)
        mask_qk = sb("mask_qk", [P, P], BF16)
        mask_kq = sb("mask_kq", [P, P], BF16)
        ps = ctx.enter_context(nc.psum_tensor("psB", [P, 8, CH], F32))
        PV, MB = 4, 5
        q_in = [sem(f"q_in{s}") for s in range(4)]
        kv_in = [[sem(f"kv{w}_in{c}") for c in range(NC)] for w in range(2)]
        consts, masks, kones, stepped = sem("consts"), sem("masks"), sem("kones"), sem("stepped")
        scored, expd, pv_done, ou_ready = sem("scored"), sem("expd"), sem("pv_done"), sem("ou_ready")
        maxed, reduced, negmax, mparts = sem("maxed"), sem("reduced"), sem("negmax"), sem("mparts")
        ou_out = [sem("ou_out0"), sem("ou_out1")]

        with nc.Block() as block:
            @block.sync
            def _(sp):
                def load_q(group, i):
                    c = steps[i % LS][1]
                    for r, (a, _) in enumerate(PAIRS):
                        sp.dma_start(QS[HD * r:HD * (r + 1), i % 4, :, :],
                                     qk[a, 0, bass.ds(group, 1), :, :, c * CH:(c + 1) * CH].rearrange("g d h n -> (g d) h n")).then_inc(q_in[i % 4], 16)

                def load_k(w, group, c):
                    for r, (_, b) in enumerate(PAIRS):
                        sp.dma_start(KS[w][HD * r:HD * (r + 1), :, c * CH:(c + 1) * CH],
                                     qk[b, 1, bass.ds(group, 1), :, :, c * CH:(c + 1) * CH].rearrange("g d h n -> (g d) h n")).then_inc(kv_in[w][c], 16)

                def load_v(w, group, c):
                    sp.dma_start(V[w][:, TPC * c:TPC * (c + 1), :],
                                 vv[bass.ds(group, 1), :, TPC * c:TPC * (c + 1), :].rearrange("g p t n -> (g p) t n")).then_inc(kv_in[w][c], 16)

                def store_sums(first, i):
                    w, c = steps[i]
                    for h in range(HG):
                        sp.dma_start(ao[bass.ds(first + w, 1), h, :, c * CH:(c + 1) * CH].rearrange("g r n -> (g r) n"),
                                     OU[32 * h:32 * h + HD, i % 2, :]).then_inc(ou_out[i % 2], 16)
                        sp.dma_start(den[bass.ds(first + w, 1), h:h + 1, c * CH:(c + 1) * CH].rearrange("g r n -> (g r) n"),
                                     OU[32 * h + HD:32 * h + HD + 1, i % 2, :]).then_inc(ou_out[i % 2], 16)

                for c in range(NC):
                    if c < 2:
                        load_q(0, c)
                    load_k(0, 0, c)
                    load_v(0, 0, c)
                with sp.Fori(0, NG // 2) as g:
                    here = sp.snap(g * 2)
                    after = sp.snap((g + 1) % (NG // 2) * 2)
                    for i in range(LS):
                        sp.wait_ge(scored, g * S_PER + s_base[i])
                        sp.sem_inc(stepped, 1)
                        load_q(here + steps[i + 2][0] if i + 2 < LS else after, i + 2)
                        if i == 0:
                            sp.wait_ge(pv_done, g * U_PER + RING)
                            sp.sem_inc(stepped, 1)
                            for c in range(NC):
                                load_k(1, here + 1, c)
                                load_v(1, here + 1, c)
                        if i == NC + 1:
                            sp.wait_ge(pv_done, g * U_PER + RING + u_base[NC])
                            sp.sem_inc(stepped, 1)
                            for c in range(NC):
                                load_k(0, after, c)
                                load_v(0, after, c)
                        if i > 0:
                            sp.wait_ge(ou_ready, g * LS + i + 1)
                            sp.sem_inc(stepped, 1)
                            store_sums(here, i - 1)
                    sp.wait_ge(ou_ready, g * LS + LS + 1)
                    sp.sem_inc(stepped, 1)
                    store_sums(here, LS - 1)
                for half in range(2):
                    sp.wait_ge(ou_out[half], 32 * HG * (NG * NC // 2 + 1))
                for s in range(4):
                    sp.wait_ge(q_in[s], 96 * (LS // 4 * (NG // 2) + (1 if s < 2 else 0)))
                for c in range(NC):
                    for w in range(2):
                        sp.wait_ge(kv_in[w][c], 112 * (NG // 2 + 1 - w))

            @block.gpsimd
            def _(pool):
                nc.gpsimd.memset(idb[:, :], 0.0).then_inc(consts, 1)
                nc.gpsimd.memset(mask_qk[:, :], 0.0).then_inc(consts, 1)
                nc.gpsimd.memset(mask_kq[:, :], 0.0).then_inc(consts, 1)
                pool.wait_ge(consts, 3)
                nc.gpsimd.affine_select(out=idb[:, :], in_=idb[:, :], compare_op=ALU.not_equal, fill=1.0, base=0,
                                        pattern=[[-1, P]], channel_multiplier=1).then_inc(masks, 1)
                nc.gpsimd.affine_select(out=mask_qk[:, :], in_=mask_qk[:, :], compare_op=ALU.is_ge, fill=BIG, base=0,
                                        pattern=[[-1, P]], channel_multiplier=1).then_inc(masks, 1)
                nc.gpsimd.affine_select(out=mask_kq[:, :], in_=mask_kq[:, :], compare_op=ALU.is_ge, fill=BIG, base=0,
                                        pattern=[[1, P]], channel_multiplier=-1).then_inc(masks, 1)
                pool.wait_ge(masks, 3)
                made = 3
                for w in range(2):
                    for c in range(NC):
                        part = KS[w][MROW:KROWS, :, c * CH:(c + 1) * CH]
                        nc.gpsimd.memset(part, 0.0).then_inc(consts, 1)
                        for first in range(2):
                            made += 1
                            pool.wait_ge(consts, made)
                            nc.gpsimd.affine_select(out=part, in_=part, compare_op=ALU.not_equal, fill=1.0, base=-HG * first,
                                                    pattern=[[-1, HG], [0, CH]], channel_multiplier=1).then_inc(consts, 1)
                        made += 1
                        pool.wait_ge(consts, made)
                        pool.sem_inc(kones, 1)

            @block.tensor
            def _(pe):
                def max_job(reads, i, off, job, used):
                    j, h, kc = job
                    w, c = steps[i % LS]
                    width = CH if kc < c else P * (j + 1)
                    if h == 0 and j == 0:
                        pe.wait_ge(kv_in[w][kc], 112 * (reads + 1))
                    if used is not None:
                        pe.wait_ge(reduced, used)
                    bank = MB + off % 3
                    mm = nc.tensor.matmul(ps[:, bank, 0:width], QS[0:MROW, i % 4, h, j * P:(j + 1) * P],
                                          KS[w][0:MROW, h, kc * CH:kc * CH + width], start=True, stop=(kc < c))
                    if kc == c:
                        mm = nc.tensor.matmul(ps[:, bank, width - P:width], idb[:, :], mask_qk[:, :], start=False, stop=True)
                    mm.then_inc(maxed, 1)

                def max_rows(s, used, need):
                    pe.wait_ge(mparts, need)
                    if used is not None:
                        pe.wait_ge(expd, used)
                    for j in range(TPC):
                        mm = nc.tensor.matmul(ps[MROW:KROWS, 2 * (s % 2), j * P:(j + 1) * P],
                                              MH[:, j, :, :].rearrange("p s h -> p (s h)"), idb[:, :], start=True, stop=True)
                    mm.then_inc(scored, 1)

                def scores(g, i, k, pair):
                    w, c = steps[i]
                    kb, r = units[i][k]
                    s = s_of(i, k, pair)
                    if s > 1:
                        pe.wait_ge(expd, g * S_PER + s - 1)
                    if pair == 0 and kb % TPC == 0:
                        pe.wait_ge(kones, NC * w + kb // TPC + 1)
                    for b in range(2):
                        h = 2 * pair + b
                        bank = 2 * (s % 2) + b
                        mm = nc.tensor.matmul(ps[:, bank, r * P:CH], KS[w][0:KROWS, h, kb * P:(kb + 1) * P],
                                              QS[0:KROWS, i % 4, h, r * P:CH], start=True, stop=(kb < TPC * c))
                        if kb >= TPC * c:
                            mm = nc.tensor.matmul(ps[:, bank, r * P:(r + 1) * P], idb[:, :], mask_kq[:, :], start=False, stop=True)
                    mm.then_inc(scored, 1)

                def weigh(g, i, k):
                    w = steps[i][0]
                    kb, r = units[i][k]
                    pe.wait_ge(expd, g * S_PER + s_of(i, k, 1) + 1)
                    if k == 0:
                        pe.wait_ge(ou_ready, g * LS + i + 1)
                    u = u_base[i] + k
                    for h in range(HG):
                        mm = nc.tensor.matmul(ps[32 * h:32 * (h + 1), PV, r * P:CH], V[w][:, kb, 32 * h:32 * (h + 1)],
                                              PB[:, u % RING, h, r * P:CH], start=(k == 0), stop=(k == len(units[i]) - 1))
                    mm.then_inc(pv_done, 1)

                pe.sem_inc(ou_ready, 1)
                pe.sem_inc(pv_done, RING)
                pe.wait_ge(masks, 3)
                pe.wait_ge(q_in[0], 96)
                for n, job in enumerate(jobs[0]):
                    max_job(0, 0, n, job, n - 2 if n > 2 else None)
                max_rows(0, None, 1)
                with pe.Fori(0, NG // 2) as g:
                    pe.wait_ge(expd, g * S_PER + 1)
                    behind = None
                    for i in range(LS):
                        todo = jobs[(i + 1) % LS]
                        at = 0

                        def some(upto):
                            nonlocal at
                            while at < upto:
                                off = j_base[i + 1] + at
                                max_job(g + (1 if i == LS - 1 else 0), i + 1, off, todo[at], g * J_PER + off - 2)
                                at += 1

                        for k in range(len(units[i])):
                            share = len(todo) if k >= rows_at(i) else -(-len(todo) * (k + 1) // rows_at(i))
                            new = share - at
                            scores(g, i, k, 0)
                            if k == 0:
                                pe.wait_ge(q_in[(i + 1) % 4], 96 * (LS // 4 * g + (i + 1) // 4 + 1))
                            some(share - new + new // 4)
                            scores(g, i, k, 1)
                            some(share - new + new // 2)
                            if k == rows_at(i):
                                max_rows(s_rows(i), g * S_PER + s_rows(i) - 1, g * LS + i + 2)
                            if behind is not None:
                                weigh(g, *behind)
                            behind = (i, k)
                            some(share)
                    weigh(g, *behind)

            @block.scalar
            def _(act):
                def rows(i, s, need):
                    act.wait_ge(scored, need)
                    nc.scalar.activation(QS[MROW:KROWS, i % 4, :, :],
                                         ps[MROW:KROWS, 2 * (s % 2):2 * (s % 2) + 1, :].broadcast_to([2 * HG, HG, CH]),
                                         ACT.Copy).then_inc(expd, 1)

                def sums(g, i):
                    act.wait_ge(pv_done, RING + g * U_PER + u_base[i + 1])
                    act.wait_ge(ou_out[i % 2], 32 * HG * (g * (LS // 2) + i // 2 + 1))
                    nc.scalar.activation(OU[:, i % 2, :], ps[:, PV, :], ACT.Copy).then_inc(ou_ready, 1)

                act.sem_inc(ou_out[0], 32 * HG)
                act.sem_inc(ou_out[1], 32 * HG)
                act.wait_ge(q_in[0], 96)
                rows(0, 0, 1)
                with act.Fori(0, NG // 2) as g:
                    for i in range(LS):
                        for k in range(len(units[i])):
                            kb, r = units[i][k]
                            u = u_base[i] + k
                            for pair in range(2):
                                s = s_of(i, k, pair)
                                act.wait_ge(scored, g * S_PER + s + 1)
                                if pair == 0:
                                    act.wait_ge(pv_done, g * U_PER + u + 1)
                                nc.scalar.activation(PB[:, u % RING, 2 * pair:2 * pair + 2, r * P:CH],
                                                     ps[:, 2 * (s % 2):2 * (s % 2) + 2, r * P:CH], ACT.Exp, scale=HD ** -0.5).then_inc(expd, 1)
                            if k == rows_at(i):
                                rows(i + 1, s_rows(i), g * S_PER + s_rows(i) + 1)
                            if k == 0 and i > 0:
                                sums(g, i - 1)
                    sums(g, LS - 1)

            @block.vector
            def _(dve):
                def reduce_job(off, need, job, c):
                    j, h, kc = job
                    w = CH if kc < c else P * (j + 1)
                    dve.wait_ge(maxed, need)
                    nc.vector.tensor_reduce(MX[:, HG * j + h, kc:kc + 1], ps[:, MB + off % 3, 0:w], AX.X, ALU.max).then_inc(reduced, 1)

                def finish(c, all_jobs, before):
                    dve.wait_ge(reduced, all_jobs)
                    if not isinstance(before, int):
                        dve.wait_ge(mparts, before)
                    nc.vector.tensor_reduce(NM[:, :], MX[:, :, 0:c + 1], AX.X, ALU.max, negate=True).then_inc(negmax, 1)
                    dve.wait_ge(negmax, 2 * before + 1)
                    nm = NM[:, :].rearrange("p (j h) -> p j h", h=HG)
                    nc.vector.tensor_copy(MH[:, :, 0, :], nm).then_inc(negmax, 1)
                    dve.wait_ge(negmax, 2 * before + 2)
                    nc.vector.tensor_tensor(MH[:, :, 1, :], nm, MH[:, :, 0, :], ALU.subtract).then_inc(mparts, 1)

                for n, job in enumerate(jobs[0]):
                    reduce_job(n, n + 1, job, 0)
                finish(0, len(jobs[0]), 0)
                with dve.Fori(0, NG // 2) as g:
                    for i in range(LS):
                        c = steps[(i + 1) % LS][1]
                        dve.wait_ge(negmax, 2 * (g * LS + i + 1))
                        for at, job in enumerate(jobs[(i + 1) % LS]):
                            off = j_base[i + 1] + at
                            reduce_job(off, g * J_PER + off + 1, job, c)
                        dve.wait_ge(scored, g * S_PER + s_base[i])
                        finish(c, g * J_PER + j_base[i + 1] + len(jobs[(i + 1) % LS]), g * LS + i + 1)
def route(nc, scratch, keep):
    CAP = N // E
    with ExitStack() as ctx:
        sb = lambda name, shape, dt=F32: ctx.enter_context(nc.sbuf_tensor("route_" + name, shape, dt))
        sem = lambda name: ctx.enter_context(nc.semaphore("route_" + name))
        LG, FB, KEPT, SLOT, TAKE, XN = keep["LG"], keep["FB"], keep["KEPT"], keep["SLOT"], keep["TAKE"], keep["XN"]
        W8 = sb("W8", [P, E])
        ONE = sb("ONE", [P, NT])
        TOK = sb("TOK", [P, NT])
        TOKI = sb("TOKI", [P, NT], I32)
        tri = sb("tri", [P, P], BF16)
        ones = sb("ones", [P, P], BF16)
        ZR = sb("ZR", [P, D])
        OH = [sb(f"OH{i}", [P, NT, E]) for i in range(2)]
        OHB = sb("OHB", [P, 2, NT, E], BF16)
        A = sb("A", [P, NT, E])
        B = sb("B", [P, NT, E])
        INC = sb("INC", [P, NT, E])
        POS = sb("POS", [P, NT, E])
        M = sb("M", [P, NT])
        R = [sb(f"R{i}", [P, NT]) for i in range(2)]
        PT1 = sb("PT1", [P, NT])
        PT2 = sb("PT2", [P, NT])
        USED = sb("USED", [P, E])
        OVF = sb("OVF", [P, NT])
        T2 = sb("T2", [P, NT])
        S1 = sb("S1", [P, NT])
        S2 = sb("S2", [P, NT])
        ps = ctx.enter_context(nc.psum_tensor("psR", [P, 4, CH], F32))
        consts, cum, link, ohb, slots = sem("r_consts"), sem("r_cum"), sem("r_link"), sem("r_ohb"), sem("r_slots")
        zeroed, sent = sem("r_zeroed"), sem("r_sent")
        over_t = lambda ap: ap.rearrange("p (a e) -> p a e", a=1).broadcast_to([P, NT, E])
        over_e = lambda ap: ap.rearrange("p (t a) -> p t a", a=1).broadcast_to([P, NT, E])
        with nc.Block() as block:
            @block.sync
            def _(sp):
                sp.wait_ge(consts, 3)
                for t in range(E * CAP // P):
                    sp.dma_start(scratch["xs"][t * P:(t + 1) * P, :], ZR[:, :]).then_inc(zeroed, 16)

            @block.gpsimd
            def _(pool):
                nc.gpsimd.memset(tri[:, :], 1.0).then_inc(consts, 1)
                nc.gpsimd.memset(ones[:, :], 1.0).then_inc(consts, 1)
                nc.gpsimd.memset(ZR[:, :], 0.0).then_inc(consts, 1)
                pool.wait_ge(consts, 3)
                nc.gpsimd.affine_select(out=tri[:, :], in_=tri[:, :], compare_op=ALU.is_gt, fill=0.0, base=0,
                                        pattern=[[1, P]], channel_multiplier=-1).then_inc(consts, 1)
                nc.gpsimd.iota(TOKI[:, :], pattern=[[P, NT]], base=0, channel_multiplier=1).then_inc(consts, 1)
                pool.wait_ge(slots, 1)
                pool.wait_ge(zeroed, 16 * E * CAP // P)
                for t in range(NT):
                    nc.gpsimd.indirect_dma_start(out=scratch["xs"], out_offset=bass.IndirectOffsetOnAxis(ap=SLOT[:, t:t + 1], axis=0),
                                                 in_=XN[:, t, :], in_offset=None).then_inc(sent, 16)
                pool.wait_ge(sent, 16 * NT)

            @block.tensor
            def _(pe):
                for i in range(2):
                    pe.wait_ge(ohb, i + 1)
                    pe.wait_ge(consts, 5)
                    rhs = OHB[:, i, :, :].rearrange("p t e -> p (t e)")
                    nc.tensor.matmul(ps[:, 2 * i, 0:NT * E], tri[:, :], rhs, start=True, stop=True).then_inc(cum, 1)
                    nc.tensor.matmul(ps[:, 2 * i + 1, 0:NT * E], ones[:, :], rhs, start=True, stop=True).then_inc(cum, 1)

            @block.vector
            def _(dve):
                v = nc.vector
                made = [0]

                def link_up(ins):
                    made[0] += 1
                    ins.then_inc(link, 1)
                    dve.wait_ge(link, made[0])

                def first_of(logits, i):
                    link_up(v.tensor_reduce(M[:, :], logits[:, :, :], AX.X, ALU.max))
                    link_up(v.tensor_tensor(A[:, :, :], logits[:, :, :], over_e(M[:, :]), ALU.is_equal))
                    link_up(v.tensor_tensor(A[:, :, :], A[:, :, :], over_t(W8[:, :]), ALU.mult))
                    link_up(v.tensor_reduce(R[i][:, :], A[:, :, :], AX.X, ALU.max))
                    link_up(v.tensor_tensor(OH[i][:, :, :], A[:, :, :], over_e(R[i][:, :]), ALU.is_equal))

                def places(i, out):
                    psv = lambda b: ps[:, b, 0:NT * E].rearrange("p (t e) -> p t e", e=E)
                    dve.wait_ge(cum, 2 * (i + 1))
                    link_up(v.tensor_copy(B[:, :, :], psv(2 * i + 1)))
                    for e in range(E):
                        link_up(v.tensor_tensor_scan(INC[:, :, e], ONE[:, :], B[:, :, e], 0.0, ALU.mult, ALU.add))
                    link_up(v.tensor_tensor(B[:, :, :], INC[:, :, :], B[:, :, :], ALU.subtract))
                    link_up(v.tensor_tensor(POS[:, :, :], psv(2 * i), B[:, :, :], ALU.add))

                for e in range(E):
                    link_up(v.memset(W8[:, e:e + 1], float(E - e)))
                link_up(v.memset(ONE[:, :], 1.0))
                first_of(LG, 0)
                v.tensor_copy(OHB[:, 0, :, :], OH[0][:, :, :]).then_inc(ohb, 1)
                link_up(v.scalar_tensor_tensor(B[:, :, :], OH[0][:, :, :], BIG, LG[:, :, :], ALU.mult, ALU.add))
                first_of(B, 1)
                places(0, POS)
                link_up(v.tensor_tensor(A[:, :, :], OH[0][:, :, :], POS[:, :, :], ALU.mult))
                link_up(v.tensor_reduce(PT1[:, :], A[:, :, :], AX.X, ALU.add))
                link_up(v.tensor_scalar(KEPT[:, :], PT1[:, :], float(CAP), None, ALU.is_lt))
                link_up(v.tensor_scalar(USED[:, :], INC[:, NT - 1, :], float(CAP), None, ALU.min))
                link_up(v.tensor_scalar(OVF[:, :], KEPT[:, :], -1.0, 1.0, ALU.mult, ALU.add))
                v.tensor_tensor(OHB[:, 1, :, :], OH[1][:, :, :], over_e(OVF[:, :]), ALU.mult).then_inc(ohb, 1)
                places(1, POS)
                link_up(v.tensor_tensor(A[:, :, :], POS[:, :, :], over_t(USED[:, :]), ALU.add))
                link_up(v.tensor_tensor(A[:, :, :], A[:, :, :], OH[1][:, :, :], ALU.mult))
                link_up(v.tensor_reduce(PT2[:, :], A[:, :, :], AX.X, ALU.add))
                link_up(v.tensor_scalar(T2[:, :], PT2[:, :], float(CAP), None, ALU.is_lt))
                link_up(v.tensor_tensor(T2[:, :], T2[:, :], OVF[:, :], ALU.mult))
                link_up(v.tensor_tensor(FB[:, :], OVF[:, :], T2[:, :], ALU.subtract))
                for r, pos, gate, out in ((R[0], PT1, KEPT, S1), (R[1], PT2, T2, S2)):
                    link_up(v.tensor_scalar(out[:, :], r[:, :], -float(CAP), float(N), ALU.mult, ALU.add))
                    link_up(v.tensor_tensor(out[:, :], out[:, :], pos[:, :], ALU.add))
                    link_up(v.tensor_tensor(out[:, :], out[:, :], gate[:, :], ALU.mult))
                dve.wait_ge(consts, 5)
                link_up(v.tensor_copy(TOK[:, :], TOKI[:, :]))
                link_up(v.tensor_scalar(TOK[:, :], TOK[:, :], float(N), None, ALU.add))
                link_up(v.tensor_tensor(TOK[:, :], TOK[:, :], FB[:, :], ALU.mult))
                link_up(v.tensor_tensor(S1[:, :], S1[:, :], S2[:, :], ALU.add))
                link_up(v.tensor_tensor(S1[:, :], S1[:, :], TOK[:, :], ALU.add))
                link_up(v.tensor_copy(SLOT[:, :], S1[:, :]))
                link_up(v.tensor_scalar(S1[:, :], S1[:, :], float(N - 1), None, ALU.min))
                link_up(v.tensor_copy(TAKE[:, :], S1[:, :]))
                link_up(v.tensor_scalar(KEPT[:, :], FB[:, :], -1.0, 1.0, ALU.mult, ALU.add))
                dve.sem_inc(slots, 1)


def networks(nc, io, scratch, keep, kind):
    experts, dense = kind == "experts", kind == "dense"
    FBK = F // P
    KX = D // P
    QW = 4
    with ExitStack() as ctx:
        sb = lambda name, shape, dt=F32: ctx.enter_context(nc.sbuf_tensor(f"{name}_{kind}", shape, dt))
        sem = lambda name: ctx.enter_context(nc.semaphore(f"{kind}_{name}"))
        EB = E if experts else 1
        XI = sb("XI", [P, TPC, D])
        XF = sb("XF", [P, KX, CH])
        XH, XL = sb("XH", [P, KX, CH], F32R), sb("XL", [P, KX, CH], F32R)
        W1, W2 = sb("W1", [P, KX, F]), sb("W2", [P, FBK, D])
        W1H, W1L = sb("W1H", [P, KX, F], F32R), sb("W1L", [P, KX, F], F32R)
        W2H, W2L = sb("W2H", [P, FBK, D], F32R), sb("W2L", [P, FBK, D], F32R)
        B1 = sb("B1", [P, EB, FBK])
        B2 = sb("B2", [P, EB, D])
        HT = sb("HT", [P, FBK, CH])
        HH, HL = sb("HH", [P, FBK, CH], F32R), sb("HL", [P, FBK, CH], F32R)
        Y = sb("Y", [P, TPC, D])
        X1, MV, ident = keep["XN"], keep["MV"], keep["ident"]
        ps = ctx.enter_context(nc.psum_tensor(f"ps_{kind}", [P, 8, CH], F32))
        TB, HB, YB, OB = 0, 2, 4, 6
        b_in, w1_in, w2_in, x_in, xi_ready = sem("b_in"), sem("w1_in"), sem("w2_in"), sem("x_in"), sem("xi")
        w1_hi, w1_lo, w2_hi, w2_lo = sem("w1_hi"), sem("w1_lo"), sem("w2_hi"), sem("w2_lo")
        xposed, x_sb, x_hi, x_lo = sem("xposed"), sem("x_sb"), sem("x_hi"), sem("x_lo")
        h_ps, h_act, h_hi, h_lo = sem("h_ps"), sem("h_act"), sem("h_hi"), sem("h_lo")
        y_ps, y_taken, y_sum, y_done, y_out = sem("y_ps"), sem("y_taken"), sem("y_sum"), sem("y_done"), sem("y_out")
        if experts:
            AO, DN, AT = sb("AO", [P, 2, CH]), sb("DN", [P, 2, CH]), sb("AT", [P, 2, CH])
            RC = sb("RC", [P, CH])
            WO, BO = sb("WO", [P, 2, D]), sb("BO", [P, D])
            ST = sb("ST", [P, NT, 6])
            wo_in, den_in, inv, inv_out, ao_in, dn_in = sem("wo_in"), sem("den_in"), sem("inv"), sem("inv_out"), sem("ao_in"), sem("dn_in")
            at_ready, o_ps, o_sum, x1_ready, st_ready, mv_ready = sem("at"), sem("o_ps"), sem("o_sum"), sem("x1"), sem("st"), sem("mv")
        if dense:
            G2 = sb("G2", [P, 2, KX])
            SD, VE, RD, TN = [sb(n, [P, NT]) for n in ("SD", "VE", "RD", "TN")]
            XR = sb("XR", [P, TPC, D])
            YS, YG = sb("YS", [P, TPC, D]), sb("YG", [P, TPC, D])
            G = sb("G", [P, TPC, D])
            TI = sb("TI", [P, TPC], I32)
            index, stepped, root, product_made, ys_in, yg_in, kept, mixed, gated = sem("index"), sem("stepped"), sem("root"), sem("product"), sem("ys_in"), sem("yg_in"), sem("kept"), sem("mixed"), sem("gated")
        nb = 2 if experts else 4
        row = lambda ap, n: ap.rearrange("(a n) -> a n", a=1).broadcast_to([P, n])
        tile = lambda buf, i, j: buf[:, bass.ds(TPC * i + j, 1), :].rearrange("p a d -> p (a d)")
        quarter = lambda w, q: w[:, :, :].rearrange("p a b -> p (a b)")[:, q * KX * F // QW:(q + 1) * KX * F // QW]
        with nc.Block() as block:
            @block.sync
            def _(sp):
                if experts:
                    sp.dma_start(XI[:, :, :], scratch["xs"][0:CH, :].rearrange("(j p) d -> p j d", p=P)).then_inc(x_in, 16)
                    sp.dma_start(W1[:, :, :], io["w_1"][0, :, :].rearrange("(k p) f -> p k f", p=P)).then_inc(w1_in, 16)
                    sp.dma_start(W2[:, :, :], io["w_2"][0, :, :].rearrange("(f p) d -> p f d", p=P)).then_inc(w2_in, 16)
                    sp.dma_start(B1[:, :, :], io["w_b1"].rearrange("e (f p) -> p e f", p=P), allow_slow_non_contiguous=True).then_inc(b_in, 16)
                    sp.dma_start(B2[:, :, :].rearrange("p e d -> p (e d)"), row(io["w_b2"].rearrange("e d -> (e d)"), E * D)).then_inc(b_in, 16)
                    sp.dma_start(RC[:, :], scratch["den"].rearrange("h (c n) -> (h c) n", n=CH)).then_inc(den_in, 16)
                    sp.dma_start(WO[:, :, :], io["wo"].rearrange("(k p) n -> p k n", p=P)).then_inc(wo_in, 16)
                    sp.dma_start(BO[:, :], row(io["bo"], D)).then_inc(wo_in, 16)
                    sp.wait_ge(inv, 1)
                    sp.dma_start(scratch["inv"].rearrange("h (c n) -> (h c) n", n=CH), RC[:, :]).then_inc(inv_out, 16)
                    sp.wait_ge(inv_out, 16)
                else:
                    sp.dma_start(W1[:, :, :], io["w_1"].rearrange("(k p) f -> p k f", p=P)).then_inc(w1_in, 16)
                    sp.dma_start(W2[:, :, :], io["w_2"].rearrange("(f p) d -> p f d", p=P)).then_inc(w2_in, 16)
                    sp.dma_start(B1[:, 0, :], io["w_b1"].rearrange("(f p) -> p f", p=P), allow_slow_non_contiguous=True).then_inc(b_in, 16)
                    sp.dma_start(B2[:, 0, :], row(io["w_b2"], D)).then_inc(b_in, 16)
                    sp.dma_start(G2[:, 0, :], io["ln2_g"].rearrange("(k p) -> p k", p=P), allow_slow_non_contiguous=True).then_inc(b_in, 16)
                    sp.dma_start(G2[:, 1, :], io["ln2_b"].rearrange("(k p) -> p k", p=P), allow_slow_non_contiguous=True).then_inc(b_in, 16)
                sp.sem_inc(y_ps, TPC)
                sp.sem_inc(y_done, TPC)
                if experts:
                    sp.sem_inc(at_ready, 2)
                if dense:
                    sp.sem_inc(gated, 1)
                with sp.Fori(0, NC) as i:
                    after = sp.snap((i + 1) % NC)
                    rows = sp.snap(i * CH)
                    if experts:
                        sp.wait_ge(at_ready, 2 * (i + 1))
                        sp.dma_start(AO[:, :, :], scratch["ao"].rearrange("(k p) n -> p k n", p=P)[:, :, bass.ds(rows, CH)]).then_inc(ao_in, 16)
                        for h in range(H):
                            r = h % (H // 2) * HD
                            sp.dma_start(DN[r:r + HD, h // (H // 2), :], scratch["inv"][h:h + 1, bass.ds(rows, CH)].broadcast_to([HD, CH])).then_inc(dn_in, 16)
                        sp.wait_ge(w1_lo, QW * (i + 1))
                        sp.dma_start(W1[:, :, :], io["w_1"][bass.ds(after, 1), :, :].rearrange("e (k p) f -> p (e k) f", p=P)).then_inc(w1_in, 16)
                        sp.wait_ge(w2_lo, QW * (i + 1))
                        sp.dma_start(W2[:, :, :], io["w_2"][bass.ds(after, 1), :, :].rearrange("e (f p) d -> p (e f) d", p=P)).then_inc(w2_in, 16)
                        sp.wait_ge(xposed, KX * (i + 1))
                        sp.dma_start(XI[:, :, :], scratch["xs"][bass.ds(after * CH, CH), :].rearrange("(j p) d -> p j d", p=P)).then_inc(x_in, 16)
                    if dense:
                        sp.wait_ge(gated, i + 1)
                        sp.dma_start(YS[:, :, :], scratch["ysh"].rearrange("(t p) d -> p t d", p=P)[:, bass.ds(i * TPC, TPC), :]).then_inc(ys_in, 16)
                        sp.wait_ge(y_done, TPC * (i + 1))
                        sp.dma_start(XR[:, :, :], io["x"].rearrange("o (t p) d -> p (o t) d", p=P)[:, bass.ds(i * TPC, TPC), :]).then_inc(x_in, 16)
                    sp.wait_ge(y_done, TPC * (i + 2))
                    if experts:
                        sp.dma_start(scratch["ys"][bass.ds(rows, CH), :].rearrange("(j p) d -> p j d", p=P), Y[:, :, :]).then_inc(y_out, 16)
                    else:
                        sp.dma_start(io["out"].rearrange("o (t p) d -> p (o t) d", p=P)[:, bass.ds(i * TPC, TPC), :], Y[:, :, :]).then_inc(y_out, 16)
                sp.wait_ge(y_out, 16 * (NC + 1))
                if experts:
                    sp.wait_ge(x_in, 16 * (NC + 1))
                    sp.wait_ge(w1_in, 16 * (NC + 1))
                    sp.wait_ge(w2_in, 16 * (NC + 1))

            @block.gpsimd
            def _(pool):
                def low(raw, hi, lo, q, ready, done, need):
                    pool.wait_ge(ready, need)
                    nc.gpsimd.tensor_tensor(quarter(lo, q), quarter(raw, q), quarter(hi, q).bitcast(F32), ALU.subtract).then_inc(done, 1)

                for q in range(QW):
                    low(W1, W1H, W1L, q, w1_hi, w1_lo, q + 1)
                if dense:
                    for q in range(QW):
                        low(W2, W2H, W2L, q, w2_hi, w2_lo, q + 1)
                with pool.Fori(0, NC) as i:
                    if experts:
                        for q in range(QW):
                            low(W2, W2H, W2L, q, w2_hi, w2_lo, QW * i + q + 1)
                        for q in range(QW):
                            low(W1, W1H, W1L, q, w1_hi, w1_lo, QW * (i + 1) + q + 1)
                    if dense:
                        pool.wait_ge(gated, i + 1)
                        nc.gpsimd.tensor_copy(TI[:, :], keep["TAKE"][:, bass.ds(TPC * i, TPC)]).then_inc(index, 1)
                        pool.wait_ge(index, i + 1)
                        pool.sem_inc(stepped, 1)
                        for j in range(TPC):
                            nc.gpsimd.indirect_dma_start(out=YG[:, j, :], out_offset=None, in_=scratch["ys"],
                                                         in_offset=bass.IndirectOffsetOnAxis(ap=TI[:, j:j + 1], axis=0)).then_inc(yg_in, 16)
                        for j in range(TPC):
                            pool.wait_ge(y_sum, TPC * i + j + 1)
                            if j == 0:
                                pool.wait_ge(gated, i + 2)
                                pool.wait_ge(x_in, 16 * (i + 1))
                            nc.gpsimd.tensor_tensor(Y[:, j, :], Y[:, j, :], G[:, j, :], ALU.mult).then_inc(product_made, 1)
                            pool.wait_ge(product_made, TPC * i + j + 1)
                            nc.gpsimd.tensor_tensor(Y[:, j, :], Y[:, j, :], XR[:, j, :], ALU.add).then_inc(y_done, 1)

            @block.tensor
            def _(pe):
                def product(out, lhs, rhs, pick_l, pick_r, n):
                    terms = [(b, l, r) for b in range(n) for l, r in ((0, 0), (0, 1), (1, 0))]
                    for at, (b, l, r) in enumerate(terms):
                        mm = nc.tensor.matmul(out, pick_l(lhs[l], b), pick_r(rhs[r], b), start=(at == 0), stop=(at == len(terms) - 1))
                    return mm

                def transposes():
                    for k in range(KX):
                        for j in range(TPC):
                            mm = nc.tensor.transpose(ps[:, TB + k, j * P:(j + 1) * P], XI[:, j, k * P:(k + 1) * P], ident[:, :])
                        mm.then_inc(xposed, 1)

                pe.wait_ge(*((x_in, 16) if experts else (xi_ready, TPC)))
                transposes()
                with pe.Fori(0, NC) as i:
                    pe.wait_ge(x_lo, KX * (i + 1))
                    pe.wait_ge(w1_lo, QW * (i + 1) if experts else QW)
                    for f in range(FBK):
                        pe.wait_ge(h_act, FBK * i + f + 1)
                        product(ps[:, HB + f % 2, :], (W1H, W1L), (XH, XL), lambda w, k: w[:, k, f * P:(f + 1) * P],
                                lambda x, k: x[:, k, :], KX).then_inc(h_ps, 1)
                    pe.wait_ge(*((x_in, 16 * (i + 2)) if experts else (xi_ready, TPC * (i + 2))))
                    transposes()
                    if experts:
                        pe.wait_ge(at_ready, 2 * (i + 2))
                        for j in range(TPC):
                            if j == 0:
                                pe.wait_ge(wo_in, 32)
                            pe.wait_ge(o_sum, TPC * i + j + 1)
                            for k in range(2):
                                mm = nc.tensor.matmul(ps[:, OB + j % 2, 0:D], AT[:, k, j * P:(j + 1) * P], WO[:, k, :], start=(k == 0), stop=(k == 1))
                            mm.then_inc(o_ps, 1)
                    pe.wait_ge(w2_lo, QW * (i + 1) if experts else QW)
                    pe.wait_ge(h_lo, FBK * (i + 1))
                    for j in range(TPC):
                        pe.wait_ge(y_taken, TPC * i + j + 1)
                        product(ps[:, YB + j % 2, 0:D], (HH, HL), (W2H, W2L), lambda h, f: h[:, f, j * P:(j + 1) * P],
                                lambda w, f: w[:, f, :], FBK).then_inc(y_ps, 1)

            @block.scalar
            def _(act):
                act.sem_inc(h_act, 2)

                def high(raw, hi, q, done):
                    nc.scalar.activation(quarter(hi, q), quarter(raw, q), ACT.Copy).then_inc(done, 1)

                def evacuate(need):
                    for k in range(KX):
                        act.wait_ge(xposed, need + k + 1)
                        if dense:
                            nc.scalar.activation(XF[:, k, :], ps[:, TB + k, :], ACT.Identity, scale=G2[:, 0, k:k + 1], bias=G2[:, 1, k:k + 1]).then_inc(x_sb, 1)
                        else:
                            nc.scalar.activation(XF[:, k, :], ps[:, TB + k, :], ACT.Copy).then_inc(x_sb, 1)

                act.wait_ge(w1_in, 16)
                for q in range(QW):
                    high(W1, W1H, q, w1_hi)
                if dense:
                    act.wait_ge(root, 1)
                    nc.scalar.activation(SD[:, :], VE[:, :], ACT.Sqrt).then_inc(root, 1)
                act.wait_ge(b_in, 16 * nb)
                evacuate(0)
                if dense:
                    act.wait_ge(w2_in, 16)
                    for q in range(QW):
                        high(W2, W2H, q, w2_hi)
                with act.Fori(0, NC) as i:
                    for f in range(FBK):
                        act.wait_ge(h_ps, FBK * i + f + 1)
                        bias = B1[:, bass.ds(i, 1), f:f + 1].rearrange("p a f -> p (a f)") if experts else B1[:, 0, f:f + 1]
                        nc.scalar.activation(HT[:, f, :], ps[:, HB + f % 2, :], ACT.Gelu, bias=bias).then_inc(h_act, 1)
                        if experts and f >= 2 and f < 2 + QW:
                            if f == 2:
                                act.wait_ge(w2_in, 16 * (i + 1))
                            high(W2, W2H, f - 2, w2_hi)
                    evacuate(KX * (i + 1))
                    if experts:
                        act.wait_ge(w1_in, 16 * (i + 2))
                        for q in range(QW):
                            high(W1, W1H, q, w1_hi)
                    if dense:
                        act.wait_ge(mixed, TPC * (i + 1))
                        act.wait_ge(y_done, TPC * (i + 1))
                        nc.scalar.activation(G[:, :, :], YS[:, :, :], ACT.Silu).then_inc(gated, 1)

            @block.vector
            def _(dve):
                dve.sem_inc(y_taken, 2)
                dve.sem_inc(y_out, 16)
                if experts:
                    dve.sem_inc(o_sum, 2)
                    dve.sem_inc(o_ps, TPC)

                def center(i):
                    for j in range(TPC):
                        nc.vector.tensor_scalar(XI[:, j, :], tile(X1, i, j), tile(MV, i, j)[:, 0:1], RD[:, bass.ds(TPC * i + j, 1)],
                                                ALU.subtract, ALU.mult).then_inc(xi_ready, 1)

                def cut(src, hi, lo, n, count, ready, made_hi, made_lo):
                    for b in range(n + 1):
                        if b < n:
                            dve.wait_ge(ready, count + b + 1 + (2 if ready is h_act else 0))
                            nc.vector.tensor_copy(hi[:, b, :], src[:, b, :]).then_inc(made_hi, 1)
                        if b > 0:
                            dve.wait_ge(made_hi, count + b)
                            nc.vector.tensor_tensor(lo[:, b - 1, :], src[:, b - 1, :], hi[:, b - 1, :].bitcast(F32), ALU.subtract).then_inc(made_lo, 1)

                if dense:
                    nc.vector.tensor_scalar(VE[:, :], MV[:, :, 1], EPS, None, ALU.add).then_inc(root, 1)
                    dve.wait_ge(root, 2)
                    root_steps(nc, dve, (root, 2), RD[:, :], VE[:, :], SD[:, :], TN[:, :])
                    center(0)
                cut(XF, XH, XL, KX, 0, x_sb, x_hi, x_lo)
                if experts:
                    dve.wait_ge(den_in, 16)
                    nc.vector.reciprocal(RC[:, :], RC[:, :]).then_inc(inv, 1)
                dve.wait_ge(b_in, 16 * nb)
                with dve.Fori(0, NC) as i:
                    if experts:
                        dve.wait_ge(ao_in, 16 * (i + 1))
                        dve.wait_ge(dn_in, 16 * H * (i + 1))
                        dve.wait_ge(o_ps, TPC * (i + 1))
                        for k in range(2):
                            nc.vector.tensor_tensor(AT[:, k, :], AO[:, k, :], DN[:, k, :], ALU.mult).then_inc(at_ready, 1)
                    if dense:
                        dve.wait_ge(xposed, KX * (i + 1))
                        center((i + 1) % NC)
                        dve.wait_ge(ys_in, 16 * (i + 1))
                        dve.wait_ge(yg_in, 16 * TPC * (i + 1))
                        for j in range(TPC):
                            at = bass.ds(TPC * i + j, 1)
                            nc.vector.tensor_scalar(YG[:, j, :], YG[:, j, :], keep["KEPT"][:, at], None, ALU.mult).then_inc(kept, 1)
                        for j in range(TPC):
                            at = bass.ds(TPC * i + j, 1)
                            dve.wait_ge(kept, TPC * i + j + 1)
                            nc.vector.scalar_tensor_tensor(YS[:, j, :], YS[:, j, :], keep["FB"][:, at], YG[:, j, :], ALU.mult, ALU.add).then_inc(mixed, 1)
                    cut(HT, HH, HL, FBK, FBK * i, h_act, h_hi, h_lo)
                    cut(XF, XH, XL, KX, KX * (i + 1), x_sb, x_hi, x_lo)
                    if experts:
                        for j in range(TPC):
                            t = TPC * i + j
                            dve.wait_ge(o_ps, TPC * (i + 1) + j + 1)
                            if j == 0:
                                dve.wait_ge(wo_in, 32)
                            nc.vector.tensor_tensor(tile(X1, i, j), ps[:, OB + j % 2, 0:D], tile(X1, i, j), ALU.add).then_inc(o_sum, 1)
                            dve.wait_ge(o_sum, t + 3)
                            nc.vector.tensor_tensor(tile(X1, i, j), tile(X1, i, j), BO[:, :], ALU.add).then_inc(x1_ready, 1)
                            dve.wait_ge(x1_ready, t + 1)
                            nc.vector.bn_stats(tile(ST, i, j), tile(X1, i, j)).then_inc(st_ready, 1)
                    for j in range(TPC):
                        t = TPC * i + j
                        dve.wait_ge(y_ps, TPC * (i + 1) + j + 1)
                        if j == 0:
                            dve.wait_ge(y_out, 16 * (i + 1))
                        bias = B2[:, bass.ds(i, 1), :].rearrange("p a d -> p (a d)") if experts else B2[:, 0, :]
                        nc.vector.tensor_tensor(Y[:, j, :], ps[:, YB + j % 2, 0:D], bias, ALU.add).then_inc(y_taken, 1)
                        dve.wait_ge(y_taken, t + 3)
                        if experts:
                            dve.sem_inc(y_done, 1)
                        else:
                            nc.vector.tensor_tensor(Y[:, j, :], Y[:, j, :], tile(X1, i, j), ALU.add).then_inc(y_sum, 1)
                if experts:
                    dve.wait_ge(st_ready, NT)
                    for t in range(NT):
                        nc.vector.bn_aggr(MV[:, t, :], ST[:, t, :]).then_inc(mv_ready, 1)


def build(nc, io):
    scratch = {
        "v": nc.dram_tensor("v_rows", [N, 2 * D], F32, kind="Internal").ap(),
        "qkp": nc.dram_tensor("qk_parts", [3, 2 * D, N], BF16, kind="Internal").ap(),
        "ao": nc.dram_tensor("attention_sums", [D, N], F32, kind="Internal").ap(),
        "den": nc.dram_tensor("denominators", [H, N], F32, kind="Internal").ap(),
        "inv": nc.dram_tensor("denominators_inverse", [H, N], F32, kind="Internal").ap(),
        "xs": nc.dram_tensor("rows_by_place", [2 * N, D], F32, kind="Internal").ap(),
        "ys": nc.dram_tensor("experts_rows", [N, D], F32, kind="Internal").ap(),
        "ysh": nc.dram_tensor("shared_rows", [N, D], F32, kind="Internal").ap(),
    }
    with ExitStack() as ctx:
        sb = lambda name, shape, dt=F32: ctx.enter_context(nc.sbuf_tensor(name, shape, dt))
        keep = {
            "ident": sb("ident", [P, P]), "XN": sb("XN", [P, NT, D]), "LG": sb("LG", [P, NT, E]),
            "FB": sb("FB", [P, NT]), "KEPT": sb("KEPT", [P, NT]), "SLOT": sb("SLOT", [P, NT], I32), "TAKE": sb("TAKE", [P, NT], I32),
            "MV": sb("MVX", [P, NT, 2]), "routed": ctx.enter_context(nc.semaphore("routed")),
        }
        project_tokens(nc, io, scratch, keep)
        route(nc, scratch, keep)
        attend(nc, scratch)
        networks(nc, dict(w_1=io["w1"], w_b1=io["b1"], w_2=io["w2"], w_b2=io["b2"], wo=io["wo"], bo=io["bo"]), scratch, keep, "experts")
        networks(nc, dict(w_1=io["W1"], w_b1=io["bb1"], w_2=io["W2"], w_b2=io["bb2"], ln2_g=io["ln2_g"], ln2_b=io["ln2_b"],
                          x=io["x"], out=io["out"]), scratch, keep, "dense")


_INS = {"x": "L0_attn_x", "ln1_g": "L0_attn_ln1_g", "ln1_b": "L0_attn_ln1_b", "wqkv": "L0_attn_Wqkv", "bqkv": "L0_attn_bqkv",
        "wo": "L0_attn_Wo", "bo": "L0_attn_bo", "ln2_g": "L0_attn_ln2_g", "ln2_b": "L0_attn_ln2_b", "W1": "L0_attn_W1",
        "bb1": "L0_attn_b1", "W2": "L0_attn_W2", "bb2": "L0_attn_b2", "rb": "L0_ffn_rb", "w1": "L0_ffn_w1", "b1": "L0_ffn_b1",
        "w2": "L0_ffn_w2", "b2": "L0_ffn_b2", "sw1": "L0_ffn_sw1", "sb1": "L0_ffn_sb1", "sw2": "L0_ffn_sw2", "sb2": "L0_ffn_sb2"}


def rotary_tables():
    inv = np.float32(1) / (10000.0 ** (np.arange(0, HD, 2) / HD)).astype(np.float32)
    angle = np.arange(N, dtype=np.float32)[:, None] * inv[None]
    c, s = np.cos(angle), np.sin(angle)
    return np.concatenate([c, c], 1).astype(np.float32), np.concatenate([-s, s], 1).astype(np.float32)


def kernel(**inputs):
    import concourse.bacc as bacc
    from concourse.bass_utils import run_bass_kernel_spmd

    nc = bacc.Bacc("TRN2", target_bir_lowering=False, num_devices=1)
    arrays = {short: np.ascontiguousarray(inputs[name]) for short, name in _INS.items()}
    arrays["rwT"] = np.ascontiguousarray(np.asarray(inputs["L0_ffn_rw"]).T)
    arrays["cos"], arrays["sin"] = rotary_tables()
    feed, io = {}, {}
    for short, a in arrays.items():
        feed[f"in_{short}"] = a
        io[short] = nc.dram_tensor(f"in_{short}", a.shape, mybir.dt.from_np(a.dtype), kind="ExternalInput").ap()
    io["out"] = nc.dram_tensor("out", (1, N, D), F32, kind="ExternalOutput").ap()
    build(nc, io)
    r = run_bass_kernel_spmd(nc, [feed], core_ids=[0])
    return r.results[0]["out"]
```

```python
import numpy as np
import concourse.bass as bass
from concourse import mybir
from contextlib import ExitStack

F32, BF16, I32 = mybir.dt.float32, mybir.dt.bfloat16, mybir.dt.int32
F32R = mybir.dt.float32r
ACT, ALU, AX = mybir.ActivationFunctionType, mybir.AluOpType, mybir.AxisListType

P = 128
N, D = 4096, 256
H, HD = 16, 16
F, E = 1024, 8
NT = N // P
CH = 512
NC = N // CH
TPC = CH // P
EPS = 1e-5
def root_steps(nc, dve, made, out, var, root, t):
    sem, n = made
    steps = (lambda: nc.vector.reciprocal(out, root),
             lambda: nc.vector.tensor_tensor(t, out, out, ALU.mult),
             lambda: nc.vector.tensor_tensor(t, t, var, ALU.mult),
             lambda: nc.vector.tensor_scalar(t, t, -0.5, 1.5, ALU.mult, ALU.add),
             lambda: nc.vector.tensor_tensor(out, out, t, ALU.mult))
    for step in steps:
        step().then_inc(sem, 1)
        n += 1
        dve.wait_ge(sem, n)
    return n


def product(nc, out, lhs, rhs, pick_l, pick_r, n, ready=None):
    terms = [(b, l, r) for b in range(n) for l, r in ((0, 0), (0, 1), (1, 0))]
    for at, (b, l, r) in enumerate(terms):
        if ready and (l, r) == (0, 0):
            ready(b)
        mm = nc.tensor.matmul(out, pick_l(lhs[l], b), pick_r(rhs[r], b), start=(at == 0), stop=(at == len(terms) - 1))
    return mm


def project_tokens(nc, io, scratch, keep):
    x, wqkv, rwT = io["x"], io["wqkv"], io["rwT"]
    with ExitStack() as ctx:
        sb = lambda name, shape, dt=F32: ctx.enter_context(nc.sbuf_tensor("proj_" + name, shape, dt))
        sem = lambda name: ctx.enter_context(nc.semaphore("proj_" + name))
        X = XN = keep["XN"]
        XNs = sb("XNs", [P, TPC, D])
        XNN = sb("XNN", [P, TPC, D])
        XT = sb("XT", [P, 2, CH])
        NX = sb("NX", [P, 2, CH])
        NXH, NXL = sb("NXH", [P, 2, CH], F32R), sb("NXL", [P, 2, CH], F32R)
        WH, WL = sb("WH", [P, 2, 3 * D], F32R), sb("WL", [P, 2, 3 * D], F32R)
        RW = sb("RW", [P, 2, E])
        BQ = sb("BQ", [P, 3 * D])
        RB = sb("RB", [P, E])
        G1 = sb("G1", [P, 2, 2])
        COS = sb("COS", [P, NT, HD])
        SIN = sb("SIN", [P, NT, HD])
        QB = sb("QB", [P, 2, 2 * D])
        QC = sb("QC", [P, 2, 2 * D])
        QS = sb("QS", [P, 2, 2 * D])
        QR = sb("QR", [P, TPC, 2 * D])
        VA = sb("VA", [P, 2, H, 2 * HD])
        S1H, S1L = sb("S1H", [P, 2, F], F32R), sb("S1L", [P, 2, F], F32R)
        S2H, S2L = sb("S2H", [P, F // P, D], F32R), sb("S2L", [P, F // P, D], F32R)
        XTH, XTL = sb("XTH", [P, 2, CH], F32R), sb("XTL", [P, 2, CH], F32R)
        SB1 = sb("SB1", [P, F // P])
        SB2 = sb("SB2", [P, D])
        HT = sb("HT", [P, 4, CH])
        HH, HL = sb("HH", [P, F // P, CH], F32R), sb("HL", [P, F // P, CH], F32R)
        YS = sb("YS", [P, TPC, D])
        flat = lambda w: w[:, :, :].rearrange("p a b -> p (a b)")
        pieces = lambda w, n, size=CH: [w[:, q * size:(q + 1) * size] for q in range(n)]
        WRAW = [flat(buf)[:, 0:3 * D] for buf in (QS, YS)]
        RAW = pieces(WRAW[0], 2, 3 * D // 2) + pieces(WRAW[1], 2, 3 * D // 2) + pieces(flat(QR), 4) + pieces(flat(QB), 2) + pieces(flat(QC), 2)
        HIGH = pieces(flat(WH), 4, 3 * D // 2) + pieces(flat(S1H), 4) + pieces(flat(S2H), 4)
        LOW = pieces(flat(WL), 4, 3 * D // 2) + pieces(flat(S1L), 4) + pieces(flat(S2L), 4)
        PT = sb("PT", [P, 4, 3, CH], BF16)
        RS = sb("RS", [P, 2, CH])
        ST = sb("ST", [P, NT, 6])
        MV = sb("MV", [P, NT, 2])
        SD = sb("SD", [P, NT])
        VE = sb("VE", [P, NT])
        TN = sb("TN", [P, NT])
        R1 = sb("R1", [P, NT])
        MV2 = sb("MV2", [P, NT, 2])
        SD2 = sb("SD2", [P, NT])
        R2 = sb("R2", [P, NT])
        B2 = sb("B2", [P, NT])
        ident = keep["ident"]
        LG = keep["LG"]
        ps = ctx.enter_context(nc.psum_tensor("psA", [P, 8, CH], F32))
        TB, QKB, VB, QTB = 0, 2, 4, 6
        FBK = F // P
        s1_in, s2_in, s_hi, s_lo, x_hi, x_lo, h_hi, h_lo = [sem(n) for n in ("s1_in", "s2_in", "s_hi", "s_lo", "x_hi", "x_lo", "h_hi", "h_lo")]
        nx_hi, nx_lo = sem("nx_hi"), sem("nx_lo")
        w_in, stats, std, rstd = sem("w_in"), sem("stats"), sem("std"), sem("rstd")
        xn_ready, stats2, std2, rstd2 = sem("xn_ready"), sem("stats2"), sem("std2"), sem("rstd2")
        chunk_in, xposed, xt_ready = sem("chunk_in"), sem("xposed"), sem("xt_ready")
        h_ps, h_act, y_ps, y_taken, y_out = sem("h_ps"), sem("h_act"), sem("y_ps"), sem("y_taken"), sem("y_out")
        qk_ps, qk_biased, v_ps, v_biased = sem("qk_ps"), sem("qk_biased"), sem("v_ps"), sem("v_biased")
        cosed, sined, rotated = sem("cosed"), sem("sined"), sem("rotated")
        qt_ps, part1, rest1, part2, part3 = sem("qt_ps"), sem("part1"), sem("rest1"), sem("part2"), sem("part3")
        va_ok = sem("va_ok")
        v_out, p_out = [sem("v_out0"), sem("v_out1")], [sem(f"p_out{u}") for u in range(4)]
        consts, first_part = sem("consts"), sem("first_part")
        x_in = [sem(f"x_in{c}") for c in range(NC // 2)]
        xv = x.rearrange("o (t p) d -> p (o t) d", p=P)
        with nc.Block() as block:
            @block.sync
            def _(sp):
                for c in range(NC):
                    sp.dma_start(X[:, TPC * c:TPC * (c + 1), :], xv[:, TPC * c:TPC * (c + 1), :]).then_inc(x_in[c // 2], 16)
                for dst, src in ((WRAW[0], wqkv[0:P, :]),
                                 (WRAW[1], wqkv[P:2 * P, :]),
                                 (RW[:, :, :], rwT.rearrange("(k p) n -> p k n", p=P)),
                                 (COS[:, :, :], io["cos"].rearrange("(t p) d -> p t d", p=P)),
                                 (SIN[:, :, :], io["sin"].rearrange("(t p) d -> p t d", p=P)),
                                 (BQ[:, :], io["bqkv"].rearrange("(a n) -> a n", a=1).broadcast_to([P, 3 * D])),
                                 (RB[:, :], io["rb"].rearrange("(a n) -> a n", a=1).broadcast_to([P, E])),
                                 (G1[:, 0, :], io["ln1_g"].rearrange("(k p) -> p k", p=P)),
                                 (G1[:, 1, :], io["ln1_b"].rearrange("(k p) -> p k", p=P)),
                                 (SB1[:, :], io["sb1"].rearrange("(f p) -> p f", p=P)),
                                 (SB2[:, :], io["sb2"].rearrange("(a n) -> a n", a=1).broadcast_to([P, D]))):
                    sp.dma_start(dst, src, allow_slow_non_contiguous=True).then_inc(w_in, 16)
                sp.dma_start(QR[:, :, :].rearrange("p a b -> p (a b)").rearrange("p (k f) -> p k f", k=2),
                             io["sw1"].rearrange("(k p) f -> p k f", p=P)).then_inc(s1_in, 16)
                for buf, half in ((QB, 0), (QC, 1)):
                    sp.dma_start(buf[:, :, :].rearrange("p a b -> p (a b)").rearrange("p (f d) -> p f d", d=D),
                                 io["sw2"].rearrange("(h f p) d -> h p f d", p=P, h=2)[half, :, :, :]).then_inc(s2_in, 16)
                with sp.Fori(0, NC) as c:
                    col = sp.snap(c * CH)
                    for j in range(TPC):
                        sp.wait_ge(v_biased, TPC * c + j + 1)
                        sp.dma_start(scratch["v"].rearrange("(t p) n -> p t n", p=P)[:, bass.ds(TPC * c + j, 1), :],
                                     VA[:, j % 2, :, :].rearrange("p h d -> p (h d)").rearrange("p (a n) -> p a n", a=1)).then_inc(v_out[j % 2], 16)
                    for u in range(4):
                        sp.wait_ge(part3, 4 * (c + 1) + u + 1)
                        if u == 0:
                            sp.sem_inc(first_part, 1)
                        sp.dma_start(scratch["qkp"].rearrange("s (u p) n -> u p s n", u=4)[u, :, :, bass.ds(col, CH)],
                                     PT[:, u, :, :]).then_inc(p_out[u], 16)
                    sp.wait_ge(y_taken, 4 * (c + 2))
                    sp.dma_start(scratch["ysh"].rearrange("(t p) d -> p t d", p=P)[:, bass.ds(TPC * c, TPC), :], YS[:, :, :]).then_inc(y_out, 16)
                sp.wait_ge(y_out, 16 * (NC + 1))
                for half in range(2):
                    sp.wait_ge(v_out[half], 16 * (NT // 2 + 1))
                for u in range(4):
                    sp.wait_ge(p_out[u], 16 * (NC + 1))

            @block.gpsimd
            def _(pool):
                nc.gpsimd.memset(ident[:, :], 0.0).then_inc(consts, 1)
                nc.gpsimd.memset(VA[:, :, :, :], 0.0).then_inc(consts, 1)
                pool.wait_ge(consts, 2)
                nc.gpsimd.affine_select(out=ident[:, :], in_=ident[:, :], compare_op=ALU.not_equal, fill=1.0,
                                        base=0, pattern=[[-1, P]], channel_multiplier=1).then_inc(va_ok, 1)
                nc.gpsimd.memset(VA[:, :, :, HD:HD + 1], 1.0).then_inc(va_ok, 1)
                for q in range(len(RAW)):
                    pool.wait_ge(s_hi, q + 1)
                    nc.gpsimd.tensor_tensor(LOW[q], RAW[q], HIGH[q].bitcast(F32), ALU.subtract).then_inc(s_lo, 1)
                pool.wait_ge(w_in, 16 * 11)
                with pool.Fori(0, NC) as c:
                    for j in range(TPC):
                        pool.wait_ge(qk_biased, TPC * c + j + 1)
                        pool.wait_ge(rotated, TPC * c + j + 1)
                        nc.gpsimd.tensor_tensor(
                            QC[:, j % 2, :].rearrange("p (h d) -> p h d", d=HD),
                            QB[:, j % 2, :].rearrange("p (h d) -> p h d", d=HD),
                            COS[:, bass.ds(TPC * c + j, 1), :].broadcast_to([P, 2 * H, HD]), ALU.mult).then_inc(cosed, 1)

            @block.vector
            def _(dve):
                dve.sem_inc(rotated, 2)
                dve.sem_inc(rest1, 2)
                dve.sem_inc(qt_ps, 4)
                dve.sem_inc(part3, 4)
                dve.sem_inc(y_taken, 4)
                dve.sem_inc(y_out, 16)
                dve.sem_inc(v_out[0], 16)
                dve.sem_inc(v_out[1], 16)
                for c in range(NC):
                    dve.wait_ge(x_in[c // 2], 32)
                    for t in range(TPC * c, TPC * (c + 1)):
                        nc.vector.bn_stats(ST[:, t, :], X[:, t, :]).then_inc(stats, 1)
                for t in range(NT):
                    dve.wait_ge(stats, t + 1)
                    nc.vector.bn_aggr(MV[:, t, :], ST[:, t, :]).then_inc(std, 1)
                dve.wait_ge(std, NT)
                nc.vector.tensor_scalar(VE[:, :], MV[:, :, 1], EPS, None, ALU.add).then_inc(std, 1)
                dve.wait_ge(rstd, 1)
                root_steps(nc, dve, (rstd, 1), R1[:, :], VE[:, :], SD[:, :], TN[:, :])
                for t in range(NT):
                    nc.vector.tensor_scalar(XN[:, t, :], X[:, t, :], MV[:, t, 0:1], R1[:, t:t + 1],
                                            ALU.subtract, ALU.mult).then_inc(xn_ready, 1)
                for t in range(NT):
                    dve.wait_ge(xn_ready, t + 1)
                    nc.vector.bn_stats(ST[:, t, :], XN[:, t, :]).then_inc(stats2, 1)
                for t in range(NT):
                    dve.wait_ge(stats2, t + 1)
                    nc.vector.bn_aggr(MV2[:, t, :], ST[:, t, :]).then_inc(std2, 1)
                dve.wait_ge(std2, NT)
                nc.vector.tensor_scalar(VE[:, :], MV2[:, :, 1], EPS, None, ALU.add).then_inc(std2, 1)
                dve.wait_ge(rstd2, 1)
                root_steps(nc, dve, (rstd2, 1), R2[:, :], VE[:, :], SD2[:, :], TN[:, :])
                nc.vector.scalar_tensor_tensor(B2[:, :], MV2[:, :, 0], -1.0, R2[:, :], ALU.mult, ALU.mult).then_inc(rstd2, 1)
                dve.wait_ge(w_in, 16 * 11)
                dve.wait_ge(va_ok, 2)
                dve.wait_ge(s_lo, len(RAW))

                def rotate(c, j):
                    dve.wait_ge(cosed, TPC * c + j + 1)
                    dve.wait_ge(sined, 2 * (TPC * c + j + 1))
                    nc.vector.tensor_tensor(QR[:, j, :], QC[:, j % 2, :], QS[:, j % 2, :], ALU.add).then_inc(rotated, 1)

                def cut(src, slots, hi, lo, n, count, ready, made_hi, made_lo):
                    for b in range(n + 1):
                        if b < n:
                            if ready is h_act:
                                dve.wait_ge(ready, count + b + 1)
                            nc.vector.tensor_copy(hi[:, b, :], src[:, b % slots, :]).then_inc(made_hi, 1)
                        if b > 0:
                            dve.wait_ge(made_hi, count + b)
                            nc.vector.tensor_tensor(lo[:, b - 1, :], src[:, (b - 1) % slots, :], hi[:, b - 1, :].bitcast(F32), ALU.subtract).then_inc(made_lo, 1)

                dve.wait_ge(xt_ready, 4)
                cut(NX, 2, NXH, NXL, 2, 0, xt_ready, nx_hi, nx_lo)
                with dve.Fori(0, NC) as c:
                    for j in range(TPC):
                        if j == 2:
                            dve.wait_ge(xt_ready, 4 * c + 2)
                            cut(XT, 2, XTH, XTL, 2, 2 * c, xt_ready, x_hi, x_lo)
                        dve.wait_ge(qk_ps, TPC * c + j + 1)
                        dve.wait_ge(rotated, TPC * c + j + 1)
                        nc.vector.tensor_tensor(QB[:, j % 2, :], ps[:, QKB + j % 2, :], BQ[:, 0:2 * D], ALU.add).then_inc(qk_biased, 1)
                        dve.wait_ge(v_ps, TPC * c + j + 1)
                        dve.wait_ge(v_out[j % 2], 16 * (2 * c + j // 2 + 1))
                        nc.vector.tensor_tensor(VA[:, j % 2, :, 0:HD],
                                                ps[:, VB + j % 2, 0:D].rearrange("p (h d) -> p h d", d=HD),
                                                BQ[:, 2 * D:3 * D].rearrange("p (h d) -> p h d", d=HD), ALU.add).then_inc(v_biased, 1)
                        nc.vector.tensor_tensor(LG[:, bass.ds(TPC * c + j, 1), :].rearrange("p a e -> p (a e)"),
                                                ps[:, VB + j % 2, D:D + E], RB[:, :], ALU.add).then_inc(keep["routed"], 1)
                        dve.wait_ge(qk_biased, TPC * c + j + 1)
                        qb = QB[:, j % 2, :].rearrange("p (h d) -> p h d", d=HD)
                        qs = QS[:, j % 2, :].rearrange("p (h d) -> p h d", d=HD)
                        for lo, hi in ((0, HD // 2), (HD // 2, 0)):
                            nc.vector.tensor_tensor(qs[:, :, lo:lo + HD // 2], qb[:, :, hi:hi + HD // 2],
                                                    SIN[:, bass.ds(TPC * c + j, 1), lo:lo + HD // 2].broadcast_to([P, 2 * H, HD // 2]),
                                                    ALU.mult).then_inc(sined, 1)
                        if j == 0:
                            dve.wait_ge(qt_ps, 4 * (c + 1))
                        if j > 0:
                            rotate(c, j - 1)
                    rotate(c, TPC - 1)
                    cut(HT, 4, HH, HL, FBK, FBK * c, h_act, h_hi, h_lo)
                    for u in range(5):
                        if u == 2:
                            dve.wait_ge(xt_ready, 4 * c + 8)
                            cut(NX, 2, NXH, NXL, 2, 2 * (c + 1), xt_ready, nx_hi, nx_lo)
                        if u < 4:
                            dve.wait_ge(part1, 4 * c + u + 1)
                            if u < 2:
                                dve.wait_ge(part3, 4 * (c + 1))
                            else:
                                dve.wait_ge(part3, 4 * (c + 1) + u - 1)
                            nc.vector.tensor_tensor(RS[:, u % 2, :], ps[:, QTB + u % 2, :], PT[:, u, 0, :], ALU.subtract).then_inc(rest1, 1)
                        if u > 0:
                            dve.wait_ge(part2, 4 * c + u)
                            nc.vector.tensor_tensor(PT[:, u - 1, 2, :], RS[:, (u - 1) % 2, :], PT[:, u - 1, 1, :],
                                                    ALU.subtract).then_inc(part3, 1)
                        if u > 0:
                            dve.wait_ge(y_ps, TPC * c + u)
                            if u == 1:
                                dve.wait_ge(y_out, 16 * (c + 1))
                            nc.vector.tensor_tensor(YS[:, u - 1, :], ps[:, VB + (u - 1) % 2, 0:D], SB2[:, :], ALU.add).then_inc(y_taken, 1)

            @block.scalar
            def _(act):
                def stage_first(t):
                    nc.scalar.activation(XNs[:, :, :], XN[:, bass.ds(t, TPC), :], ACT.Copy).then_inc(chunk_in, 1)

                for u in range(4):
                    act.sem_inc(p_out[u], 16)
                act.wait_ge(std, NT + 1)
                nc.scalar.activation(SD[:, :], VE[:, :], ACT.Sqrt).then_inc(rstd, 1)
                for q in range(len(RAW)):
                    if q in (0, 4, 8):
                        act.wait_ge(*{0: (w_in, 16 * 11), 4: (s1_in, 16), 8: (s2_in, 32)}[q])
                    nc.scalar.activation(HIGH[q], RAW[q], ACT.Copy).then_inc(s_hi, 1)
                act.wait_ge(xn_ready, TPC)
                stage_first(0)
                act.wait_ge(std2, NT + 1)
                nc.scalar.activation(SD2[:, :], VE[:, :], ACT.Sqrt).then_inc(rstd2, 1)
                act.wait_ge(rstd2, 7)
                act.wait_ge(w_in, 16 * 11)

                def stage_second(t):
                    for j in range(TPC):
                        nc.scalar.activation(XNN[:, j, :], XN[:, bass.ds(t + j, 1), :].rearrange("p a n -> p (a n)"),
                                             ACT.Identity, scale=R2[:, bass.ds(t + j, 1)], bias=B2[:, bass.ds(t + j, 1)]).then_inc(chunk_in, 1)

                def take(c):
                    for k in range(2):
                        act.wait_ge(xposed, 4 * c + k + 1)
                        nc.scalar.activation(XT[:, k, :], ps[:, TB + k, :], ACT.Copy).then_inc(xt_ready, 1)
                    for k in range(2):
                        act.wait_ge(xposed, 4 * c + k + 3)
                        nc.scalar.activation(NX[:, k, :], ps[:, QKB + k, :], ACT.Identity, scale=G1[:, 0, k:k + 1],
                                             bias=G1[:, 1, k:k + 1]).then_inc(xt_ready, 1)

                stage_second(0)
                take(0)
                with act.Fori(0, NC) as c:
                    stage_first((c + 1) % NC * TPC)
                    stage_second((c + 1) % NC * TPC)
                    for f in range(FBK):
                        act.wait_ge(h_ps, FBK * c + f + 1)
                        if f >= 4:
                            act.wait_ge(h_lo, FBK * c + f - 3)
                        nc.scalar.activation(HT[:, f % 4, :], ps[:, TB + f % 4, :], ACT.Gelu, bias=SB1[:, f:f + 1]).then_inc(h_act, 1)
                    take(c + 1)
                    for u in range(5):
                        if u < 4:
                            act.wait_ge(qt_ps, 4 * (c + 1) + u + 1)
                            act.wait_ge(p_out[u], 16 * (c + 1))
                            nc.scalar.activation(PT[:, u, 0, :], ps[:, QTB + u % 2, :], ACT.Copy).then_inc(part1, 1)
                        if u > 0:
                            act.wait_ge(rest1, 4 * c + u + 2)
                            nc.scalar.activation(PT[:, u - 1, 1, :], RS[:, (u - 1) % 2, :], ACT.Copy).then_inc(part2, 1)

            @block.tensor
            def _(pe):
                def transposes(c, hidden):
                    for v, (src, need) in enumerate(((XNs, 1), (XNN, 5))):
                        pe.wait_ge(chunk_in, 5 * c + need)
                        for k in range(2):
                            if hidden is not None:
                                pe.wait_ge(h_act, hidden - 3 + 2 * v + k)
                            for j in range(TPC):
                                mm = nc.tensor.transpose(ps[:, TB + 2 * v + k, j * P:(j + 1) * P], src[:, j, k * P:(k + 1) * P], ident[:, :])
                            mm.then_inc(xposed, 1)

                pe.sem_inc(keep["routed"], TPC)
                pe.wait_ge(va_ok, 1)
                pe.wait_ge(w_in, 16 * 11)
                transposes(0, None)
                pe.wait_ge(s_lo, len(RAW))
                with pe.Fori(0, NC) as c:
                    pe.wait_ge(xt_ready, 4 * c + 4)
                    pe.wait_ge(nx_lo, 2 * (c + 1))
                    for j in range(TPC):
                        tok = slice(j * P, (j + 1) * P)
                        if j >= 2:
                            pe.wait_ge(qk_biased, TPC * c + j - 1)
                        product(nc, ps[:, QKB + j % 2, :], (NXH, NXL), (WH, WL), lambda x, k: x[:, k, tok],
                                lambda w, k: w[:, k, 0:2 * D], 2).then_inc(qk_ps, 1)
                        if j == 0:
                            pe.wait_ge(y_taken, TPC * (c + 1))
                        if j >= 2:
                            pe.wait_ge(keep["routed"], TPC * (c + 1) + j - 1)
                        product(nc, ps[:, VB + j % 2, 0:D], (NXH, NXL), (WH, WL), lambda x, k: x[:, k, tok],
                                lambda w, k: w[:, k, 2 * D:3 * D], 2)
                        for k in range(2):
                            mm = nc.tensor.matmul(ps[:, VB + j % 2, D:D + E], XT[:, k, tok], RW[:, k, :], start=(k == 0), stop=(k == 1))
                        mm.then_inc(v_ps, 1)
                    for f in range(FBK):
                        if f == 0:
                            pe.wait_ge(x_lo, 2 * (c + 1))
                        if f == 2:
                            pe.wait_ge(qk_biased, TPC * (c + 1))
                        if f >= 4:
                            pe.wait_ge(h_act, FBK * c + f - 3)
                        product(nc, ps[:, TB + f % 4, :], (S1H, S1L), (XTH, XTL), lambda w, k: w[:, k, f * P:(f + 1) * P],
                                lambda x, k: x[:, k, :], 2).then_inc(h_ps, 1)
                    transposes(c + 1, FBK * (c + 1))
                    for j in range(TPC):
                        pe.wait_ge(rest1, 4 * c + j + 1)
                        for i in range(TPC):
                            if j == 0:
                                pe.wait_ge(rotated, TPC * c + i + 3)
                            mm = nc.tensor.transpose(ps[:, QTB + j % 2, i * P:(i + 1) * P], QR[:, i, j * P:(j + 1) * P], ident[:, :])
                        mm.then_inc(qt_ps, 1)
                        if j == 0:
                            pe.wait_ge(keep["routed"], TPC * (c + 2))
                        if j >= 2:
                            pe.wait_ge(y_taken, TPC * (c + 1) + j - 1)
                        product(nc, ps[:, VB + j % 2, 0:D], (HH, HL), (S2H, S2L), lambda h, f: h[:, f, j * P:(j + 1) * P],
                                lambda w, f: w[:, f, :], FBK,
                                (lambda f: pe.wait_ge(h_lo, FBK * c + f + 1)) if j == 0 else None).then_inc(y_ps, 1)
def routing(nc, ctx, scratch, keep, ps):
    CAP = N // E
    sb = lambda name, shape, dt=F32: ctx.enter_context(nc.sbuf_tensor("route_" + name, shape, dt))
    sem = lambda name: ctx.enter_context(nc.semaphore("route_" + name))
    LG, FB, KEPT, SLOT, TAKE = keep["LG"], keep["FB"], keep["KEPT"], keep["SLOT"], keep["TAKE"]
    W8 = sb("W8", [P, E])
    ONE = sb("ONE", [P, NT])
    TOK = sb("TOK", [P, NT])
    TOKI = sb("TOKI", [P, NT], I32)
    tri = sb("tri", [P, P], BF16)
    ones = sb("ones", [P, P], BF16)
    ZR = sb("ZR", [P, D])
    OH = [sb(f"OH{i}", [P, NT, E]) for i in range(2)]
    OHB = sb("OHB", [P, 2, NT, E], BF16)
    A = sb("A", [P, NT, E])
    B = sb("B", [P, NT, E])
    INC = sb("INC", [P, NT, E])
    POS = sb("POS", [P, NT, E])
    M = sb("M", [P, NT])
    R = [sb(f"R{i}", [P, NT]) for i in range(2)]
    PT1 = sb("PT1", [P, NT])
    PT2 = sb("PT2", [P, NT])
    USED = sb("USED", [P, E])
    OVF = sb("OVF", [P, NT])
    T2 = sb("T2", [P, NT])
    S1 = sb("S1", [P, NT])
    S2 = sb("S2", [P, NT])
    consts, cum, link, ohb, slots, sent = sem("r_consts"), sem("r_cum"), sem("r_link"), sem("r_ohb"), sem("r_slots"), sem("r_sent")
    zeroed = sem("r_zeroed")
    over_t = lambda ap: ap.rearrange("p (a e) -> p a e", a=1).broadcast_to([P, NT, E])
    over_e = lambda ap: ap.rearrange("p (t a) -> p t a", a=1).broadcast_to([P, NT, E])
    def zero_places(sp):
        sp.wait_ge(consts, 3)
        for t in range(E * CAP // P):
            sp.dma_start(scratch["xs"][t * P:(t + 1) * P, :], ZR[:, :]).then_inc(zeroed, 16)

    def constants(pool):
        nc.gpsimd.memset(tri[:, :], 1.0).then_inc(consts, 1)
        nc.gpsimd.memset(ones[:, :], 1.0).then_inc(consts, 1)
        nc.gpsimd.memset(ZR[:, :], 0.0).then_inc(consts, 1)
        pool.wait_ge(consts, 3)
        nc.gpsimd.affine_select(out=tri[:, :], in_=tri[:, :], compare_op=ALU.is_gt, fill=0.0, base=0,
                                pattern=[[1, P]], channel_multiplier=-1).then_inc(consts, 1)
        nc.gpsimd.iota(TOKI[:, :], pattern=[[P, NT]], base=0, channel_multiplier=1).then_inc(consts, 1)

    def send_rows(pool):
        pool.wait_ge(slots, 1)
        pool.wait_ge(zeroed, 16 * E * CAP // P)
        for t in range(NT):
            nc.gpsimd.indirect_dma_start(out=scratch["xs"], out_offset=bass.IndirectOffsetOnAxis(ap=SLOT[:, t:t + 1], axis=0),
                                         in_=keep["XN"][:, t, :], in_offset=None).then_inc(sent, 16)
        pool.wait_ge(sent, 16 * NT)

    def count(pe):
        for i in range(2):
            pe.wait_ge(ohb, i + 1)
            pe.wait_ge(consts, 5)
            rhs = OHB[:, i, :, :].rearrange("p t e -> p (t e)")
            nc.tensor.matmul(ps[:, 2 * i, 0:NT * E], tri[:, :], rhs, start=True, stop=True).then_inc(cum, 1)
            nc.tensor.matmul(ps[:, 2 * i + 1, 0:NT * E], ones[:, :], rhs, start=True, stop=True).then_inc(cum, 1)

    def choose(dve):
        v = nc.vector
        made = [0]

        def link_up(ins):
            made[0] += 1
            ins.then_inc(link, 1)
            dve.wait_ge(link, made[0])

        def first_of(logits, i):
            link_up(v.tensor_reduce(M[:, :], logits[:, :, :], AX.X, ALU.max))
            link_up(v.tensor_tensor(A[:, :, :], logits[:, :, :], over_e(M[:, :]), ALU.is_equal))
            link_up(v.tensor_tensor(A[:, :, :], A[:, :, :], over_t(W8[:, :]), ALU.mult))
            link_up(v.tensor_reduce(R[i][:, :], A[:, :, :], AX.X, ALU.max))
            link_up(v.tensor_tensor(OH[i][:, :, :], A[:, :, :], over_e(R[i][:, :]), ALU.is_equal))

        def places(i, out):
            psv = lambda b: ps[:, b, 0:NT * E].rearrange("p (t e) -> p t e", e=E)
            dve.wait_ge(cum, 2 * (i + 1))
            link_up(v.tensor_copy(B[:, :, :], psv(2 * i + 1)))
            for e in range(E):
                link_up(v.tensor_tensor_scan(INC[:, :, e], ONE[:, :], B[:, :, e], 0.0, ALU.mult, ALU.add))
            link_up(v.tensor_tensor(B[:, :, :], INC[:, :, :], B[:, :, :], ALU.subtract))
            link_up(v.tensor_tensor(POS[:, :, :], psv(2 * i), B[:, :, :], ALU.add))

        for e in range(E):
            link_up(v.memset(W8[:, e:e + 1], float(E - e)))
        link_up(v.memset(ONE[:, :], 1.0))
        first_of(LG, 0)
        v.tensor_copy(OHB[:, 0, :, :], OH[0][:, :, :]).then_inc(ohb, 1)
        link_up(v.scalar_tensor_tensor(B[:, :, :], OH[0][:, :, :], BIG, LG[:, :, :], ALU.mult, ALU.add))
        first_of(B, 1)
        places(0, POS)
        link_up(v.tensor_tensor(A[:, :, :], OH[0][:, :, :], POS[:, :, :], ALU.mult))
        link_up(v.tensor_reduce(PT1[:, :], A[:, :, :], AX.X, ALU.add))
        link_up(v.tensor_scalar(KEPT[:, :], PT1[:, :], float(CAP), None, ALU.is_lt))
        link_up(v.tensor_scalar(USED[:, :], INC[:, NT - 1, :], float(CAP), None, ALU.min))
        link_up(v.tensor_scalar(OVF[:, :], KEPT[:, :], -1.0, 1.0, ALU.mult, ALU.add))
        v.tensor_tensor(OHB[:, 1, :, :], OH[1][:, :, :], over_e(OVF[:, :]), ALU.mult).then_inc(ohb, 1)
        places(1, POS)
        link_up(v.tensor_tensor(A[:, :, :], POS[:, :, :], over_t(USED[:, :]), ALU.add))
        link_up(v.tensor_tensor(A[:, :, :], A[:, :, :], OH[1][:, :, :], ALU.mult))
        link_up(v.tensor_reduce(PT2[:, :], A[:, :, :], AX.X, ALU.add))
        link_up(v.tensor_scalar(T2[:, :], PT2[:, :], float(CAP), None, ALU.is_lt))
        link_up(v.tensor_tensor(T2[:, :], T2[:, :], OVF[:, :], ALU.mult))
        link_up(v.tensor_tensor(FB[:, :], OVF[:, :], T2[:, :], ALU.subtract))
        for r, pos, gate, out in ((R[0], PT1, KEPT, S1), (R[1], PT2, T2, S2)):
            link_up(v.tensor_scalar(out[:, :], r[:, :], -float(CAP), float(N), ALU.mult, ALU.add))
            link_up(v.tensor_tensor(out[:, :], out[:, :], pos[:, :], ALU.add))
            link_up(v.tensor_tensor(out[:, :], out[:, :], gate[:, :], ALU.mult))
        dve.wait_ge(consts, 5)
        link_up(v.tensor_copy(TOK[:, :], TOKI[:, :]))
        link_up(v.tensor_scalar(TOK[:, :], TOK[:, :], float(N), None, ALU.add))
        link_up(v.tensor_tensor(TOK[:, :], TOK[:, :], FB[:, :], ALU.mult))
        link_up(v.tensor_tensor(S1[:, :], S1[:, :], S2[:, :], ALU.add))
        link_up(v.tensor_tensor(S1[:, :], S1[:, :], TOK[:, :], ALU.add))
        link_up(v.tensor_copy(SLOT[:, :], S1[:, :]))
        link_up(v.tensor_scalar(S1[:, :], S1[:, :], float(N - 1), None, ALU.min))
        link_up(v.tensor_copy(TAKE[:, :], S1[:, :]))
        link_up(v.tensor_scalar(KEPT[:, :], FB[:, :], -1.0, 1.0, ALU.mult, ALU.add))
        dve.sem_inc(slots, 1)

    return zero_places, constants, send_rows, count, choose



HG = 4
NG = H // HG
PAIRS = ((0, 0), (0, 1), (1, 0), (1, 1), (0, 2), (2, 0))
MROW = HD * len(PAIRS)
KROWS = MROW + 2 * HG
BIG = -1e30


def key_blocks(c):
    full = [(kb, 0) for kb in range(TPC * c + 1)]
    short = [(TPC * c + r, r) for r in reversed(range(1, TPC))]
    order = []
    for at, unit in enumerate(full):
        order.append(unit)
        if at < len(short) and c > 0:
            order.append(short[at])
    return order if c > 0 else full + short


AHEAD = 2
PACE = 4.5


def max_pass_pace(steps, units, jobs, j_base):
    LS = len(steps)
    cost = [(TPC if kc < steps[m % LS][1] else j + 1) / TPC for m in range(LS + AHEAD) for j, _, kc in jobs[m % LS]]
    end = lambda m: j_base[m] if m <= LS else j_base[LS] + j_base[m - LS]
    at, room, upto = end(AHEAD), 0.0, []
    for i in range(LS):
        upto.append([])
        for k, (_, r) in enumerate(units[i]):
            room = min(room, 1.0) + PACE * (TPC - r) / TPC
            while at < end(i + 1 + AHEAD) and room >= cost[at]:
                room -= cost[at]
                at += 1
            if k >= len(units[i]) - 3:
                at = max(at, end(i + 2))
            if (i, k) == (LS - 1, len(units[i]) - 1):
                at = end(LS + AHEAD)
            upto[i].append(at)
    return upto


def attend(nc, io, scratch, keep):
    qk = scratch["qkp"].rearrange("s (w g h d) n -> s w g d h n", w=2, g=NG, h=HG)
    vv = scratch["v"].rearrange("(t p) (g n) -> g p t n", p=P, g=NG)
    ao = scratch["ao"].rearrange("(g h d) n -> g h d n", g=NG, h=HG)
    den = scratch["den"].rearrange("(g h) n -> g h n", g=NG)
    steps = [(0, c) for c in range(NC)] + [(1, c) for c in reversed(range(NC))]
    LS = len(steps)
    units = [key_blocks(c) for _, c in steps]
    jobs = [[(j, h, kc) for kc in range(c + 1) for j in range(TPC) for h in range(HG)] for _, c in steps]
    S_PER = sum(2 * len(u) + 1 for u in units)
    J_PER = sum(len(j) for j in jobs)
    U_PER = sum(len(u) for u in units)
    s_base = [1 + sum(2 * len(u) + 1 for u in units[:i]) for i in range(LS + 1)]
    u_base = [sum(len(u) for u in units[:i]) for i in range(LS + 1)]
    j_base = [sum(len(j) for j in jobs[:i]) for i in range(LS + 1)]
    ahead = [(m, n) for m in range(LS + AHEAD) for n in range(len(jobs[m % LS]))]
    upto = max_pass_pace(steps, units, jobs, j_base)
    RING = 3
    rows_at = lambda i: len(units[i]) - 2
    s_of = lambda i, k, pair: s_base[i] + 2 * k + pair + (1 if k > rows_at(i) else 0)
    s_rows = lambda i: s_base[i] + 2 * (rows_at(i) + 1)

    with ExitStack() as ctx:
        sb = lambda name, shape, dt=F32: ctx.enter_context(nc.sbuf_tensor("attn_" + name, shape, dt))
        sem = lambda name: ctx.enter_context(nc.semaphore("attn_" + name))
        KS = [sb(f"KS{w}", [P, HG, N], BF16) for w in range(2)]
        V = [sb(f"V{w}", [P, NT, HG * 2 * HD]) for w in range(2)]
        QS = sb("QS", [P, 4, HG, CH], BF16)
        PB = sb("PB", [P, RING, HG, CH])
        MX = sb("MX", [P, 4, TPC * HG, NC])
        NM = sb("NM", [P, 4, TPC * HG])
        MH = sb("MH", [P, 4, TPC, 2, HG], BF16)
        OU = sb("OU", [P, 2, CH])
        idb = sb("idb", [P, P], BF16)
        mask_qk = sb("mask_qk", [P, P], BF16)
        mask_kq = sb("mask_kq", [P, P], BF16)
        ps = ctx.enter_context(nc.psum_tensor("psB", [P, 8, CH], F32))
        PV, MB = 4, 5
        q_in = [sem(f"q_in{s}") for s in range(4)]
        kv_in = [[sem(f"kv{w}_in{c}") for c in range(NC)] for w in range(2)]
        rows_set, early, consts, masks, kones, stepped = sem("rows_set"), sem("early"), sem("consts"), sem("masks"), sem("kones"), sem("stepped")
        scored, expd, pv_done, ou_ready = sem("scored"), sem("expd"), sem("pv_done"), sem("ou_ready")
        maxed, reduced, negmax, mparts = sem("maxed"), sem("reduced"), sem("negmax"), sem("mparts")
        ou_out = [sem("ou_out0"), sem("ou_out1")]

        zero_places, constants, send_rows, count, choose = routing(nc, ctx, scratch, keep, ps)

        with nc.Block() as block:
            @block.sync
            def _(sp):
                def load_q(group, i):
                    c = steps[i % LS][1]
                    for r, (a, _) in enumerate(PAIRS):
                        sp.dma_start(QS[HD * r:HD * (r + 1), i % 4, :, :],
                                     qk[a, 0, bass.ds(group, 1), :, :, c * CH:(c + 1) * CH].rearrange("g d h n -> (g d) h n")).then_inc(q_in[i % 4], 16)

                def load_k(w, group, c):
                    for r, (_, b) in enumerate(PAIRS):
                        sp.dma_start(KS[w][HD * r:HD * (r + 1), :, c * CH:(c + 1) * CH],
                                     qk[b, 1, bass.ds(group, 1), :, :, c * CH:(c + 1) * CH].rearrange("g d h n -> (g d) h n")).then_inc(kv_in[w][c], 16)

                def load_v(w, group, c):
                    sp.dma_start(V[w][:, TPC * c:TPC * (c + 1), :],
                                 vv[bass.ds(group, 1), :, TPC * c:TPC * (c + 1), :].rearrange("g p t n -> (g p) t n")).then_inc(kv_in[w][c], 16)

                def store_sums(first, i):
                    w, c = steps[i]
                    for h in range(HG):
                        sp.dma_start(ao[bass.ds(first + w, 1), h, :, c * CH:(c + 1) * CH].rearrange("g r n -> (g r) n"),
                                     OU[32 * h:32 * h + HD, i % 2, :]).then_inc(ou_out[i % 2], 16)
                        sp.dma_start(den[bass.ds(first + w, 1), h:h + 1, c * CH:(c + 1) * CH].rearrange("g r n -> (g r) n"),
                                     OU[32 * h + HD:32 * h + HD + 1, i % 2, :]).then_inc(ou_out[i % 2], 16)

                for c in range(NC):
                    if c <= AHEAD:
                        load_q(0, c)
                    load_k(0, 0, c)
                    load_v(0, 0, c)
                zero_places(sp)
                sp.dma_start(keep["W1"][:, :, :], io["w1"][0, :, :].rearrange("(k p) f -> p k f", p=P)).then_inc(early, 16)
                sp.dma_start(keep["W2"][:, :, :], io["w2"][0, :, :].rearrange("(f p) d -> p f d", p=P)).then_inc(early, 16)
                with sp.Fori(0, NG // 2) as g:
                    here = sp.snap(g * 2)
                    after = sp.snap((g + 1) % (NG // 2) * 2)
                    for i in range(LS):
                        sp.wait_ge(scored, g * S_PER + s_base[i])
                        sp.sem_inc(stepped, 1)
                        load_q(here + steps[i + 1 + AHEAD][0] if i + 1 + AHEAD < LS else after, i + 1 + AHEAD)
                        if i == 0:
                            sp.wait_ge(pv_done, g * U_PER + RING)
                            sp.sem_inc(stepped, 1)
                            for c in range(NC):
                                load_k(1, here + 1, c)
                                load_v(1, here + 1, c)
                        if i == NC + 1:
                            sp.wait_ge(pv_done, g * U_PER + RING + u_base[NC])
                            sp.sem_inc(stepped, 1)
                            for c in range(NC):
                                load_k(0, after, c)
                                load_v(0, after, c)
                        if i > 0:
                            sp.wait_ge(ou_ready, g * LS + i + 1)
                            sp.sem_inc(stepped, 1)
                            store_sums(here, i - 1)
                    sp.wait_ge(ou_ready, g * LS + LS + 1)
                    sp.sem_inc(stepped, 1)
                    store_sums(here, LS - 1)
                sp.wait_ge(early, 32)
                for half in range(2):
                    sp.wait_ge(ou_out[half], 32 * HG * (NG * NC // 2 + 1))
                for s in range(4):
                    sp.wait_ge(q_in[s], 96 * (LS // 4 * (NG // 2) + (1 if s <= AHEAD else 0)))
                for c in range(NC):
                    for w in range(2):
                        sp.wait_ge(kv_in[w][c], 112 * (NG // 2 + 1 - w))

            @block.gpsimd
            def _(pool):
                constants(pool)
                nc.gpsimd.memset(idb[:, :], 0.0).then_inc(consts, 1)
                nc.gpsimd.memset(mask_qk[:, :], 0.0).then_inc(consts, 1)
                nc.gpsimd.memset(mask_kq[:, :], 0.0).then_inc(consts, 1)
                pool.wait_ge(consts, 3)
                nc.gpsimd.affine_select(out=idb[:, :], in_=idb[:, :], compare_op=ALU.not_equal, fill=1.0, base=0,
                                        pattern=[[-1, P]], channel_multiplier=1).then_inc(masks, 1)
                nc.gpsimd.affine_select(out=mask_qk[:, :], in_=mask_qk[:, :], compare_op=ALU.is_ge, fill=BIG, base=0,
                                        pattern=[[-1, P]], channel_multiplier=1).then_inc(masks, 1)
                nc.gpsimd.affine_select(out=mask_kq[:, :], in_=mask_kq[:, :], compare_op=ALU.is_ge, fill=BIG, base=0,
                                        pattern=[[1, P]], channel_multiplier=-1).then_inc(masks, 1)
                pool.wait_ge(masks, 3)
                made = 3
                for w in range(2):
                    for c in range(NC):
                        part = KS[w][MROW:KROWS, :, c * CH:(c + 1) * CH]
                        nc.gpsimd.memset(part, 0.0).then_inc(consts, 1)
                        for first in range(2):
                            made += 1
                            pool.wait_ge(consts, made)
                            nc.gpsimd.affine_select(out=part, in_=part, compare_op=ALU.not_equal, fill=1.0, base=-HG * first,
                                                    pattern=[[-1, HG], [0, CH]], channel_multiplier=1).then_inc(consts, 1)
                        made += 1
                        pool.wait_ge(consts, made)
                        pool.sem_inc(kones, 1)
                send_rows(pool)

            @block.tensor
            def _(pe):
                def max_job(reads, i, off, job, used, q_need):
                    j, h, kc = job
                    w, c = steps[i % LS]
                    width = CH if kc < c else P * (j + 1)
                    if h == 0 and j == 0 and kc == 0:
                        pe.wait_ge(q_in[i % 4], q_need)
                    if h == 0 and j == 0:
                        pe.wait_ge(kv_in[w][kc], 112 * (reads + 1))
                    if used is not None:
                        pe.wait_ge(reduced, used)
                    bank = MB + off % 3
                    mm = nc.tensor.matmul(ps[:, bank, 0:width], QS[0:MROW, i % 4, h, j * P:(j + 1) * P],
                                          KS[w][0:MROW, h, kc * CH:kc * CH + width], start=True, stop=(kc < c))
                    if kc == c:
                        mm = nc.tensor.matmul(ps[:, bank, width - P:width], idb[:, :], mask_qk[:, :], start=False, stop=True)
                    mm.then_inc(maxed, 1)

                def max_rows(i, s, used, need):
                    pe.wait_ge(mparts, need)
                    if used is not None:
                        pe.wait_ge(expd, used)
                    for j in range(TPC):
                        mm = nc.tensor.matmul(ps[MROW:KROWS, 2 * (s % 2), j * P:(j + 1) * P],
                                              MH[:, i % 4, j, :, :].rearrange("p s h -> p (s h)"), idb[:, :], start=True, stop=True)
                    mm.then_inc(scored, 1)

                def scores(g, i, k, pair):
                    w, c = steps[i]
                    kb, r = units[i][k]
                    s = s_of(i, k, pair)
                    if s > 1:
                        pe.wait_ge(expd, g * S_PER + s - 1)
                    if k == 0 and pair == 0:
                        pe.wait_ge(rows_set, g * LS + i + 1)
                    if k == 0 and pair == 1:
                        pe.wait_ge(expd, g * S_PER + (s_rows(i - 1) if i > 0 else 0) + 1)
                    if pair == 0 and kb // TPC not in [b // TPC for b, _ in units[i][:k]]:
                        pe.wait_ge(kones, NC * w + kb // TPC + 1)
                    for b in range(2):
                        h = 2 * pair + b
                        bank = 2 * (s % 2) + b
                        mm = nc.tensor.matmul(ps[:, bank, r * P:CH], KS[w][0:KROWS, h, kb * P:(kb + 1) * P],
                                              QS[0:KROWS, i % 4, h, r * P:CH], start=True, stop=(kb < TPC * c))
                        if kb >= TPC * c:
                            mm = nc.tensor.matmul(ps[:, bank, r * P:(r + 1) * P], idb[:, :], mask_kq[:, :], start=False, stop=True)
                    mm.then_inc(scored, 1)

                def weigh(g, i, k):
                    w = steps[i][0]
                    kb, r = units[i][k]
                    pe.wait_ge(expd, g * S_PER + s_of(i, k, 1) + 1)
                    if k == 0:
                        pe.wait_ge(ou_ready, g * LS + i + 1)
                    u = u_base[i] + k
                    for h in range(HG):
                        mm = nc.tensor.matmul(ps[32 * h:32 * (h + 1), PV, r * P:CH], V[w][:, kb, 32 * h:32 * (h + 1)],
                                              PB[:, u % RING, h, r * P:CH], start=(k == 0), stop=(k == len(units[i]) - 1))
                    mm.then_inc(pv_done, 1)

                pe.sem_inc(ou_ready, 1)
                pe.sem_inc(pv_done, RING)
                count(pe)
                pe.wait_ge(masks, 3)
                for m in range(AHEAD):
                    for n, job in enumerate(jobs[m], j_base[m]):
                        max_job(0, m, n, job, n - 2 if n > 2 else None, 96)
                max_rows(0, 0, None, 1)
                with pe.Fori(0, NG // 2) as g:
                    behind = None
                    at = j_base[AHEAD]
                    for i in range(LS):
                        def ask(count):
                            nonlocal at
                            while at < count:
                                m, n = ahead[at]
                                max_job(g + m // LS, m, at, jobs[m % LS][n], g * J_PER + at - 2, 96 * (LS // 4 * g + m // 4 + 1))
                                at += 1

                        for k in range(len(units[i])):
                            new = upto[i][k] - at
                            scores(g, i, k, 0)
                            ask(at + new // 4)
                            scores(g, i, k, 1)
                            ask(upto[i][k] - new // 2)
                            if k == rows_at(i):
                                max_rows(i + 1, s_rows(i), g * S_PER + s_rows(i) - 1, g * LS + i + 2)
                            if behind is not None:
                                weigh(g, *behind)
                            behind = (i, k)
                            ask(upto[i][k])
                    weigh(g, *behind)

            @block.scalar
            def _(act):
                def rows(i, s, need):
                    act.wait_ge(scored, need)
                    for pair in range(2):
                        nc.scalar.activation(QS[MROW:KROWS, i % 4, 2 * pair:2 * pair + 2, :],
                                             ps[MROW:KROWS, 2 * (s % 2):2 * (s % 2) + 1, :].broadcast_to([2 * HG, 2, CH]),
                                             ACT.Copy).then_inc((rows_set, expd)[pair], 1)

                def sums(g, i):
                    act.wait_ge(pv_done, RING + g * U_PER + u_base[i + 1])
                    act.wait_ge(ou_out[i % 2], 32 * HG * (g * (LS // 2) + i // 2 + 1))
                    nc.scalar.activation(OU[:, i % 2, :], ps[:, PV, :], ACT.Copy).then_inc(ou_ready, 1)

                act.sem_inc(ou_out[0], 32 * HG)
                act.sem_inc(ou_out[1], 32 * HG)
                act.wait_ge(q_in[0], 96)
                rows(0, 0, 1)
                with act.Fori(0, NG // 2) as g:
                    for i in range(LS):
                        for k in range(len(units[i])):
                            kb, r = units[i][k]
                            u = u_base[i] + k
                            for pair in range(2):
                                s = s_of(i, k, pair)
                                act.wait_ge(scored, g * S_PER + s + 1)
                                if pair == 0:
                                    act.wait_ge(pv_done, g * U_PER + u + 1)
                                nc.scalar.activation(PB[:, u % RING, 2 * pair:2 * pair + 2, r * P:CH],
                                                     ps[:, 2 * (s % 2):2 * (s % 2) + 2, r * P:CH], ACT.Exp, scale=HD ** -0.5).then_inc(expd, 1)
                            if k == rows_at(i):
                                rows(i + 1, s_rows(i), g * S_PER + s_rows(i) + 1)
                            if k == 0 and i > 0:
                                sums(g, i - 1)
                    sums(g, LS - 1)

            @block.vector
            def _(dve):
                def reduce_job(m, off, need, job):
                    j, h, kc = job
                    w = CH if kc < steps[m % LS][1] else P * (j + 1)
                    dve.wait_ge(maxed, need)
                    nc.vector.tensor_reduce(MX[:, m % 4, HG * j + h, kc:kc + 1], ps[:, MB + off % 3, 0:w], AX.X, ALU.max).then_inc(reduced, 1)

                def finish(m, all_jobs, before):
                    dve.wait_ge(reduced, all_jobs)
                    if not isinstance(before, int) or before > 0:
                        dve.wait_ge(mparts, before)
                    slot = m % 4
                    nc.vector.tensor_reduce(NM[:, slot, :], MX[:, slot, :, 0:steps[m % LS][1] + 1], AX.X, ALU.max, negate=True).then_inc(negmax, 1)
                    dve.wait_ge(negmax, 2 * before + 1)
                    nm = NM[:, slot, :].rearrange("p (j h) -> p j h", h=HG)
                    nc.vector.tensor_copy(MH[:, slot, :, 0, :], nm).then_inc(negmax, 1)
                    dve.wait_ge(negmax, 2 * before + 2)
                    nc.vector.tensor_tensor(MH[:, slot, :, 1, :], nm, MH[:, slot, :, 0, :], ALU.subtract).then_inc(mparts, 1)

                choose(dve)
                for m in range(AHEAD):
                    for n, job in enumerate(jobs[m], j_base[m]):
                        reduce_job(m, n, n + 1, job)
                    finish(m, j_base[m + 1], m)
                with dve.Fori(0, NG // 2) as g:
                    for m in range(AHEAD, LS + AHEAD):
                        first = j_base[m] if m < LS else J_PER + j_base[m - LS]
                        dve.wait_ge(negmax, 2 * (g * LS + m))
                        for off, job in enumerate(jobs[m % LS], first):
                            reduce_job(m, off, g * J_PER + off + 1, job)
                        finish(m, g * J_PER + first + len(jobs[m % LS]), g * LS + m)
def networks(nc, io, scratch, keep, kind):
    experts, dense = kind == "experts", kind == "dense"
    FBK = F // P
    KX = D // P
    QW = 4
    with ExitStack() as ctx:
        sb = lambda name, shape, dt=F32: ctx.enter_context(nc.sbuf_tensor(f"{name}_{kind}", shape, dt))
        sem = lambda name: ctx.enter_context(nc.semaphore(f"{kind}_{name}"))
        EB = E if experts else 1
        XI = sb("XI", [P, TPC, D])
        XF = sb("XF", [P, KX, CH])
        XH, XL = sb("XH", [P, KX, CH], F32R), sb("XL", [P, KX, CH], F32R)
        W1, W2, W1H, W1L, W2H, W2L = [keep[name] for name in ("W1", "W2", "W1H", "W1L", "W2H", "W2L")]
        B1 = sb("B1", [P, EB, FBK])
        B2 = sb("B2", [P, EB, D])
        HT = sb("HT", [P, FBK, CH])
        HH, HL = sb("HH", [P, FBK, CH], F32R), sb("HL", [P, FBK, CH], F32R)
        Y = sb("Y", [P, TPC, D])
        X1, MV, ident = keep["XN"], keep["MV"], keep["ident"]
        ps = ctx.enter_context(nc.psum_tensor(f"ps_{kind}", [P, 8, CH], F32))
        TB, YB, OB = 0, 4, (6, 7, 2, 3)
        b_in, x_in, w2_hi, w2_lo = sem("b_in"), sem("x_in"), sem("w2_hi"), sem("w2_lo")
        xposed, x_sb, x_hi, x_lo = sem("xposed"), sem("x_sb"), sem("x_hi"), sem("x_lo")
        h_ps, h_act, h_hi, h_lo = sem("h_ps"), sem("h_act"), sem("h_hi"), sem("h_lo")
        y_ps, y_taken, y_done, y_out = sem("y_ps"), sem("y_taken"), sem("y_done"), sem("y_out")
        stepped = sem("stepped")
        if experts:
            w1_in, w1_hi, w1_lo, w2_in = sem("w1_in"), sem("w1_hi"), sem("w1_lo"), sem("w2_in")
            AO, DN, AT = sb("AO", [P, 2, CH]), sb("DN", [P, 2, CH]), sb("AT", [P, 2, CH])
            RC = sb("RC", [P, CH])
            WO, BO = sb("WO", [P, 2, D]), sb("BO", [P, D])
            ST = sb("ST", [P, NT, 6])
            wo_in, den_in, inv, inv_out, ao_in = sem("wo_in"), sem("den_in"), sem("inv"), sem("inv_out"), sem("ao_in")
            at_ready, o_ps, o_sum, x1_ready, st_ready, mv_ready = sem("at"), sem("o_ps"), sem("o_sum"), sem("x1"), sem("st"), sem("mv")
        if dense:
            G2 = sb("G2", [P, 2, KX])
            SD, VE, RD, TN = [sb(n, [P, NT]) for n in ("SD", "VE", "RD", "TN")]
            XR = sb("XR", [P, TPC, D])
            YS, YG = sb("YS", [P, TPC, D]), sb("YG", [P, TPC, D])
            G = sb("G", [P, TPC, D])
            TI = sb("TI", [P, TPC], I32)
            xi_ready, y_sum = sem("xi"), sem("y_sum")
            index, indexed, root, product_made, ys_in, yg_in, kept, mixed, gated = sem("index"), sem("indexed"), sem("root"), sem("product"), sem("ys_in"), sem("yg_in"), sem("kept"), sem("mixed"), sem("gated")
        nb = 2 if experts else 4
        row = lambda ap, n: ap.rearrange("(a n) -> a n", a=1).broadcast_to([P, n])
        tile = lambda buf, i, j: buf[:, bass.ds(TPC * i + j, 1), :].rearrange("p a d -> p (a d)")
        quarter = lambda w, q: w[:, :, :].rearrange("p a b -> p (a b)")[:, q * KX * F // QW:(q + 1) * KX * F // QW]
        with nc.Block() as block:
            @block.sync
            def _(sp):
                def load_x(i):
                    sp.dma_start(XI[:, :, :], scratch["xs"][bass.ds(i * CH, CH), :].rearrange("(j p) d -> p j d", p=P)).then_inc(x_in, 16)

                def load_sums(i):
                    sp.dma_start(AO[:, :, :], scratch["ao"].rearrange("(k p) n -> p k n", p=P)[:, :, bass.ds(i * CH, CH)]).then_inc(ao_in, 16)
                    for h in range(H):
                        r = h % (H // 2) * HD
                        sp.dma_start(DN[r:r + HD, h // (H // 2), :], scratch["inv"][h:h + 1, bass.ds(i * CH, CH)].broadcast_to([HD, CH])).then_inc(ao_in, 16)

                sp.sem_inc(y_ps, TPC)
                sp.sem_inc(y_done, TPC)
                if experts:
                    sp.sem_inc(at_ready, 2)
                    sp.sem_inc(w1_in, 16)
                    sp.sem_inc(w2_in, 16)
                    load_x(0)
                    sp.dma_start(RC[:, :], scratch["den"].rearrange("h (c n) -> (h c) n", n=CH)).then_inc(den_in, 16)
                    sp.dma_start(B1[:, :, :], io["w_b1"].rearrange("e (f p) -> p e f", p=P), allow_slow_non_contiguous=True).then_inc(b_in, 16)
                    sp.dma_start(B2[:, :, :].rearrange("p e d -> p (e d)"), row(io["w_b2"].rearrange("e d -> (e d)"), E * D)).then_inc(b_in, 16)
                    sp.dma_start(WO[:, :, :], io["wo"].rearrange("(k p) n -> p k n", p=P)).then_inc(wo_in, 16)
                    sp.dma_start(BO[:, :], row(io["bo"], D)).then_inc(wo_in, 16)
                    sp.wait_ge(inv, 1)
                    sp.dma_start(scratch["inv"].rearrange("h (c n) -> (h c) n", n=CH), RC[:, :]).then_inc(inv_out, 16)
                    sp.wait_ge(inv_out, 16)
                    load_sums(0)
                else:
                    sp.sem_inc(gated, 1)
                    sp.dma_start(G2[:, 0, :], io["ln2_g"].rearrange("(k p) -> p k", p=P), allow_slow_non_contiguous=True).then_inc(b_in, 16)
                    sp.dma_start(G2[:, 1, :], io["ln2_b"].rearrange("(k p) -> p k", p=P), allow_slow_non_contiguous=True).then_inc(b_in, 16)
                    sp.dma_start(B1[:, 0, :], io["w_b1"].rearrange("(f p) -> p f", p=P), allow_slow_non_contiguous=True).then_inc(b_in, 16)
                    sp.dma_start(B2[:, 0, :], row(io["w_b2"], D)).then_inc(b_in, 16)
                with sp.Fori(0, NC) as i:
                    after = sp.snap((i + 1) % NC)
                    then = sp.snap(i + 1)
                    if experts:
                        sp.wait_ge(w1_lo, QW * (i + 1))
                        sp.sem_inc(stepped, 1)
                        sp.dma_start(W1[:, :, :], io["w_1"][bass.ds(then, 1), :, :].rearrange("e (k p) f -> p (e k) f", p=P)).then_inc(w1_in, 16)
                        sp.wait_ge(xposed, KX * (i + 1))
                        sp.sem_inc(stepped, 1)
                        load_x(after)
                        sp.wait_ge(at_ready, 2 * (i + 2))
                        sp.sem_inc(stepped, 1)
                        load_sums(after)
                        sp.wait_ge(w2_lo, QW * (i + 1))
                        sp.sem_inc(stepped, 1)
                        sp.dma_start(W2[:, :, :], io["w_2"][bass.ds(then, 1), :, :].rearrange("e (f p) d -> p (e f) d", p=P)).then_inc(w2_in, 16)
                    if dense:
                        sp.wait_ge(gated, i + 1)
                        sp.sem_inc(stepped, 1)
                        sp.dma_start(YS[:, :, :], scratch["ysh"].rearrange("(t p) d -> p t d", p=P)[:, bass.ds(i * TPC, TPC), :]).then_inc(ys_in, 16)
                        sp.wait_ge(y_done, TPC * (i + 1))
                        sp.sem_inc(stepped, 1)
                        sp.dma_start(XR[:, :, :], io["x"].rearrange("o (t p) d -> p (o t) d", p=P)[:, bass.ds(i * TPC, TPC), :]).then_inc(x_in, 16)
                    sp.wait_ge(y_done, TPC * (i + 2))
                    sp.sem_inc(stepped, 1)
                    if experts:
                        sp.dma_start(scratch["ys"][bass.ds(i * CH, CH), :].rearrange("(j p) d -> p j d", p=P), Y[:, :, :]).then_inc(y_out, 16)
                    else:
                        sp.dma_start(io["out"].rearrange("o (t p) d -> p (o t) d", p=P)[:, bass.ds(i * TPC, TPC), :], Y[:, :, :]).then_inc(y_out, 16)
                sp.wait_ge(y_out, 16 * (NC + 1))
                if experts:
                    sp.wait_ge(x_in, 16 * (NC + 1))
                    sp.wait_ge(ao_in, 16 * (H + 1) * (NC + 1))
                    sp.wait_ge(w1_in, 16 * (NC + 1))
                    sp.wait_ge(w2_in, 16 * (NC + 1))

            @block.gpsimd
            def _(pool):
                def low(raw, hi, lo, q, ready, done, need):
                    pool.wait_ge(ready, need)
                    nc.gpsimd.tensor_tensor(quarter(lo, q), quarter(raw, q), quarter(hi, q).bitcast(F32), ALU.subtract).then_inc(done, 1)

                if experts:
                    for q in range(QW):
                        low(W1, W1H, W1L, q, w1_hi, w1_lo, q + 1)
                if dense:
                    for q in range(QW):
                        low(W2, W2H, W2L, q, w2_hi, w2_lo, q + 1)
                with pool.Fori(0, NC) as i:
                    if experts:
                        for q in range(QW):
                            low(W2, W2H, W2L, q, w2_hi, w2_lo, QW * i + q + 1)
                        for q in range(QW):
                            low(W1, W1H, W1L, q, w1_hi, w1_lo, QW * (i + 1) + q + 1)
                    if dense:
                        pool.wait_ge(gated, i + 1)
                        nc.gpsimd.tensor_copy(TI[:, :], keep["TAKE"][:, bass.ds(TPC * i, TPC)]).then_inc(index, 1)
                        pool.wait_ge(index, i + 1)
                        pool.sem_inc(indexed, 1)
                        for j in range(TPC):
                            nc.gpsimd.indirect_dma_start(out=YG[:, j, :], out_offset=None, in_=scratch["ys"],
                                                         in_offset=bass.IndirectOffsetOnAxis(ap=TI[:, j:j + 1], axis=0)).then_inc(yg_in, 16)
                        for j in range(TPC):
                            pool.wait_ge(y_sum, TPC * i + j + 1)
                            if j == 0:
                                pool.wait_ge(gated, i + 2)
                                pool.wait_ge(x_in, 16 * (i + 1))
                            nc.gpsimd.tensor_tensor(Y[:, j, :], Y[:, j, :], G[:, j, :], ALU.mult).then_inc(product_made, 1)
                            pool.wait_ge(product_made, TPC * i + j + 1)
                            nc.gpsimd.tensor_tensor(Y[:, j, :], Y[:, j, :], XR[:, j, :], ALU.add).then_inc(y_done, 1)

            @block.tensor
            def _(pe):
                def transposes():
                    for k in range(KX):
                        for j in range(TPC):
                            mm = nc.tensor.transpose(ps[:, TB + k, j * P:(j + 1) * P], XI[:, j, k * P:(k + 1) * P], ident[:, :])
                        mm.then_inc(xposed, 1)

                pe.wait_ge(*((x_in, 16) if experts else (xi_ready, TPC)))
                transposes()
                with pe.Fori(0, NC) as i:
                    pe.wait_ge(x_lo, KX * (i + 1))
                    if experts:
                        pe.wait_ge(w1_lo, QW * (i + 1))
                    for f in range(FBK):
                        pe.wait_ge(h_act, FBK * i + f + 1)
                        product(nc, ps[:, f % 4, :], (W1H, W1L), (XH, XL), lambda w, k: w[:, k, f * P:(f + 1) * P],
                                lambda x, k: x[:, k, :], KX).then_inc(h_ps, 1)
                    pe.wait_ge(h_act, FBK * (i + 1) + 2)
                    pe.wait_ge(*((x_in, 16 * (i + 2)) if experts else (xi_ready, TPC * (i + 2))))
                    transposes()
                    if experts:
                        pe.wait_ge(at_ready, 2 * (i + 2))
                        for j in range(TPC):
                            if j == 0:
                                pe.wait_ge(wo_in, 32)
                            if j == 2:
                                pe.wait_ge(h_act, FBK * (i + 1) + 4)
                            pe.wait_ge(o_sum, TPC * i + j + 1)
                            for k in range(2):
                                mm = nc.tensor.matmul(ps[:, OB[j], 0:D], AT[:, k, j * P:(j + 1) * P], WO[:, k, :], start=(k == 0), stop=(k == 1))
                            mm.then_inc(o_ps, 1)
                    pe.wait_ge(w2_lo, QW * (i + 1) if experts else QW)
                    for j in range(TPC):
                        pe.wait_ge(y_taken, TPC * i + j + 1)
                        product(nc, ps[:, YB + j % 2, 0:D], (HH, HL), (W2H, W2L), lambda h, f: h[:, f, j * P:(j + 1) * P],
                                lambda w, f: w[:, f, :], FBK,
                                (lambda f: pe.wait_ge(h_lo, FBK * i + f + 1)) if j == 0 else None).then_inc(y_ps, 1)

            @block.scalar
            def _(act):
                act.sem_inc(h_act, 4)

                def high(raw, hi, q, done):
                    nc.scalar.activation(quarter(hi, q), quarter(raw, q), ACT.Copy).then_inc(done, 1)

                def evacuate(need):
                    for k in range(KX):
                        act.wait_ge(xposed, need + k + 1)
                        if dense:
                            nc.scalar.activation(XF[:, k, :], ps[:, TB + k, :], ACT.Identity, scale=G2[:, 0, k:k + 1], bias=G2[:, 1, k:k + 1]).then_inc(x_sb, 1)
                        else:
                            nc.scalar.activation(XF[:, k, :], ps[:, TB + k, :], ACT.Copy).then_inc(x_sb, 1)

                if experts:
                    act.wait_ge(w1_in, 16)
                    for q in range(QW):
                        high(W1, W1H, q, w1_hi)
                    evacuate(0)
                    act.wait_ge(b_in, 16 * nb)
                else:
                    act.wait_ge(root, 1)
                    nc.scalar.activation(SD[:, :], VE[:, :], ACT.Sqrt).then_inc(root, 1)
                    for q in range(QW):
                        high(W2, W2H, q, w2_hi)
                    act.wait_ge(b_in, 16 * nb)
                    evacuate(0)
                with act.Fori(0, NC) as i:
                    for f in range(FBK):
                        act.wait_ge(h_ps, FBK * i + f + 1)
                        bias = B1[:, bass.ds(i, 1), f:f + 1].rearrange("p a f -> p (a f)") if experts else B1[:, 0, f:f + 1]
                        nc.scalar.activation(HT[:, f, :], ps[:, f % 4, :], ACT.Gelu, bias=bias).then_inc(h_act, 1)
                        if experts and f >= 2 and f < 2 + QW:
                            if f == 2:
                                act.wait_ge(w2_in, 16 * (i + 1))
                            high(W2, W2H, f - 2, w2_hi)
                    evacuate(KX * (i + 1))
                    if experts:
                        act.wait_ge(w1_in, 16 * (i + 2))
                        for q in range(QW):
                            high(W1, W1H, q, w1_hi)
                    if dense:
                        act.wait_ge(mixed, TPC * (i + 1))
                        act.wait_ge(y_done, TPC * (i + 1))
                        nc.scalar.activation(G[:, :, :], YS[:, :, :], ACT.Silu).then_inc(gated, 1)

            @block.vector
            def _(dve):
                dve.sem_inc(y_taken, 2)
                dve.sem_inc(y_out, 16)
                if experts:
                    dve.sem_inc(o_sum, 4)
                    dve.sem_inc(o_ps, TPC)

                def center(i):
                    for j in range(TPC):
                        nc.vector.tensor_scalar(XI[:, j, :], tile(X1, i, j), tile(MV, i, j)[:, 0:1], RD[:, bass.ds(TPC * i + j, 1)],
                                                ALU.subtract, ALU.mult).then_inc(xi_ready, 1)

                def cut(src, hi, lo, n, count, ready, made_hi, made_lo):
                    for b in range(n + 1):
                        if b < n:
                            dve.wait_ge(ready, count + b + 1 + (4 if ready is h_act else 0))
                            nc.vector.tensor_copy(hi[:, b, :], src[:, b, :]).then_inc(made_hi, 1)
                        if b > 0:
                            dve.wait_ge(made_hi, count + b)
                            nc.vector.tensor_tensor(lo[:, b - 1, :], src[:, b - 1, :], hi[:, b - 1, :].bitcast(F32), ALU.subtract).then_inc(made_lo, 1)

                if dense:
                    nc.vector.tensor_scalar(VE[:, :], MV[:, :, 1], EPS, None, ALU.add).then_inc(root, 1)
                    dve.wait_ge(root, 2)
                    root_steps(nc, dve, (root, 2), RD[:, :], VE[:, :], SD[:, :], TN[:, :])
                    center(0)
                cut(XF, XH, XL, KX, 0, x_sb, x_hi, x_lo)
                if experts:
                    dve.wait_ge(den_in, 16)
                    nc.vector.reciprocal(RC[:, :], RC[:, :]).then_inc(inv, 1)
                dve.wait_ge(b_in, 16 * nb)
                with dve.Fori(0, NC) as i:
                    if experts:
                        dve.wait_ge(ao_in, 16 * (H + 1) * (i + 1))
                        dve.wait_ge(o_ps, TPC * (i + 1))
                        for k in range(2):
                            nc.vector.tensor_tensor(AT[:, k, :], AO[:, k, :], DN[:, k, :], ALU.mult).then_inc(at_ready, 1)
                    if dense:
                        dve.wait_ge(xposed, KX * (i + 1))
                        center((i + 1) % NC)
                    cut(HT, HH, HL, FBK, FBK * i, h_act, h_hi, h_lo)
                    if dense:
                        dve.wait_ge(ys_in, 16 * (i + 1))
                        dve.wait_ge(yg_in, 16 * TPC * (i + 1))
                        for j in range(TPC):
                            at = bass.ds(TPC * i + j, 1)
                            nc.vector.tensor_scalar(YG[:, j, :], YG[:, j, :], keep["KEPT"][:, at], None, ALU.mult).then_inc(kept, 1)
                        for j in range(TPC):
                            at = bass.ds(TPC * i + j, 1)
                            dve.wait_ge(kept, TPC * i + j + 1)
                            nc.vector.scalar_tensor_tensor(YS[:, j, :], YS[:, j, :], keep["FB"][:, at], YG[:, j, :], ALU.mult, ALU.add).then_inc(mixed, 1)
                    if experts:
                        for j in range(TPC):
                            t = TPC * i + j
                            dve.wait_ge(o_ps, TPC * (i + 1) + j + 1)
                            if j == 0:
                                dve.wait_ge(wo_in, 32)
                            nc.vector.tensor_tensor(tile(X1, i, j), ps[:, OB[j], 0:D], tile(X1, i, j), ALU.add).then_inc(o_sum, 1)
                            dve.wait_ge(o_sum, t + 5)
                            nc.vector.tensor_tensor(tile(X1, i, j), tile(X1, i, j), BO[:, :], ALU.add).then_inc(x1_ready, 1)
                            dve.wait_ge(x1_ready, t + 1)
                            nc.vector.bn_stats(tile(ST, i, j), tile(X1, i, j)).then_inc(st_ready, 1)
                    cut(XF, XH, XL, KX, KX * (i + 1), x_sb, x_hi, x_lo)
                    for j in range(TPC):
                        t = TPC * i + j
                        dve.wait_ge(y_ps, TPC * (i + 1) + j + 1)
                        if j == 0:
                            dve.wait_ge(y_out, 16 * (i + 1))
                        bias = B2[:, bass.ds(i, 1), :].rearrange("p a d -> p (a d)") if experts else B2[:, 0, :]
                        nc.vector.tensor_tensor(Y[:, j, :], ps[:, YB + j % 2, 0:D], bias, ALU.add).then_inc(y_taken, 1)
                        dve.wait_ge(y_taken, t + 3)
                        if experts:
                            dve.sem_inc(y_done, 1)
                        else:
                            nc.vector.tensor_tensor(Y[:, j, :], Y[:, j, :], tile(X1, i, j), ALU.add).then_inc(y_sum, 1)
                if experts:
                    dve.wait_ge(st_ready, NT)
                    for t in range(NT):
                        nc.vector.bn_aggr(MV[:, t, :], ST[:, t, :]).then_inc(mv_ready, 1)


def build(nc, io):
    scratch = {
        "v": nc.dram_tensor("v_rows", [N, 2 * D], F32, kind="Internal").ap(),
        "qkp": nc.dram_tensor("qk_parts", [3, 2 * D, N], BF16, kind="Internal").ap(),
        "ao": nc.dram_tensor("attention_sums", [D, N], F32, kind="Internal").ap(),
        "den": nc.dram_tensor("denominators", [H, N], F32, kind="Internal").ap(),
        "inv": nc.dram_tensor("denominators_inverse", [H, N], F32, kind="Internal").ap(),
        "xs": nc.dram_tensor("rows_by_place", [2 * N, D], F32, kind="Internal").ap(),
        "ys": nc.dram_tensor("experts_rows", [N, D], F32, kind="Internal").ap(),
        "ysh": nc.dram_tensor("shared_rows", [N, D], F32, kind="Internal").ap(),
    }
    with ExitStack() as ctx:
        sb = lambda name, shape, dt=F32: ctx.enter_context(nc.sbuf_tensor(name, shape, dt))
        keep = {
            "ident": sb("ident", [P, P]), "XN": sb("XN", [P, NT, D]), "LG": sb("LG", [P, NT, E]),
            "FB": sb("FB", [P, NT]), "KEPT": sb("KEPT", [P, NT]), "SLOT": sb("SLOT", [P, NT], I32), "TAKE": sb("TAKE", [P, NT], I32),
            "MV": sb("MVX", [P, NT, 2]), "routed": ctx.enter_context(nc.semaphore("routed")),
        }
        project_tokens(nc, io, scratch, keep)
        keep["W1"], keep["W2"] = sb("W1", [P, D // P, F]), sb("W2", [P, F // P, D])
        attend(nc, io, scratch, keep)
        for name, shape in (("W1H", [P, D // P, F]), ("W1L", [P, D // P, F]), ("W2H", [P, F // P, D]), ("W2L", [P, F // P, D])):
            keep[name] = sb(name, shape, F32R)
        networks(nc, dict(w_1=io["w1"], w_b1=io["b1"], w_2=io["w2"], w_b2=io["b2"], wo=io["wo"], bo=io["bo"]), scratch, keep, "experts")
        networks(nc, dict(w_b1=io["bb1"], w_b2=io["bb2"], ln2_g=io["ln2_g"], ln2_b=io["ln2_b"],
                          x=io["x"], out=io["out"]), scratch, keep, "dense")


_INS = {"x": "L0_attn_x", "ln1_g": "L0_attn_ln1_g", "ln1_b": "L0_attn_ln1_b", "wqkv": "L0_attn_Wqkv", "bqkv": "L0_attn_bqkv",
        "wo": "L0_attn_Wo", "bo": "L0_attn_bo", "ln2_g": "L0_attn_ln2_g", "ln2_b": "L0_attn_ln2_b", "W1": "L0_attn_W1",
        "bb1": "L0_attn_b1", "W2": "L0_attn_W2", "bb2": "L0_attn_b2", "rb": "L0_ffn_rb", "w1": "L0_ffn_w1", "b1": "L0_ffn_b1",
        "w2": "L0_ffn_w2", "b2": "L0_ffn_b2", "sw1": "L0_ffn_sw1", "sb1": "L0_ffn_sb1", "sw2": "L0_ffn_sw2", "sb2": "L0_ffn_sb2"}


def rotary_tables():
    inv = np.float32(1) / (10000.0 ** (np.arange(0, HD, 2) / HD)).astype(np.float32)
    angle = np.arange(N, dtype=np.float32)[:, None] * inv[None]
    c, s = np.cos(angle), np.sin(angle)
    return np.concatenate([c, c], 1).astype(np.float32), np.concatenate([-s, s], 1).astype(np.float32)


def kernel(**inputs):
    import concourse.bacc as bacc
    from concourse.bass_utils import run_bass_kernel_spmd

    nc = bacc.Bacc("TRN2", target_bir_lowering=False, num_devices=1)
    arrays = {short: np.ascontiguousarray(inputs[name]) for short, name in _INS.items()}
    arrays["rwT"] = np.ascontiguousarray(np.asarray(inputs["L0_ffn_rw"]).T)
    for w in ("w1", "w2"):
        arrays[w] = np.concatenate([arrays[w], arrays.pop(w.upper())[None]])
    arrays["cos"], arrays["sin"] = rotary_tables()
    feed, io = {}, {}
    for short, a in arrays.items():
        feed[f"in_{short}"] = a
        io[short] = nc.dram_tensor(f"in_{short}", a.shape, mybir.dt.from_np(a.dtype), kind="ExternalInput").ap()
    io["out"] = nc.dram_tensor("out", (1, N, D), F32, kind="ExternalOutput").ap()
    build(nc, io)
    r = run_bass_kernel_spmd(nc, [feed], core_ids=[0])
    return r.results[0]["out"]
```
